# Optimizing a Trainium2 kernel written in Bass

```python
import numpy as np
import jax
import jax.numpy as jnp

def _softmax(x, axis=-1):
    return jax.nn.softmax(x, axis=axis)

def _gelu(x):
    return jax.nn.gelu(x, approximate=True)

def _silu(x):
    return jax.nn.silu(x)

def _sigmoid(x):
    return jax.nn.sigmoid(x)

def _layernorm(x, axis=-1, eps=1e-05):
    m = jnp.mean(x, axis=axis, keepdims=True)
    v = jnp.var(x, axis=axis, keepdims=True)
    return (x - m) / jnp.sqrt(v + eps)

def _scatter_add(tgt, idx, src, axis=0):
    return tgt.at[idx].add(src)

def _segment_sum(src, seg, n):
    return jax.ops.segment_sum(src, seg, n)
kernel_name = 'mk_decoder_postln_d1_seqx_r8_9dc3cb'

def setup_inputs(seed: int=0):
    np.random.seed(seed)
    _w = jnp.asarray

    def _rec_inputs():
        import jax
        import jax.numpy as jnp
        _rk = jax.random.key(seed)
        x = 4.136e-05 + 0.9999 * jax.random.normal(jax.random.fold_in(_rk, 1), (4, 256, 256), jnp.float32)
        _lenS = 256 - jax.random.randint(jax.random.fold_in(_rk, 7), (4,), 0, max(1, 256 // 4) + 1, jnp.int32)
        _lenS2 = 256 - jax.random.randint(jax.random.fold_in(_rk, 8), (4,), 0, max(1, 256 // 4) + 1, jnp.int32)
        _ctx_1024P = jax.random.normal(jax.random.fold_in(_rk, 11), (4, 16, 128), jnp.float32)
        _ctx_1024c = jax.random.dirichlet(jax.random.fold_in(_rk, 511), 0.3 * jnp.ones((16,), jnp.float32), (4, 256))
        _ctx_1024t = jnp.einsum('bsk,bkd->bsd', _ctx_1024c, _ctx_1024P)
        _ctx_1024t = _ctx_1024t * jax.lax.rsqrt(jnp.mean(jnp.square(_ctx_1024t)) + 1e-12) * 0.953939
        ctx_1024 = -0.000292821 + 1.00034 * (_ctx_1024t + 0.3 * jax.random.normal(jax.random.fold_in(_rk, 611), (4, 256, 128), jnp.float32))
        return (x, ctx_1024)
    x, ctx_1024 = _rec_inputs()

    def _L0_attn_setup():
        import jax, jax.numpy as jnp
        import numpy as np
        HIDDEN = 256
        HEADS = 16
        HEAD_DIM = HIDDEN // HEADS
        key = jax.random.key(seed)
        kx, kq, kk, kv, ko = jax.random.split(key, 5)
        s = 1.0 / np.sqrt(HIDDEN)
        return {'x': jax.random.normal(kx, (2, 256, HIDDEN), dtype=jnp.float32), 'Wq': jax.random.normal(kq, (HIDDEN, HIDDEN), dtype=jnp.float32) * s, 'Wk': jax.random.normal(kk, (HIDDEN, HIDDEN), dtype=jnp.float32) * s, 'Wv': jax.random.normal(kv, (HIDDEN, HIDDEN), dtype=jnp.float32) * s, 'Wo': jax.random.normal(ko, (HIDDEN, HIDDEN), dtype=jnp.float32) * s}
    _L0_attn_all = _L0_attn_setup()
    _L0_attn_in = {k: v for k, v in _L0_attn_all.items() if k in ('Wq', 'Wk', 'Wv', 'Wo')}
    del _L0_attn_all

    def _L0_xattn_setup():
        import jax, jax.numpy as jnp
        import numpy as np
        import math
        B, L, DM = (2, 256, 128)
        DS, DC, EXP = (16, 4, 2)
        DI = EXP * DM
        DR = math.ceil(DM / 16)
        DT_MIN, DT_MAX, DT_FLOOR = (0.001, 0.1, 0.0001)

        def _ssm_forward(hidden_states, z, in_proj_w, conv_w, conv_b, x_proj_w, dt_proj_w, dt_proj_b, A_log, D):
            b = hidden_states.shape[0]
            x = jnp.einsum('ed,bld->bel', in_proj_w, hidden_states)
            xp = jnp.pad(x, ((0, 0), (0, 0), (DC - 1, 0)))
            xc = jax.lax.conv_general_dilated(xp, conv_w[:, None, :], window_strides=(1,), padding='VALID', dimension_numbers=('NCH', 'OIH', 'NCH'), feature_group_count=DI)
            u = jax.nn.silu(xc + conv_b[None, :, None])
            x_dbl = jnp.einsum('ke,bel->bkl', x_proj_w, u)
            dt_lo = x_dbl[:, :DR]
            Bm = x_dbl[:, DR:DR + DS]
            Cm = x_dbl[:, DR + DS:]
            delta = jax.nn.softplus(jnp.einsum('er,brl->bel', dt_proj_w, dt_lo) + dt_proj_b[None, :, None])
            A = -jnp.exp(A_log)

            def step(state, xs):
                d_t, B_t, C_t, u_t = xs
                dA = jnp.exp(d_t[..., None] * A)
                state = state * dA + (d_t * u_t)[..., None] * B_t[:, None, :]
                y_t = jnp.einsum('ben,bn->be', state, C_t)
                return (state, y_t)
            xs = (jnp.moveaxis(delta, -1, 0), jnp.moveaxis(Bm, -1, 0), jnp.moveaxis(Cm, -1, 0), jnp.moveaxis(u, -1, 0))
            state0 = jnp.zeros((b, DI, DS), delta.dtype)
            _, ys = jax.lax.scan(step, state0, xs)
            y = jnp.moveaxis(ys, 0, -1)
            y = y + D[None, :, None] * u
            y = y * jax.nn.silu(z)
            return jnp.swapaxes(y, 1, 2)
        key = jax.random.key(seed)
        ks = jax.random.split(key, 8)
        hidden_states = jax.random.normal(ks[0], (B, L, DM), jnp.float32)
        z = jax.random.normal(ks[1], (B, DI, L), jnp.float32)
        in_proj_w = jax.random.normal(ks[2], (DI, DM), jnp.float32) * DM ** (-0.5)
        conv_w = jax.random.normal(ks[3], (DI, DC), jnp.float32) * DC ** (-0.5)
        conv_b = jnp.zeros((DI,), jnp.float32)
        x_proj_w = jax.random.normal(ks[4], (DR + 2 * DS, DI), jnp.float32) * DI ** (-0.5)
        dt_std = DR ** (-0.5)
        dt_proj_w = jax.random.uniform(ks[5], (DI, DR), jnp.float32, -dt_std, dt_std)
        dt = jnp.exp(jax.random.uniform(ks[6], (DI,), jnp.float32) * (math.log(DT_MAX) - math.log(DT_MIN)) + math.log(DT_MIN))
        dt = jnp.clip(dt, DT_FLOOR)
        dt_proj_b = dt + jnp.log(-jnp.expm1(-dt))
        A_log = jnp.log(jnp.broadcast_to(jnp.arange(1, DS + 1, dtype=jnp.float32), (DI, DS)))
        D = jnp.ones((DI,), jnp.float32)
        return dict(hidden_states=hidden_states, z=z, in_proj_w=in_proj_w, conv_w=conv_w, conv_b=conv_b, x_proj_w=x_proj_w, dt_proj_w=dt_proj_w, dt_proj_b=dt_proj_b, A_log=A_log, D=D)
    _L0_xattn_all = _L0_xattn_setup()
    _L0_xattn_in = {k: v for k, v in _L0_xattn_all.items() if k in ('in_proj_w', 'conv_w', 'conv_b', 'x_proj_w', 'dt_proj_w', 'dt_proj_b', 'A_log', 'D')}
    del _L0_xattn_all

    def _L0_ffn_setup():
        import jax, jax.numpy as jnp
        import numpy as np
        NUM_EXPERTS = 8
        TOP_K = 2
        HIDDEN = 256
        INTER = 512
        GATE_MULT = 0.5
        DOWN_MULT = 0.25
        key = jax.random.key(seed)
        k1, k2, k3, k4, k5 = jax.random.split(key, 5)
        s_h = 1.0 / np.sqrt(HIDDEN)
        s_i = 1.0 / np.sqrt(INTER)
        return {'hidden_states': jax.random.normal(k1, (4, 256, HIDDEN), dtype=jnp.float32), 'w_router': jax.random.normal(k2, (HIDDEN, NUM_EXPERTS), dtype=jnp.float32) * s_h, 'w_gate': jax.random.normal(k3, (NUM_EXPERTS, HIDDEN, INTER), dtype=jnp.float32) * s_h, 'w_up': jax.random.normal(k4, (NUM_EXPERTS, HIDDEN, INTER), dtype=jnp.float32) * s_h, 'w_down': jax.random.normal(k5, (NUM_EXPERTS, INTER, HIDDEN), dtype=jnp.float32) * s_i}
    _L0_ffn_all = _L0_ffn_setup()
    _L0_ffn_in = {k: v for k, v in _L0_ffn_all.items() if k in ('w_router', 'w_gate', 'w_up', 'w_down')}
    del _L0_ffn_all
    return {'x': x, 'ctx_1024': ctx_1024, 'L0_attn_Wq': _L0_attn_in['Wq'], 'L0_attn_Wk': _L0_attn_in['Wk'], 'L0_attn_Wv': _L0_attn_in['Wv'], 'L0_attn_Wo': _L0_attn_in['Wo'], 'L0_xattn_in_proj_w': _L0_xattn_in['in_proj_w'], 'L0_xattn_conv_w': _L0_xattn_in['conv_w'], 'L0_xattn_conv_b': _L0_xattn_in['conv_b'], 'L0_xattn_x_proj_w': _L0_xattn_in['x_proj_w'], 'L0_xattn_dt_proj_w': _L0_xattn_in['dt_proj_w'], 'L0_xattn_dt_proj_b': _L0_xattn_in['dt_proj_b'], 'L0_xattn_A_log': _L0_xattn_in['A_log'], 'L0_xattn_D': _L0_xattn_in['D'], 'L0_ffn_w_router': _L0_ffn_in['w_router'], 'L0_ffn_w_gate': _L0_ffn_in['w_gate'], 'L0_ffn_w_up': _L0_ffn_in['w_up'], 'L0_ffn_w_down': _L0_ffn_in['w_down']}

def reference(x, ctx_1024, L0_attn_Wq, L0_attn_Wk, L0_attn_Wv, L0_attn_Wo, L0_xattn_in_proj_w, L0_xattn_conv_w, L0_xattn_conv_b, L0_xattn_x_proj_w, L0_xattn_dt_proj_w, L0_xattn_dt_proj_b, L0_xattn_A_log, L0_xattn_D, L0_ffn_w_router, L0_ffn_w_gate, L0_ffn_w_up, L0_ffn_w_down):
    import jax
    import jax.numpy as jnp

    def _L0_attn_ref(x, Wq, Wk, Wv, Wo):
        import jax, jax.numpy as jnp
        import numpy as np
        HIDDEN = 256
        HEADS = 16
        HEAD_DIM = HIDDEN // HEADS
        b, s, _ = x.shape

        def split_heads(t):
            return t.reshape(b, s, HEADS, HEAD_DIM).transpose(0, 2, 1, 3)
        Q = split_heads(x @ Wq.T)
        K = split_heads(x @ Wk.T)
        V = split_heads(x @ Wv.T)
        scores = jnp.einsum('bhqd,bhkd->bhqk', Q, K) / jnp.sqrt(jnp.float32(HEAD_DIM))
        causal = jnp.tril(jnp.ones((s, s), dtype=bool))
        scores = jnp.where(causal, scores, jnp.float32(-jnp.inf))
        attn = jax.nn.softmax(scores, axis=-1)
        out = jnp.einsum('bhqk,bhkd->bhqd', attn, V)
        out = out.transpose(0, 2, 1, 3).reshape(b, s, HIDDEN)
        return out @ Wo.T

    def _L0_xattn_ref(hidden_states, z, in_proj_w, conv_w, conv_b, x_proj_w, dt_proj_w, dt_proj_b, A_log, D):
        import jax, jax.numpy as jnp
        import numpy as np
        import math
        B, L, DM = (2, 256, 128)
        DS, DC, EXP = (16, 4, 2)
        DI = EXP * DM
        DR = math.ceil(DM / 16)
        DT_MIN, DT_MAX, DT_FLOOR = (0.001, 0.1, 0.0001)

        def _ssm_forward(hidden_states, z, in_proj_w, conv_w, conv_b, x_proj_w, dt_proj_w, dt_proj_b, A_log, D):
            b = hidden_states.shape[0]
            x = jnp.einsum('ed,bld->bel', in_proj_w, hidden_states)
            xp = jnp.pad(x, ((0, 0), (0, 0), (DC - 1, 0)))
            xc = jax.lax.conv_general_dilated(xp, conv_w[:, None, :], window_strides=(1,), padding='VALID', dimension_numbers=('NCH', 'OIH', 'NCH'), feature_group_count=DI)
            u = jax.nn.silu(xc + conv_b[None, :, None])
            x_dbl = jnp.einsum('ke,bel->bkl', x_proj_w, u)
            dt_lo = x_dbl[:, :DR]
            Bm = x_dbl[:, DR:DR + DS]
            Cm = x_dbl[:, DR + DS:]
            delta = jax.nn.softplus(jnp.einsum('er,brl->bel', dt_proj_w, dt_lo) + dt_proj_b[None, :, None])
            A = -jnp.exp(A_log)

            def step(state, xs):
                d_t, B_t, C_t, u_t = xs
                dA = jnp.exp(d_t[..., None] * A)
                state = state * dA + (d_t * u_t)[..., None] * B_t[:, None, :]
                y_t = jnp.einsum('ben,bn->be', state, C_t)
                return (state, y_t)
            xs = (jnp.moveaxis(delta, -1, 0), jnp.moveaxis(Bm, -1, 0), jnp.moveaxis(Cm, -1, 0), jnp.moveaxis(u, -1, 0))
            state0 = jnp.zeros((b, DI, DS), delta.dtype)
            _, ys = jax.lax.scan(step, state0, xs)
            y = jnp.moveaxis(ys, 0, -1)
            y = y + D[None, :, None] * u
            y = y * jax.nn.silu(z)
            return jnp.swapaxes(y, 1, 2)
        return _ssm_forward(hidden_states, z, in_proj_w, conv_w, conv_b, x_proj_w, dt_proj_w, dt_proj_b, A_log, D)

    def _L0_ffn_ref(hidden_states, w_router, w_gate, w_up, w_down):
        import jax, jax.numpy as jnp
        import numpy as np
        NUM_EXPERTS = 8
        TOP_K = 2
        HIDDEN = 256
        INTER = 512
        GATE_MULT = 0.5
        DOWN_MULT = 0.25
        orig_shape = hidden_states.shape
        x = hidden_states.reshape(-1, orig_shape[-1])
        router_logits = x @ w_router
        probs = jax.nn.softmax(router_logits, axis=-1)
        top_vals, top_idx = jax.lax.top_k(probs, TOP_K)
        out = jnp.zeros_like(x)
        for e in range(NUM_EXPERTS):
            w_e = jnp.sum(jnp.where(top_idx == e, top_vals, 0.0), axis=-1)
            g = x @ w_gate[e] * GATE_MULT
            u = x @ w_up[e]
            h = jax.nn.silu(g) * u @ w_down[e] * DOWN_MULT
            out = out + w_e[:, None] * h
        return out.reshape(orig_shape)
    x = _layernorm(x + _L0_attn_ref(x, L0_attn_Wq, L0_attn_Wk, L0_attn_Wv, L0_attn_Wo), axis=-1)
    x = _layernorm(x + _L0_xattn_ref(ctx_1024, x, L0_xattn_in_proj_w, L0_xattn_conv_w, L0_xattn_conv_b, L0_xattn_x_proj_w, L0_xattn_dt_proj_w, L0_xattn_dt_proj_b, L0_xattn_A_log, L0_xattn_D), axis=-1)
    x = _layernorm(x + _L0_ffn_ref(x, L0_ffn_w_router, L0_ffn_w_gate, L0_ffn_w_up, L0_ffn_w_down), axis=-1)
    return x

_drawn_inputs = setup_inputs


def setup_inputs(seed=0):
    import zlib

    import numpy as np

    out = dict(_drawn_inputs(seed))
    spreads = {'L0_xattn_conv_b': (0.0, 0.1), 'L0_xattn_D': (1.0, 0.2)}
    factors = {'L0_xattn_dt_proj_w': 6.418, 'L0_xattn_dt_proj_b': 2.69}
    for name, (base, spread) in spreads.items():
        noise = np.random.default_rng([zlib.crc32(name.encode()), seed]).standard_normal(out[name].shape)
        drawn = base * np.exp(spread * noise) if base else spread * noise
        out[name] = jnp.asarray(drawn.astype(out[name].dtype))
    for name, factor in factors.items():
        out[name] = (out[name] * factor).astype(out[name].dtype)
    return out
```

```python
from contextlib import ExitStack

import concourse.bass as bass
from concourse import mybir

F32 = mybir.dt.float32
F32R = mybir.dt.float32r
BF16 = mybir.dt.bfloat16
U32 = mybir.dt.uint32
ALU = mybir.AluOpType
ACT = mybir.ActivationFunctionType
AX_X = mybir.AxisListType.X

P = 128
LN_EPS = 1e-5
MASKED = -1e38
GATE_MULT = 0.5
DOWN_MULT = 0.25
BANK = 512

DVE_LINKS = 17


class Chain:

    def __init__(self, engine, semaphore):
        self.engine, self.semaphore, self.base, self.n = engine, semaphore, 0, 0

    def at(self, base):
        self.base, self.n = base, 0

    def link(self, ins):
        self.n += 1
        ins.then_inc(self.semaphore, 1)
        self.engine.wait_ge(self.semaphore, self.base + self.n)


def carve(tensor, at, *shape):
    n = 1
    for s in shape:
        n *= s
    view = tensor[:, at:at + n]
    if len(shape) > 1:
        names = "abcde"[: len(shape)]
        view = view.rearrange(f"p ({' '.join(names)}) -> p {' '.join(names)}", **dict(zip(names, shape)))
    return view, at + n


def decoder_layer(
    nc: bass.Bass,
    x: bass.AP,
    ctx_in: bass.AP,
    Wq: bass.AP,
    Wk: bass.AP,
    Wv: bass.AP,
    Wo: bass.AP,
    in_proj_w: bass.AP,
    conv_w: bass.AP,
    conv_b: bass.AP,
    x_proj_w: bass.AP,
    dt_proj_w: bass.AP,
    dt_proj_b: bass.AP,
    A_log: bass.AP,
    D_skip: bass.AP,
    w_router: bass.AP,
    w_gate: bass.AP,
    w_up: bass.AP,
    w_down: bass.AP,
    out: bass.AP,
):
    B, S, HID = x.shape
    DM = ctx_in.shape[2]
    DI, DC = conv_w.shape
    DS = A_log.shape[1]
    DR = dt_proj_w.shape[1]
    NE, _, INTER = w_gate.shape
    HEADS = 16
    HD = HID // HEADS
    QC = S // P
    FC = HID // P
    NT = B * QC
    T = B * S
    HALVES = DI // P
    PAIRS = HEADS // 2
    TILE_PAIRS = PAIRS // FC
    IC = INTER // P
    SCORE = P + S
    SCALE = float(HD) ** -0.5
    BC = 2 * DS
    NP = DS // 2
    TH = T // BANK
    BH = B // TH
    assert DM == P and DI == S == HID and QC == FC == HALVES == 2 and HD == 16 and BC == 32 and TH == 2

    with ExitStack() as stack:
        def sb(name, shape, dt=F32):
            return stack.enter_context(nc.sbuf_tensor(name, shape, dt))

        def sem(name):
            return stack.enter_context(nc.semaphore(name))

        ident = sb("ident", [P, P])
        ident_b = sb("ident_b", [P, P], BF16)
        mask_qk = sb("mask_qk", [P, P], BF16)
        mask_kq = sb("mask_kq", [P, P], BF16)
        pick = sb("pick", [3 * BC, BC, P], BF16)
        iota8 = sb("iota8", [P, NE])
        exponent = sb("exponent", [P, QC])
        wT = sb("wT", [P, 4, FC, HID])
        wr_sb = sb("wr_sb", [P, FC, NE])
        convw_sb = sb("convw_sb", [P, HALVES, DC])
        vec_sb = sb("vec_sb", [P, 3, HALVES])
        A_sb = sb("A_sb", [P, HALVES, DS])
        delta = sb("delta", [P, B, HALVES, S])
        du = sb("du", [P, B, HALVES, S])
        u_sb = sb("u_sb", [P, B, HALVES, S])
        y_sum = sb("y_sum", [P, HALVES, S])
        bc_parts = sb("bc_parts", [3 * BC, T], BF16)
        x_in = sb("x_in", [P, QC, HID])
        x_sb = sb("x_sb", [P, NT, HID])
        x2T_hi = sb("x2T_hi", [P, FC, T], F32R)
        x2T_lo = sb("x2T_lo", [P, FC, T], F32R)
        w_tok = sb("w_tok", [P, NT, NE])
        x1 = sb("x1", [P, QC, HID])
        gated = sb("gated", [P, HALVES, S])
        stats = sb("stats", [P, QC, 6])
        mv = sb("mv", [P, QC, 2])
        rstd = sb("rstd", [P, QC])
        small = sb("small", [P, 8, QC])
        probs = sb("probs", [P, QC, NE])
        top_val = sb("top_val", [P, QC, 8])
        top_idx = sb("top_idx", [P, QC, 8], U32)
        top_idx_f = sb("top_idx_f", [P, QC, 8])
        w_second = sb("w_second", [P, QC, NE])
        negmax = sb("negmax", [P, QC, HEADS])
        negmax_r = sb("negmax_r", [P, QC, HEADS])
        negmax_p = sb("negmax_p", [P, QC, 3 * BC], BF16)
        nmT = sb("nmT", [3 * BC, QC, P], BF16)
        e_raw = sb("e_raw", [P, 6 * INTER])
        eg = sb("eg", [P, 2, 2, 2, FC, INTER], F32R)
        ed = sb("ed", [P, 2, IC, 2, HID], F32R)

        area = sb("area", [P, 8448])
        c_ctx, at = carve(area, 0, NT, DM)
        ctxT, at = carve(area, at, T)
        win_raw, at = carve(area, at, HALVES, DM)
        winT, at = carve(area, at, DI)
        xp_raw, at = carve(area, at, DI)
        xpT, at = carve(area, at, HALVES, 3 * BC + DR)
        dtw_raw, at = carve(area, at, HALVES, DR)
        dtwT, at = carve(area, at, DI)
        dt_lo, at = carve(area, at, T)
        xpad, at = carve(area, at, HALVES, B, DC - 1 + S)
        conv, at = carve(area, at, B, HALVES, S)
        assert at <= area.shape[1]
        ln_part, _ = carve(area, 0, B, HALVES, S)
        log_rest = conv
        bc_r = ln_part.rearrange("p b h s -> p (b h s)")[:, 0:T]
        w_raw, _ = carve(e_raw, 0, 4, FC, HID)

        dA, at = carve(area, 0, 2, 2, HALVES, S)
        dBu, at = carve(area, at, 2, 2, HALVES, S)
        state, at = carve(area, at, 2, HALVES, S)
        probT, at = carve(area, at, 2, 2, SCORE)
        xT, at = carve(area, at, FC, S)
        v1, at = carve(area, at, QC, HEADS, HD + 1)
        heads, at = carve(area, at, QC, HID)
        assert at <= area.shape[1]
        silu_g, at = carve(area, 0, 2, BANK)
        h_f, at = carve(area, at, 2, BANK)

        split = sb("split", [P, 8192], F32R)
        q4, at = carve(split, 0, PAIRS, S)
        k4, at = carve(split, at, PAIRS, S)
        pickQK, at = carve(split, at, 2, 2, TILE_PAIRS, P)
        q_hi, at = carve(split, at, FC, S)
        q_lo, at = carve(split, at, FC, S)
        k_hi, at = carve(split, at, FC, S)
        k_lo, at = carve(split, at, FC, S)
        assert at <= split.shape[1]
        h_hi, at = carve(split, 0, 2, IC, BANK)
        h_lo, at = carve(split, at, 2, IC, BANK)
        assert at <= split.shape[1]

        psW = stack.enter_context(nc.psum_tensor("psW", [P, 4, BANK], F32))
        psS = stack.enter_context(nc.psum_tensor("psS", [P, 2, BANK], F32))
        psT = stack.enter_context(nc.psum_tensor("psT", [P, 2, BANK], F32))
        psT_b = psT[:, 0, :].bitcast(BF16)

        ld_ctx, ld_ssm, ld_small, ld_x, ld_attn = (sem(s) for s in ("ld_ctx", "ld_ssm", "ld_small", "ld_x", "ld_attn"))
        ld_expert, stored = sem("ld_expert"), sem("stored")
        consts, consts_b, zeroed = sem("consts"), sem("consts_b"), sem("zeroed")
        dve_chain, act_chain, pool_chain = sem("dve_chain"), sem("act_chain"), sem("pool_chain")
        ctxT_ps, ctxT_rdy, ssmT_ps, ssmT_rdy = sem("ctxT_ps"), sem("ctxT_rdy"), sem("ssmT_ps"), sem("ssmT_rdy")
        xin_ps, xpad_rdy, wT_ps, wT_rdy = sem("xin_ps"), sem("xpad_rdy"), sem("wT_ps"), sem("wT_rdy")
        conv_rdy, u_rdy, xdbl_ps, dt_rdy = sem("conv_rdy"), sem("u_rdy"), sem("xdbl_ps"), sem("dt_rdy")
        delta_ps, relu_rdy, exp_rdy, ln_rdy = sem("delta_ps"), sem("relu_rdy"), sem("exp_rdy"), sem("ln_rdy")
        A_rdy, ssm_rdy, area_free = sem("A_rdy"), sem("ssm_rdy"), sem("area_free")
        bc_ps, dA_rdy = sem("bc_ps"), sem("dA_rdy")
        b_used, scanned, hC_rdy, y_added = sem("b_used"), sem("scanned"), sem("hC_rdy"), sem("y_added")
        xT_ps, xT_rdy, q_ps, k_ps, v_ps = (sem(s) for s in ("xT_ps", "xT_rdy", "q_ps", "k_ps", "v_ps"))
        q_hi_rdy, k_hi_rdy, q_lo_rdy, k_lo_rdy, v_rdy = (
            sem(s) for s in ("q_hi_rdy", "k_hi_rdy", "q_lo_rdy", "k_lo_rdy", "v_rdy"))
        q4_ps, q4_rdy, k4_ps, k4_rdy = sem("q4_ps"), sem("q4_rdy"), sem("k4_ps"), sem("k4_rdy")
        score_ps, max_rdy, nm_rdy, nmT_ps, nmT_rdy = (
            sem(s) for s in ("score_ps", "max_rdy", "nm_rdy", "nmT_ps", "nmT_rdy"))
        scoreT_ps, probT_rdy, pv_ps, heads_rdy = sem("scoreT_ps"), sem("probT_rdy"), sem("pv_ps"), sem("heads_rdy")
        headsT_ps, headsT_rdy, attn_ps, x1_rdy = sem("headsT_ps"), sem("headsT_rdy"), sem("attn_ps"), sem("x1_rdy")
        res_rdy, x2_kept = sem("res_rdy"), sem("x2_kept")
        var_rdy, rstd_rdy = sem("var_rdy"), sem("rstd_rdy")
        tanh_rdy, gated_rdy, gatedT_ps, x2_rdy = sem("tanh_rdy"), sem("gated_rdy"), sem("gatedT_ps"), sem("x2_rdy")
        x2T_ps, x2T_rdy, x2lo_rdy, logit_ps = sem("x2T_ps"), sem("x2T_rdy"), sem("x2lo_rdy"), sem("logit_ps")
        lmax_rdy, lexp_rdy, w_rdy = sem("lmax_rdy"), sem("lexp_rdy"), sem("w_rdy")
        ehi_rdy, elo_rdy = sem("ehi_rdy"), sem("elo_rdy")
        gu_ps, silu_rdy, h_rdy, hhi_rdy, hlo_rdy = (
            sem(s) for s in ("gu_ps", "silu_rdy", "h_rdy", "hhi_rdy", "hlo_rdy"))
        down_ps, summed, final_rdy = sem("down_ps"), sem("summed"), sem("final_rdy")

        block = stack.enter_context(nc.Block())

        @block.sync
        def _(sp):
            sp.dma_start(c_ctx, ctx_in.rearrange("b (q p) d -> p (b q) d", p=P)).then_inc(ld_ctx, 16)
            sp.dma_start(win_raw, in_proj_w.rearrange("(h p) d -> p h d", p=P)).then_inc(ld_ssm, 16)
            sp.dma_start(xp_raw[0:DR + BC, :], x_proj_w).then_inc(ld_ssm, 16)
            sp.dma_start(dtw_raw, dt_proj_w.rearrange("(h p) r -> p h r", p=P)).then_inc(ld_ssm, 16)
            sp.dma_start(convw_sb[:], conv_w.rearrange("(h p) k -> p h k", p=P)).then_inc(ld_small, 16)
            for i, v in enumerate((conv_b, dt_proj_b, D_skip)):
                with nc.allow_non_contiguous_dma(reason="256 values, one to a partition"):
                    sp.dma_start(vec_sb[:, i, :], v.rearrange("(h p) -> p h", p=P)).then_inc(ld_small, 16)
            sp.dma_start(A_sb[:], A_log.rearrange("(h p) n -> p h n", p=P)).then_inc(ld_small, 16)
            sp.dma_start(wr_sb[:], w_router.rearrange("(k p) e -> p k e", p=P)).then_inc(ld_small, 16)
            for i, w in enumerate((Wq, Wk, Wv, Wo)):
                sp.dma_start(w_raw[:, i], w.rearrange("(c p) n -> p c n", p=P)).then_inc(ld_attn, 16)
            sp.dma_start(x_in[:], x[0].rearrange("(q p) d -> p q d", p=P)).then_inc(ld_x, 16)

            def load_expert(e):
                for i, w in enumerate((w_gate, w_up)):
                    sp.dma_start(
                        e_raw[:, i * FC * INTER:(i + 1) * FC * INTER].rearrange("p (k n) -> p k n", k=FC),
                        w[bass.ds(e, 1)].rearrange("o (k p) n -> p (o k) n", p=P),
                    ).then_inc(ld_expert, 16)
                sp.dma_start(
                    e_raw[:, 2 * FC * INTER:].rearrange("p (k n) -> p k n", k=IC),
                    w_down[bass.ds(e, 1)].rearrange("o (k p) n -> p (o k) n", p=P),
                ).then_inc(ld_expert, 16)

            sp.wait_ge(wT_rdy, 4)
            load_expert(0)
            with sp.Fori(1, B) as b:
                sp.wait_ge(res_rdy, b)
                sp.dma_start(x_in[:], x[bass.ds(b, 1)].rearrange("o (q p) d -> p (o q) d", p=P)).then_inc(ld_x, 16)
            with sp.Fori(1, NE) as e:
                sp.wait_ge(ehi_rdy, 3 * e)
                sp.wait_ge(elo_rdy, 3 * e)
                load_expert(e)
            for t in range(NT):
                sp.wait_ge(final_rdy, t + 1)
                sp.dma_start(
                    out.rearrange("b (q p) d -> p (b q) d", p=P)[:, t, :], x_sb[:, t, :]
                ).then_inc(stored, 16)
            sp.wait_ge(stored, 16 * NT)

        @block.gpsimd
        def _(pool):
            chain = Chain(pool, pool_chain)
            link = chain.link
            link(pool.memset(ident[:], 0.0))
            pool.affine_select(out=ident[:], in_=ident[:], compare_op=ALU.not_equal, fill=1.0, base=0,
                               pattern=[[-1, P]], channel_multiplier=1).then_inc(consts, 1)
            pool.wait_ge(consts, 1)
            pool.memset(xpad[:, :, :, 0:DC - 1], 0.0).then_inc(zeroed, 1)
            for t in (mask_qk, mask_kq, pick, negmax_p):
                link(pool.memset(t[:], 0.0))
            link(pool.memset(exponent[:], -0.5))
            link(pool.tensor_copy(ident_b[:], ident[:]))
            link(pool.affine_select(out=mask_qk[:], in_=mask_qk[:], compare_op=ALU.is_ge, fill=MASKED, base=0,
                                    pattern=[[-1, P]], channel_multiplier=1))
            link(pool.affine_select(out=mask_kq[:], in_=mask_kq[:], compare_op=ALU.is_ge, fill=MASKED, base=0,
                                    pattern=[[1, P]], channel_multiplier=-1))
            for k in range(3):
                rows = pick[BC * k:BC * (k + 1)]
                link(pool.affine_select(out=rows, in_=rows, compare_op=ALU.not_equal, fill=1.0, base=0,
                                        pattern=[[-1, BC], [0, P]], channel_multiplier=1))
            link(pool.iota(iota8[:], pattern=[[1, NE]], base=0, channel_multiplier=0,
                           allow_small_or_imprecise_dtypes=True))
            for j in range(TILE_PAIRS):
                for qk in range(2):
                    for h in range(2):
                        stage = gated[:, qk, h * P:(h + 1) * P].rearrange("p (a k d) -> p a k d", a=2, k=4)
                        blocks = slice(h, 4, 2) if qk else slice(2 * h, 2 * h + 2)
                        link(pool.memset(stage, 0.0))
                        link(pool.affine_select(
                            out=stage[:, :, blocks, :], in_=stage[:, :, blocks, :], compare_op=ALU.not_equal,
                            fill=1.0, base=-2 * HD * j, pattern=[[-HD, 2], [0, 2], [-1, HD]], channel_multiplier=1))
                        last = pool.tensor_copy(pickQK[:, qk, h, j, :], gated[:, qk, h * P:(h + 1) * P])
                        if (j, qk, h) != (TILE_PAIRS - 1, 1, 1):
                            link(last)
            last.then_inc(consts_b, 1)
            pool.wait_ge(consts_b, 1)

            pool.wait_ge(area_free, 1)
            pool.memset(dA[:, :, :, :, 0:1].rearrange("p a n h s -> p (a n h) s"), 0.0).then_inc(zeroed, 1)
            pool.memset(v1[:, :, :, HD:HD + 1].rearrange("p q h d -> p (q h) d"), 1.0).then_inc(y_added, 4)


            def add_states(b, m):
                pool.wait_ge(hC_rdy, b * NP + m + 2)
                for n in range(2):
                    if m == 0 and n == 0:
                        pool.wait_ge(gated_rdy, b + 1)
                        pool.tensor_tensor(y_sum[:], dBu[:, 0, 0], dBu[:, 0, 1], ALU.add).then_inc(y_added, 2)
                    elif m > 0:
                        pool.wait_ge(y_added, b * DS + 2 * m + n + 4)
                        pool.tensor_tensor(y_sum[:], y_sum[:], dBu[:, m % 2, n], ALU.add).then_inc(y_added, 1)

            def inverse_deviation(k):
                pool.wait_ge(var_rdy, k + 1)
                pool.tensor_tensor(rstd[:], rstd[:], exponent[:], ALU.pow).then_inc(rstd_rdy, 1)

            def split_expert_lo(e, i, odd):
                pool.wait_ge(ehi_rdy, 3 * e + i + 1)
                raw = e_raw[:, i * FC * INTER:(i + 1) * FC * INTER]
                if i < 2:
                    raw = raw.rearrange("p (k n) -> p k n", k=FC)
                    hi, lo = eg[:, odd, 0, i], eg[:, odd, 1, i]
                else:
                    raw = raw.rearrange("p (k n) -> p k n", k=IC)
                    hi, lo = ed[:, odd, :, 0, :], ed[:, odd, :, 1, :]
                pool.tensor_tensor(lo, raw, hi.bitcast(F32), ALU.subtract).then_inc(elo_rdy, 1)

            for i in range(3):
                split_expert_lo(0, i, 0)
            with pool.Fori(0, B) as b:
                for m in range(NP):
                    add_states(b, m)
                inverse_deviation(2 * b)
                inverse_deviation(2 * b + 1)
                pool.wait_ge(x2_rdy, b + 1)
                pool.tensor_copy(x_sb[:, bass.ds(2 * b, QC), :], x1[:]).then_inc(x2_kept, 1)

            def expert(e, odd, last=False):
                for th in range(TH):
                    for c in range(IC):
                        k = (e * TH + th) * IC + c
                        pool.wait_ge(hhi_rdy, k + 1)
                        pool.tensor_tensor(h_lo[:, th, c, :], h_f[:, c % 2, :], h_hi[:, th, c, :].bitcast(F32),
                                           ALU.subtract).then_inc(hlo_rdy, 1)
                        if not last and th == 1 and c < 3:
                            split_expert_lo(e + 1, c, 1 - odd)

            expert(0, 0)
            with pool.Fori(0, (NE - 2) // 2) as j:
                expert(2 * j + 1, 1)
                expert(2 * j + 2, 0)
            expert(NE - 1, 1, last=True)
            for t in range(NT // QC):
                inverse_deviation(2 * B + t)

        @block.scalar
        def _(act):
            act.wait_ge(ctxT_ps, 1)
            act.copy(ctxT, psW[:, 0:2, :].rearrange("p a n -> p (a n)")).then_inc(ctxT_rdy, 1)
            for half in range(HALVES):
                for th in range(TH):
                    act.wait_ge(xin_ps, half * TH + th + 1)
                    act.copy(xpad[:, half, BH * th:BH * (th + 1), DC - 1:],
                             psW[:, half * TH + th, :].rearrange("p (b s) -> p b s", b=BH)).then_inc(xpad_rdy, 1)
            for i in range(4):
                act.wait_ge(wT_ps, i + 1)
                bank = psS[:, i, :] if i < 2 else psT[:, i - 2, :]
                act.copy(wT[:, i], bank.rearrange("p (k n) -> p k n", k=FC)).then_inc(wT_rdy, 1)
            for half in range(HALVES):
                act.wait_ge(conv_rdy, half + 1)
                act.activation(u_sb[:, :, half, :], conv[:, :, half, :], ACT.Silu).then_inc(u_rdy, 1)
            for half in range(HALVES):
                for th in range(TH):
                    i = half * TH + th
                    act.wait_ge(relu_rdy, i + 1)
                    act.activation(du[:, BH * th:BH * (th + 1), half, :],
                                   psW[:, (2 + i) % 4, :].rearrange("p (b s) -> p b s", b=BH), ACT.Abs,
                                   bias=vec_sb[:, 1, half:half + 1]).then_inc(act_chain, 1)
            act.wait_ge(act_chain, 4)
            act.activation(du[:], du[:], ACT.Exp, scale=-1.0).then_inc(exp_rdy, 1)
            act.wait_ge(exp_rdy, 1)
            act.activation(ln_part, du[:], ACT.Ln, bias=1.0).then_inc(ln_rdy, 1)
            act.wait_ge(ld_small, 16 * 6)
            act.activation(A_sb[:], A_sb[:], ACT.Exp).then_inc(act_chain, 1)
            act.wait_ge(act_chain, 5)
            act.mul(A_sb[:], A_sb[:], -1.0).then_inc(A_rdy, 1)

            def decay_buffer(b, m):
                act.wait_ge(scanned, b * NP + m + 1)

            def decay(b, m):
                for n in range(2):
                    for half in range(HALVES):
                        act.activation(dA[:, m % 2, n, half, 1:], delta[:, b, half, 1:], ACT.Exp,
                                       scale=A_sb[:, half, 2 * m + n:2 * m + n + 1]).then_inc(dA_rdy, 1)

            def split_expert_hi(e, i, odd):
                act.wait_ge(ld_expert, 48 * (e + 1))
                raw = e_raw[:, i * FC * INTER:(i + 1) * FC * INTER]
                if i < 2:
                    act.copy(eg[:, odd, 0, i], raw.rearrange("p (k n) -> p k n", k=FC)).then_inc(ehi_rdy, 1)
                else:
                    act.copy(ed[:, odd, :, 0, :], raw.rearrange("p (k n) -> p k n", k=IC)).then_inc(ehi_rdy, 1)

            for i in range(3):
                split_expert_hi(0, i, 0)
            act.wait_ge(A_rdy, 1)
            act.wait_ge(ssm_rdy, 1)
            act.wait_ge(area_free, 1)
            with act.Fori(0, B) as b:
                decay_buffer(b, 0)
                act.wait_ge(xT_ps, b + 1)
                act.copy(xT, psW[:, 0, :].rearrange("p (k n) -> p k n", k=FC)).then_inc(xT_rdy, 1)
                decay(b, 0)
                act.wait_ge(q_ps, b + 1)
                act.activation(q_hi, psW[:, 1, :].rearrange("p (k n) -> p k n", k=FC), ACT.Copy,
                               scale=SCALE).then_inc(q_hi_rdy, 1)
                act.wait_ge(k_ps, b + 1)
                act.copy(k_hi, psW[:, 2, :].rearrange("p (k n) -> p k n", k=FC)).then_inc(k_hi_rdy, 1)
                act.wait_ge(v_ps, b + 1)
                act.copy(v1[:, :, :, 0:HD],
                         psW[:, 3, :].rearrange("p (q h d) -> p q h d", q=QC, h=HEADS)).then_inc(v_rdy, 1)
                for i in range(4):
                    act.wait_ge(q4_ps, 4 * b + i + 1)
                    if i == 3:
                        decay_buffer(b, 1)
                    act.copy(q4[:, 2 * i:2 * i + 2, :],
                             psW[:, i, :].rearrange("p (j n) -> p j n", j=2)).then_inc(q4_rdy, 1)
                decay(b, 1)
                for p in range(PAIRS):
                    if p < NP - 2:
                        decay_buffer(b, p + 2)
                    act.wait_ge(scoreT_ps, b * PAIRS + p + 1)
                    act.wait_ge(pv_ps, b * PAIRS + p + 1)
                    w0 = 2 * (p % 2)
                    act.activation(probT[:, p % 2], psW[:, w0:w0 + 2, 0:SCORE], ACT.Exp).then_inc(probT_rdy, 1)
                    if p < NP - 2:
                        decay(b, p + 2)
                act.wait_ge(headsT_ps, b + 1)
                act.copy(xT, psW[:, 0, :].rearrange("p (k n) -> p k n", k=FC)).then_inc(headsT_rdy, 1)
                act.wait_ge(x1_rdy, b + 1)
                act.activation(gated[:], x1[:], ACT.Tanh, scale=0.5).then_inc(tanh_rdy, 1)
                act.wait_ge(x2T_ps, b + 1)
                x2T_bank = psT[:, 1, :].rearrange("p (k n) -> p k n", k=FC)
                act.copy(x2T_hi[:, :, bass.ds(b * S, S)], x2T_bank).then_inc(x2T_rdy, 1)
                act.copy(xT, x2T_bank).then_inc(x2T_rdy, 1)
                act.wait_ge(lmax_rdy, b + 1)
                for q in range(QC):
                    act.activation(probs[:, q], psT[:, 0, q * NE:(q + 1) * NE], ACT.Exp,
                                   bias=small[:, 0, q:q + 1]).then_inc(lexp_rdy, 1)

            def expert(e, odd, first=False, last=False):
                for th in range(TH):
                    for c in range(IC + 1):
                        k = (e * TH + th) * IC + c
                        if c < IC:
                            act.wait_ge(gu_ps, k + 1)
                            if not (first and th == 0 and c < 2):
                                act.wait_ge(h_rdy, k - 1)
                            act.activation(silu_g[:, c % 2], psW[:, c % 2, :], ACT.Silu,
                                           scale=GATE_MULT).then_inc(silu_rdy, 1)
                        if c > 0:
                            act.wait_ge(h_rdy, k)
                            if c == 1 and not first:
                                act.wait_ge(down_ps, (e - 1) * NT + (th + 1) * (NT // TH))
                            act.copy(h_hi[:, th, c - 1, :], h_f[:, (c - 1) % 2, :]).then_inc(hhi_rdy, 1)
                        if th == 1 and 1 <= c <= 3 and not last:
                            if c == 1 and not first:
                                act.wait_ge(down_ps, e * NT)
                            split_expert_hi(e + 1, c - 1, 1 - odd)

            act.wait_ge(logit_ps, B)
            expert(0, 0, first=True)
            with act.Fori(0, (NE - 2) // 2) as j:
                expert(2 * j + 1, 1)
                expert(2 * j + 2, 0)
            expert(NE - 1, 1, last=True)

        @block.vector
        def _(dve):
            chain = Chain(dve, dve_chain)
            link = chain.link
            dve.wait_ge(ssmT_ps, 1)
            dve.tensor_copy(winT, psW[:, 2, 0:DI])
            xp_ps = psW[:, 2, DI:DI + HALVES * (DR + BC)].rearrange("p (h n) -> p h n", h=HALVES)
            for k in range(3):
                dve.tensor_copy(xpT[:, :, BC * k:BC * (k + 1)], xp_ps[:, :, DR:])
            dve.tensor_copy(xpT[:, :, 3 * BC:], xp_ps[:, :, 0:DR])
            dve.tensor_copy(dtwT[0:DR], psW[0:DR, 3, 0:DI]).then_inc(ssmT_rdy, 1)
            dve.wait_ge(ld_small, 16 * 6)
            dve.wait_ge(zeroed, 1)
            for half in range(HALVES):
                dve.wait_ge(xpad_rdy, TH * (half + 1))
                acc = conv[:, :, half, :]
                link(dve.tensor_scalar(acc, xpad[:, half, :, 0:S], convw_sb[:, half, 0:1], vec_sb[:, 0, half:half + 1],
                                       ALU.mult, ALU.add))
                for k in range(1, DC):
                    ins = dve.scalar_tensor_tensor(out=acc, in0=xpad[:, half, :, k:k + S],
                                                   scalar=convw_sb[:, half, k:k + 1], in1=acc,
                                                   op0=ALU.mult, op1=ALU.add)
                    if k < DC - 1:
                        link(ins)
                    else:
                        ins.then_inc(conv_rdy, 1)
            for th in range(TH):
                dve.wait_ge(xdbl_ps, th + 1)
                cols = slice(th * BANK, (th + 1) * BANK)
                bank = psW[0:3 * BC, th, :]
                rest = bc_r[0:3 * BC, cols]
                link(dve.tensor_copy(bc_parts[:, cols], bank))
                link(dve.tensor_tensor(rest, bank, bc_parts[:, cols], ALU.subtract))
                for k in (1, 2):
                    rows = slice(BC * k, BC * (k + 1))
                    link(dve.tensor_copy(bc_parts[rows, cols], rest[rows]))
                link(dve.tensor_tensor(bc_parts[rows, cols], rest[rows], bc_parts[rows, cols], ALU.subtract))
                dve.tensor_copy(dt_lo[0:DR, cols], psW[3 * BC:3 * BC + DR, th, :]).then_inc(dt_rdy, 1)
            for half in range(HALVES):
                for th in range(TH):
                    i = half * TH + th
                    dve.wait_ge(delta_ps, i + 1)
                    dve.tensor_scalar(delta[:, BH * th:BH * (th + 1), half, :],
                                      psW[:, (2 + i) % 4, :].rearrange("p (b s) -> p b s", b=BH),
                                      vec_sb[:, 1, half:half + 1], 0.0, ALU.add, ALU.max).then_inc(relu_rdy, 1)
            dve.wait_ge(exp_rdy, 1)
            link(dve.tensor_scalar(log_rest, du[:], 1.0, -1.0, ALU.add, ALU.add))
            link(dve.tensor_tensor(log_rest, du[:], log_rest, ALU.subtract))
            dve.wait_ge(ln_rdy, 1)
            link(dve.tensor_tensor(log_rest, log_rest, ln_part, ALU.add))
            link(dve.tensor_tensor(delta[:], delta[:], log_rest, ALU.add))
            link(dve.tensor_tensor(du[:], delta[:], u_sb[:], ALU.mult))
            for half in range(HALVES):
                link(dve.tensor_scalar(u_sb[:, :, half, :], u_sb[:, :, half, :], vec_sb[:, 2, half:half + 1],
                                       None, ALU.mult))
            dve.engine_nop().then_inc(area_free, 1)
            dve.engine_nop().then_inc(ssm_rdy, 1)
            dve.engine_nop().then_inc(scanned, 2)
            dve.engine_nop().then_inc(b_used, 1)
            dve.engine_nop().then_inc(hC_rdy, 1)
            dve.engine_nop().then_inc(gated_rdy, 1)
            dve.engine_nop().then_inc(x2_kept, 1)
            prep_links = chain.n

            def ssm_pair(b, m):
                g = b * NP + m
                x_in = dBu[:, m % 2]
                dve.wait_ge(bc_ps, 2 * g + 1)
                dve.wait_ge(y_added, 2 * g + 2)
                dve.tensor_tensor(
                    x_in, du[:, bass.ds(b, 1)].broadcast_to([P, 2, HALVES, S]),
                    psS[:, 0, :].rearrange("p (n o s) -> p n o s", n=2, o=1).broadcast_to([P, 2, HALVES, S]),
                    ALU.mult).then_inc(b_used, 1)
                dve.wait_ge(b_used, g + 2)
                dve.wait_ge(dA_rdy, 4 * g + 4)
                if m == 0:
                    dve.wait_ge(zeroed, 2)
                dve.tensor_tensor_scan(
                    state.rearrange("p n h s -> p (n h s)"), dA[:, m % 2].rearrange("p n h s -> p (n h s)"),
                    x_in.rearrange("p n h s -> p (n h s)"), 0.0, ALU.mult, ALU.add).then_inc(scanned, 1)
                dve.wait_ge(scanned, g + 3)
                dve.wait_ge(bc_ps, 2 * g + 2)
                dve.tensor_tensor(
                    x_in, state,
                    psS[:, 1, :].rearrange("p (n o s) -> p n o s", n=2, o=1).broadcast_to([P, 2, HALVES, S]),
                    ALU.mult).then_inc(hC_rdy, 1)

            def layer_norm(k, src, dst):
                for q in range(QC):
                    ins = dve.bn_stats(stats[:, q], src(q))
                dve.drain()
                for q in range(QC):
                    ins = dve.bn_aggr(mv[:, q], stats[:, q])
                link(ins)
                dve.tensor_scalar(rstd[:], mv[:, :, 1], LN_EPS, None, ALU.add).then_inc(var_rdy, 1)
                dve.wait_ge(rstd_rdy, k + 1)
                for q in range(QC):
                    ins = dve.tensor_scalar(dst(q), src(q), mv[:, q, 0:1], rstd[:, q:q + 1], ALU.subtract, ALU.mult)
                return ins

            with dve.Fori(0, B) as b:
                chain.at(b * DVE_LINKS + prep_links)
                dve.wait_ge(q_hi_rdy, b + 1)
                dve.scalar_tensor_tensor(out=q_lo, in0=psW[:, 1, :].rearrange("p (k n) -> p k n", k=FC), scalar=SCALE,
                                         in1=q_hi.bitcast(F32), op0=ALU.mult, op1=ALU.subtract).then_inc(q_lo_rdy, 1)
                dve.wait_ge(k_hi_rdy, b + 1)
                dve.tensor_tensor(k_lo, psW[:, 2, :].rearrange("p (k n) -> p k n", k=FC), k_hi.bitcast(F32),
                                  ALU.subtract).then_inc(k_lo_rdy, 1)
                for i in range(4):
                    dve.wait_ge(k4_ps, 4 * b + i + 1)
                    dve.tensor_copy(k4[:, 2 * i:2 * i + 2, :],
                                    psW[:, i, :].rearrange("p (j n) -> p j n", j=2)).then_inc(k4_rdy, 1)
                for p in range(PAIRS):
                    dve.wait_ge(score_ps, b * PAIRS + p + 1)
                    w0 = 2 * (p % 2)
                    dve.tensor_reduce(negmax[:, 0, 2 * p:2 * p + 2], psW[:, w0:w0 + 2, 0:P], AX_X, ALU.max, negate=True)
                    dve.tensor_reduce(negmax[:, 1, 2 * p:2 * p + 2], psW[:, w0:w0 + 2, P:SCORE], AX_X, ALU.max,
                                      negate=True).then_inc(max_rdy, 1)
                    if p in (3, 7):
                        ssm_pair(b, p // 4)
                dve.wait_ge(max_rdy, (b + 1) * PAIRS)
                link(dve.tensor_copy(negmax_p[:, :, 0:HEADS], negmax[:]))
                link(dve.tensor_tensor(negmax_r[:], negmax[:], negmax_p[:, :, 0:HEADS], ALU.subtract))
                link(dve.tensor_copy(negmax_p[:, :, BC:BC + HEADS], negmax_r[:]))
                dve.tensor_tensor(negmax_p[:, :, 2 * BC:2 * BC + HEADS], negmax_r[:], negmax_p[:, :, BC:BC + HEADS],
                                  ALU.subtract).then_inc(nm_rdy, 1)
                dve.wait_ge(nmT_ps, b + 1)
                dve.tensor_copy(nmT[:], psT_b[0:3 * BC, 0:S].rearrange("p (q n) -> p q n", q=QC)).then_inc(nmT_rdy, 1)
                for m in range(2, NP):
                    ssm_pair(b, m)
                dve.wait_ge(pv_ps, (b + 1) * PAIRS + 2)
                pv = psT[:, :, 0:HEADS * (HD + 1)].rearrange("p q (h d) -> p q h d", h=HEADS)
                link(dve.reciprocal(negmax[:].rearrange("p q (h o) -> p q h o", o=1), pv[:, :, :, HD:HD + 1]))
                for q in range(QC):
                    ins = dve.tensor_tensor(
                        heads[:, q].rearrange("p (h d) -> p h d", h=HEADS), pv[:, q, :, 0:HD],
                        negmax[:, q].rearrange("p (h o) -> p h o", o=1).broadcast_to([P, HEADS, HD]), ALU.mult)
                ins.then_inc(heads_rdy, 1)
                dve.wait_ge(attn_ps, b + 1)
                dve.wait_ge(x2_kept, b + 1)
                dve.tensor_tensor(x1[:], psW[:, 1, :].rearrange("p (q n) -> p q n", q=QC), x_in[:],
                                  ALU.add).then_inc(res_rdy, 1)
                dve.wait_ge(res_rdy, b + 1)
                layer_norm(2 * b, lambda q: x1[:, q], lambda q: x1[:, q]).then_inc(x1_rdy, 1)
                dve.wait_ge(x1_rdy, b + 1)
                dve.wait_ge(tanh_rdy, b + 1)
                link(dve.scalar_tensor_tensor(out=gated[:], in0=gated[:], scalar=1.0, in1=x1[:], op0=ALU.add,
                                              op1=ALU.mult))
                dve.wait_ge(y_added, (b + 1) * DS + 4)
                link(dve.tensor_tensor(y_sum[:], u_sb[:, bass.ds(b, 1)].rearrange("p o h s -> p (o h) s"), y_sum[:],
                                       ALU.add))
                dve.scalar_tensor_tensor(out=gated[:], in0=y_sum[:], scalar=0.5, in1=gated[:], op0=ALU.mult,
                                         op1=ALU.mult).then_inc(gated_rdy, 1)
                dve.wait_ge(gatedT_ps, b + 1)
                link(dve.tensor_tensor(x1[:], psT[:, 0, :].rearrange("p (q n) -> p q n", q=QC), x1[:], ALU.add))
                layer_norm(2 * b + 1, lambda q: x1[:, q], lambda q: x1[:, q]).then_inc(x2_rdy, 1)
                dve.wait_ge(x2T_rdy, 2 * b + 2)
                dve.tensor_tensor(x2T_lo[:, :, bass.ds(b * S, S)], psT[:, 1, :].rearrange("p (k n) -> p k n", k=FC),
                                  x2T_hi[:, :, bass.ds(b * S, S)].bitcast(F32), ALU.subtract).then_inc(x2lo_rdy, 1)
                dve.wait_ge(logit_ps, b + 1)
                dve.tensor_reduce(small[:, 0, :], psT[:, 0, 0:QC * NE].rearrange("p (q e) -> p q e", q=QC), AX_X,
                                  ALU.max, negate=True).then_inc(lmax_rdy, 1)
                dve.wait_ge(lexp_rdy, 2 * b + 2)
                link(dve.tensor_reduce(small[:, 1, :], probs[:], AX_X, ALU.add))
                link(dve.reciprocal(small[:, 2, :], small[:, 1, :]))
                for q in range(QC):
                    dve.tensor_scalar(probs[:, q], probs[:, q], small[:, 2, q:q + 1], DOWN_MULT, ALU.mult, ALU.mult)
                dve.drain()
                for q in range(QC):
                    dve.max(top_val[:, q], probs[:, q])
                dve.drain()
                for q in range(QC):
                    dve.max_index(top_idx[:, q], top_val[:, q], probs[:, q])
                dve.drain()
                link(dve.tensor_copy(top_idx_f[:], top_idx[:]))
                for q in range(QC):
                    link(dve.tensor_scalar(probs[:, q], iota8[:], top_idx_f[:, q, 0:1], top_val[:, q, 0:1],
                                           ALU.is_equal, ALU.mult))
                    link(dve.tensor_scalar(w_second[:, q], iota8[:], top_idx_f[:, q, 1:2], top_val[:, q, 1:2],
                                           ALU.is_equal, ALU.mult))
                link(dve.tensor_tensor(w_tok[:, bass.ds(2 * b, QC), :], probs[:], w_second[:], ALU.add))
                assert chain.n == DVE_LINKS, chain.n

            def hidden(e, th, c):
                k = (e * TH + th) * IC + c
                dve.wait_ge(silu_rdy, k + 1)
                if not (isinstance(e, int) and e == 0 and th == 0 and c < 2):
                    dve.wait_ge(hlo_rdy, k - 1)
                dve.tensor_tensor(h_f[:, c % 2], silu_g[:, c % 2], psW[:, 2 + c % 2, :], ALU.mult).then_inc(h_rdy, 1)

            def accumulate(e, th, i, e_of):
                t = th * (NT // TH) + i
                dve.wait_ge(down_ps, e * NT + t + 1)
                bank = psS[:, i, :] if i < 2 else psT[:, i - 2, :]
                wt = w_tok[:, t, e_of] if isinstance(e, int) else w_tok[:, t, bass.ds(e, 1)]
                dve.scalar_tensor_tensor(out=x_sb[:, t], in0=bank[:, 0:HID], scalar=wt, in1=x_sb[:, t], op0=ALU.mult,
                                         op1=ALU.add).then_inc(summed, 1)
                dve.wait_ge(summed, 2 * (e * NT + t) + 1)
                dve.scalar_tensor_tensor(out=x_sb[:, t], in0=bank[:, HID:], scalar=wt, in1=x_sb[:, t], op0=ALU.mult,
                                         op1=ALU.add).then_inc(summed, 1)

            def expert(e, first=False):
                e_of = slice(e, e + 1) if isinstance(e, int) else None
                e_before = slice(e - 1, e) if isinstance(e, int) else None
                for c in range(IC):
                    hidden(e, 0, c)
                if not first:
                    for i in range(4):
                        accumulate(e - 1, 1, i, e_before)
                for c in range(IC):
                    hidden(e, 1, c)
                for i in range(4):
                    accumulate(e, 0, i, e_of)

            dve.wait_ge(logit_ps, B)
            dve.wait_ge(x2_kept, B + 1)
            expert(0, first=True)
            with dve.Fori(0, (NE - 2) // 2) as j:
                expert(2 * j + 1)
                expert(2 * j + 2)
            expert(NE - 1)
            for i in range(4):
                accumulate(NE - 1, 1, i, slice(NE - 1, NE))
            dve.wait_ge(summed, 2 * NE * NT)
            chain.at(prep_links + B * DVE_LINKS)
            for t in range(NT // QC):
                layer_norm(2 * B + t, lambda q: x_sb[:, 2 * t + q], lambda q: x_sb[:, 2 * t + q]).then_inc(final_rdy, 2)

        @block.tensor
        def _(pe):
            def transposes(bank_of, src_of, n, m, ident_of, done):
                for i in range(n):
                    for j in range(m):
                        ins = pe.transpose(bank_of(i, j), src_of(i, j), ident_of)
                ins.then_inc(done, 1)

            pe.wait_ge(consts, 1)
            pe.wait_ge(ld_ctx, 16)
            transposes(lambda i, j: psW[:, i, j * P:(j + 1) * P], lambda i, j: c_ctx[:, 4 * i + j, :], 2, 4, ident[:],
                       ctxT_ps)
            pe.wait_ge(ld_ssm, 48)
            for h in range(HALVES):
                pe.transpose(psW[:, 2, h * P:(h + 1) * P], win_raw[:, h, :], ident[:])
                n = DR + BC
                pe.transpose(psW[:, 2, DI + h * n:DI + (h + 1) * n], xp_raw[0:n, h * P:(h + 1) * P], ident[0:n, 0:n])
                ins = pe.transpose(psW[0:DR, 3, h * P:(h + 1) * P], dtw_raw[:, h, :], ident[:])
            ins.then_inc(ssmT_ps, 1)
            pe.wait_ge(ctxT_rdy, 1)
            pe.wait_ge(ssmT_rdy, 1)
            for half in range(HALVES):
                for th in range(TH):
                    pe.matmul(psW[:, half * TH + th, :], winT[:, half * P:(half + 1) * P],
                              ctxT[:, th * BANK:(th + 1) * BANK], start=True, stop=True).then_inc(xin_ps, 1)
            pe.wait_ge(ld_attn, 64)
            for i in range(4):
                bank = psS[:, i, :] if i < 2 else psT[:, i - 2, :]
                transposes(lambda k, c: bank[:, k * HID + c * P:k * HID + (c + 1) * P],
                           lambda k, c: w_raw[:, i, c, k * P:(k + 1) * P], FC, FC, ident[:], wT_ps)
            pe.wait_ge(u_rdy, 2)
            for th in range(TH):
                for half in range(HALVES):
                    ins = pe.matmul(psW[0:3 * BC + DR, th, :], xpT[:, half, :],
                                    u_sb[:, BH * th:BH * (th + 1), half, :], start=(half == 0),
                                    stop=(half == HALVES - 1))
                ins.then_inc(xdbl_ps, 1)
            pe.wait_ge(dt_rdy, 2)
            for half in range(HALVES):
                for th in range(TH):
                    pe.matmul(psW[:, (2 + half * TH + th) % 4, :], dtwT[0:DR, half * P:(half + 1) * P],
                              dt_lo[0:DR, th * BANK:(th + 1) * BANK], start=True, stop=True).then_inc(delta_ps, 1)

            def broadcast_bc(b, m):
                g = b * NP + m
                tokens = bc_parts[:, bass.ds(b * S, S)]
                pe.wait_ge(b_used, g + 1)
                for n in range(2):
                    ins = pe.matmul(psS[:, 0, n * S:(n + 1) * S], pick[:, 2 * m + n, :], tokens, start=True, stop=True)
                ins.then_inc(bc_ps, 1)
                pe.wait_ge(hC_rdy, g + 1)
                for n in range(2):
                    ins = pe.matmul(psS[:, 1, n * S:(n + 1) * S], pick[:, DS + 2 * m + n, :], tokens, start=True,
                                    stop=True)
                ins.then_inc(bc_ps, 1)

            def pv(b, p):
                pe.wait_ge(probT_rdy, b * PAIRS + p + 1)
                for a in range(2):
                    h = 2 * p + a
                    pr = probT[:, p % 2, a]
                    cols = slice(h * (HD + 1), (h + 1) * (HD + 1))
                    pe.matmul(psT[:, 0, cols], pr[:, 0:P], v1[:, 0, h, :], start=True, stop=True)
                    pe.matmul(psT[:, 1, cols], pr[:, P:S], v1[:, 0, h, :], start=True, stop=False)
                    ins = pe.matmul(psT[:, 1, cols], pr[:, S:SCORE], v1[:, 1, h, :], start=False, stop=True)
                ins.then_inc(pv_ps, 1)

            pe.wait_ge(relu_rdy, 4)
            pe.wait_ge(act_chain, 4)
            pe.wait_ge(wT_rdy, 4)
            pe.wait_ge(area_free, 1)
            pe.wait_ge(consts_b, 1)
            pe.nop().then_inc(pv_ps, 2)
            with pe.Fori(0, B) as b:
                pe.wait_ge(ld_x, 16 * b + 16)
                for q in range(QC):
                    for k in range(FC):
                        ins = pe.transpose(psW[:, 0, k * S + q * P:k * S + (q + 1) * P],
                                           x_in[:, q, k * P:(k + 1) * P], ident[:])
                ins.then_inc(xT_ps, 1)
                broadcast_bc(b, 0)
                pe.wait_ge(xT_rdy, b + 1)
                for i, done in ((0, q_ps), (1, k_ps)):
                    for c in range(FC):
                        for k in range(FC):
                            ins = pe.matmul(psW[:, 1 + i, c * S:(c + 1) * S], wT[:, i, k, c * P:(c + 1) * P], xT[:, k, :],
                                            start=(k == 0), stop=(k == FC - 1))
                    ins.then_inc(done, 1)
                for q in range(QC):
                    for k in range(FC):
                        ins = pe.matmul(psW[:, 3, q * HID:(q + 1) * HID], xT[:, k, q * P:(q + 1) * P], wT[:, 2, k, :],
                                        start=(k == 0), stop=(k == FC - 1))
                ins.then_inc(v_ps, 1)
                for qk, hi, lo, rdy_hi, rdy_lo, done in ((0, q_hi, q_lo, q_hi_rdy, q_lo_rdy, q4_ps),
                                                         (1, k_hi, k_lo, k_hi_rdy, k_lo_rdy, k4_ps)):
                    pe.wait_ge(rdy_hi, b + 1)
                    pe.wait_ge(rdy_lo, b + 1)
                    for i in range(4):
                        if qk == 1:
                            pe.wait_ge(q4_rdy, 4 * b + i + 1)
                        elif i == 2:
                            pe.wait_ge(k_lo_rdy, b + 1)
                        elif i == 3:
                            pe.wait_ge(v_rdy, b + 1)
                        for j in range(2):
                            t, jj = (2 * i + j) // TILE_PAIRS, (2 * i + j) % TILE_PAIRS
                            pe.matmul(psW[:, i, j * S:(j + 1) * S], pickQK[:, qk, 0, jj, :], hi[:, t, :], start=True,
                                      stop=False)
                            ins = pe.matmul(psW[:, i, j * S:(j + 1) * S], pickQK[:, qk, 1, jj, :], lo[:, t, :],
                                            start=False, stop=True)
                        ins.then_inc(done, 1)
                pe.wait_ge(q4_rdy, 4 * b + 4)
                pe.wait_ge(k4_rdy, 4 * b + 4)
                for p in range(PAIRS):
                    if p >= 2:
                        pe.wait_ge(max_rdy, b * PAIRS + p - 1)
                    for a in range(2):
                        bank = psW[:, 2 * (p % 2) + a, :]
                        rows = slice(64 * a, 64 * a + 64)
                        pe.matmul(bank[:, 0:P], q4[rows, p, 0:P], k4[rows, p, 0:P], start=True, stop=False)
                        pe.matmul(bank[:, 0:P], ident_b[:], mask_qk[:], start=False, stop=True)
                        pe.matmul(bank[:, P:SCORE], q4[rows, p, P:S], k4[rows, p, :], start=True, stop=True)
                        ins = pe.matmul(bank[:, S:SCORE], ident_b[:], mask_qk[:], start=False, stop=True,
                                        skip_group_check=True)
                    ins.then_inc(score_ps, 1)
                    if p == 3:
                        broadcast_bc(b, 1)
                pe.wait_ge(nm_rdy, b + 1)
                for q in range(QC):
                    ins = pe.transpose(psT_b[0:3 * BC, q * P:(q + 1) * P], negmax_p[:, q, :], ident_b[:])
                ins.then_inc(nmT_ps, 1)
                pe.wait_ge(nmT_rdy, b + 1)
                for p in range(PAIRS):
                    if p < NP - 2:
                        broadcast_bc(b, p + 2)
                    if p >= 2:
                        pe.wait_ge(probT_rdy, b * PAIRS + p - 1)
                    for a in range(2):
                        bank = psW[:, 2 * (p % 2) + a, :]
                        rows = slice(64 * a, 64 * a + 64)
                        h = 2 * p + a
                        pe.matmul(bank[:, 0:S], k4[rows, p, 0:P], q4[rows, p, :], start=True, stop=False)
                        pe.matmul(bank[:, 0:S], pick[:, h, :], nmT[:].rearrange("p q n -> p (q n)"), start=False,
                                  stop=True)
                        pe.matmul(bank[:, 0:P], ident_b[:], mask_kq[:], start=False, stop=True, skip_group_check=True)
                        pe.matmul(bank[:, S:SCORE], k4[rows, p, P:S], q4[rows, p, P:S], start=True, stop=False,
                                  skip_group_check=True)
                        pe.matmul(bank[:, S:SCORE], pick[:, h, :], nmT[:, 1, :], start=False, stop=False,
                                  skip_group_check=True)
                        ins = pe.matmul(bank[:, S:SCORE], ident_b[:], mask_kq[:], start=False, stop=True,
                                        skip_group_check=True)
                    ins.then_inc(scoreT_ps, 1)
                    if p > 0:
                        pv(b, p - 1)
                pv(b, PAIRS - 1)
                pe.wait_ge(heads_rdy, b + 1)
                for q in range(QC):
                    for k in range(FC):
                        ins = pe.transpose(psW[:, 0, k * S + q * P:k * S + (q + 1) * P], heads[:, q, k * P:(k + 1) * P],
                                           ident[:])
                ins.then_inc(headsT_ps, 1)
                pe.wait_ge(headsT_rdy, b + 1)
                for q in range(QC):
                    for k in range(FC):
                        ins = pe.matmul(psW[:, 1, q * HID:(q + 1) * HID], xT[:, k, q * P:(q + 1) * P], wT[:, 3, k, :],
                                        start=(k == 0), stop=(k == FC - 1))
                ins.then_inc(attn_ps, 1)
                pe.wait_ge(gated_rdy, b + 2)
                for q in range(QC):
                    for k in range(HALVES):
                        ins = pe.transpose(psT[:, 0, q * HID + k * P:q * HID + (k + 1) * P], gated[:, k, q * P:(q + 1) * P],
                                           ident[:])
                ins.then_inc(gatedT_ps, 1)
                pe.wait_ge(x2_rdy, b + 1)
                for q in range(QC):
                    for k in range(FC):
                        ins = pe.transpose(psT[:, 1, k * S + q * P:k * S + (q + 1) * P],
                                           x1[:, q, k * P:(k + 1) * P], ident[:])
                ins.then_inc(x2T_ps, 1)
                pe.wait_ge(x2T_rdy, 2 * b + 2)
                for q in range(QC):
                    for k in range(FC):
                        ins = pe.matmul(psT[:, 0, q * NE:(q + 1) * NE], xT[:, k, q * P:(q + 1) * P], wr_sb[:, k, :],
                                        start=(k == 0), stop=(k == FC - 1))
                ins.then_inc(logit_ps, 1)
                pe.wait_ge(lexp_rdy, 2 * b + 2)
                pe.wait_ge(x2lo_rdy, b + 1)

            def gate_up(e, odd, th, c):
                k = (e * TH + th) * IC + c
                if not (isinstance(e, int) and e == 0 and th == 0 and c < 2):
                    pe.wait_ge(h_rdy, k - 1)
                for mat in range(2):
                    bank = psW[:, 2 * mat + c % 2, :]
                    n = 0
                    for part, xT_part in ((0, x2T_hi), (0, x2T_lo), (1, x2T_hi)):
                        for kk in range(FC):
                            ins = pe.matmul(bank, eg[:, odd, part, mat, kk, c * P:(c + 1) * P],
                                            xT_part[:, kk, th * BANK:(th + 1) * BANK], start=(n == 0), stop=(n == 5))
                            n += 1
                ins.then_inc(gu_ps, 1)

            def down(e, odd, th, i):
                t = th * (NT // TH) + i
                if not (isinstance(e, int) and e == 0 and th == 0):
                    pe.wait_ge(summed, 2 * (e * NT + t - 3))
                bank = psS[:, i, :] if i < 2 else psT[:, i - 2, :]
                cols = slice(i * P, (i + 1) * P)
                for c in range(IC):
                    pe.matmul(bank, h_hi[:, th, c, cols], ed[:, odd, c].rearrange("p l n -> p (l n)"), start=(c == 0),
                              stop=(c == IC - 1))
                for c in range(IC):
                    ins = pe.matmul(bank[:, 0:HID], h_lo[:, th, c, cols], ed[:, odd, c, 0, :], start=False,
                                    stop=(c == IC - 1), skip_group_check=True)
                ins.then_inc(down_ps, 1)

            def expert(e, odd, first=False):
                pe.wait_ge(elo_rdy, 3 * e + 3)
                for c in range(IC):
                    gate_up(e, odd, 0, c)
                if not first:
                    pe.wait_ge(hlo_rdy, e * TH * IC)
                    for i in range(4):
                        down(e - 1, 1 - odd, 1, i)
                for c in range(IC):
                    gate_up(e, odd, 1, c)
                pe.wait_ge(hlo_rdy, (e * TH + 1) * IC)
                for i in range(4):
                    down(e, odd, 0, i)

            expert(0, 0, first=True)
            with pe.Fori(0, (NE - 2) // 2) as j:
                expert(2 * j + 1, 1)
                expert(2 * j + 2, 0)
            expert(NE - 1, 1)
            pe.wait_ge(hlo_rdy, NE * TH * IC)
            for i in range(4):
                down(NE - 1, 1, 1, i)


_INS = ['x', 'ctx_1024', 'L0_attn_Wq', 'L0_attn_Wk', 'L0_attn_Wv', 'L0_attn_Wo', 'L0_xattn_in_proj_w',
        'L0_xattn_conv_w', 'L0_xattn_conv_b', 'L0_xattn_x_proj_w', 'L0_xattn_dt_proj_w', 'L0_xattn_dt_proj_b',
        'L0_xattn_A_log', 'L0_xattn_D', 'L0_ffn_w_router', 'L0_ffn_w_gate', 'L0_ffn_w_up', 'L0_ffn_w_down']
_OUTS = [((4, 256, 256), 'float32')]


def kernel(**inputs):
    import numpy as _np
    import concourse.bacc as _bacc
    from concourse import mybir as _mybir
    from concourse.bass_utils import run_bass_kernel_spmd as _run

    nc = _bacc.Bacc("TRN2", target_bir_lowering=False, num_devices=1)
    arrays, args = {}, []
    for name in _INS:
        a = _np.ascontiguousarray(inputs[name])
        arrays[f"in_{name}_dram"] = a
        args.append(nc.dram_tensor(f"in_{name}_dram", a.shape, _mybir.dt.from_np(a.dtype), kind="ExternalInput").ap())
    for i, (shape, dtype) in enumerate(_OUTS):
        dt = _mybir.dt.from_np(_np.dtype(dtype))
        args.append(nc.dram_tensor(f"out_{i}_dram", shape, dt, kind="ExternalOutput").ap())
    decoder_layer(nc, *args)
    r = _run(nc, [arrays], core_ids=[0])
    got = tuple(r.results[0][f"out_{i}_dram"] for i in range(len(_OUTS)))
    return got[0]
```

```python
from contextlib import ExitStack

import concourse.bass as bass
from concourse import mybir

F32 = mybir.dt.float32
F32R = mybir.dt.float32r
BF16 = mybir.dt.bfloat16
U32 = mybir.dt.uint32
ALU = mybir.AluOpType
ACT = mybir.ActivationFunctionType
AX_X = mybir.AxisListType.X

P = 128
LN_EPS = 1e-5
MASKED = -1e38
GATE_MULT = 0.5
DOWN_MULT = 0.25
BANK = 512

DVE_LINKS = 8


class Chain:

    def __init__(self, engine, semaphore):
        self.engine, self.semaphore, self.base, self.n = engine, semaphore, 0, 0

    def at(self, base):
        self.base, self.n = base, 0

    def link(self, ins):
        self.n += 1
        ins.then_inc(self.semaphore, 1)
        self.engine.wait_ge(self.semaphore, self.base + self.n)


def carve(tensor, at, *shape):
    n = 1
    for s in shape:
        n *= s
    view = tensor[:, at:at + n]
    if len(shape) > 1:
        names = "abcde"[: len(shape)]
        view = view.rearrange(f"p ({' '.join(names)}) -> p {' '.join(names)}", **dict(zip(names, shape)))
    return view, at + n


def decoder_layer(
    nc: bass.Bass,
    x: bass.AP,
    ctx_in: bass.AP,
    Wq: bass.AP,
    Wk: bass.AP,
    Wv: bass.AP,
    Wo: bass.AP,
    in_proj_w: bass.AP,
    conv_w: bass.AP,
    conv_b: bass.AP,
    x_proj_w: bass.AP,
    dt_proj_w: bass.AP,
    dt_proj_b: bass.AP,
    A_log: bass.AP,
    D_skip: bass.AP,
    w_router: bass.AP,
    w_gate: bass.AP,
    w_up: bass.AP,
    w_down: bass.AP,
    out: bass.AP,
):
    B, S, HID = x.shape
    DM = ctx_in.shape[2]
    DI, DC = conv_w.shape
    DS = A_log.shape[1]
    DR = dt_proj_w.shape[1]
    NE, _, INTER = w_gate.shape
    HEADS = 16
    HD = HID // HEADS
    QC = S // P
    FC = HID // P
    NT = B * QC
    T = B * S
    HALVES = DI // P
    PAIRS = HEADS // 2
    TILE_PAIRS = PAIRS // FC
    IC = INTER // P
    SCORE = P + S
    SCALE = float(HD) ** -0.5
    BC = 2 * DS
    NP = DS // 2
    TH = T // BANK
    BH = B // TH
    assert DM == P and DI == S == HID and QC == FC == HALVES == 2 and HD == 16 and BC == 32 and TH == 2

    with ExitStack() as stack:
        def sb(name, shape, dt=F32):
            return stack.enter_context(nc.sbuf_tensor(name, shape, dt))

        def sem(name):
            return stack.enter_context(nc.semaphore(name))

        ident = sb("ident", [P, P])
        ident_b = sb("ident_b", [P, P], BF16)
        mask_qk = sb("mask_qk", [P, P], BF16)
        mask_kq = sb("mask_kq", [P, P], BF16)
        rows32 = sb("rows32", [3 * BC, BC])
        pick = sb("pick", [3 * BC, BC, P], BF16)
        iota8 = sb("iota8", [P, NE])
        exponent = sb("exponent", [P, QC])
        wT = sb("wT", [P, 4, FC, HID])
        wr_sb = sb("wr_sb", [P, FC, NE])
        convw_sb = sb("convw_sb", [P, HALVES, DC])
        vec_sb = sb("vec_sb", [P, 3, HALVES])
        A_sb = sb("A_sb", [P, HALVES, DS])
        delta = sb("delta", [P, B, HALVES, S])
        du = sb("du", [P, B, HALVES, S])
        u_sb = sb("u_sb", [P, B, HALVES, S])
        y_sum = sb("y_sum", [P, HALVES, S])
        bc_parts = sb("bc_parts", [3 * BC, T], BF16)
        x_in = sb("x_in", [P, QC, HID])
        x_res = sb("x_res", [P, QC, HID])
        x_sb = sb("x_sb", [P, NT, HID])
        x2T_hi = sb("x2T_hi", [P, FC, T], F32R)
        x2T_lo = sb("x2T_lo", [P, FC, T], F32R)
        w_tok = sb("w_tok", [P, NT, NE])
        x1 = sb("x1", [P, QC, HID])
        gated = sb("gated", [P, HALVES, S])
        stats = sb("stats", [P, QC, 6])
        mv = sb("mv", [P, QC, 2])
        rstd = sb("rstd", [P, QC])
        wr_split = sb("wr_split", [P, FC, 2, NE], F32R)
        top_idx = sb("top_idx", [P, NT, 8], U32)
        negmax = sb("negmax", [P, QC, HEADS])
        negmax_r = sb("negmax_r", [P, QC, HEADS])
        negmax_p = sb("negmax_p", [P, QC, 3 * BC], BF16)
        nmT = sb("nmT", [3 * BC, QC, P], BF16)
        e_raw = sb("e_raw", [P, 6 * INTER])
        SPLIT_W = 4 * FC * INTER + 2 * IC * HID
        weights = sb("weights", [P, 2, SPLIT_W], F32R)
        eg, ed = [], []
        for buf in range(2):
            view, at = carve(weights[:, buf], 0, 2, 2, FC, INTER)
            eg.append(view)
            view, at = carve(weights[:, buf], at, IC, 2, HID)
            ed.append(view)
        V_AT, ONES_AT = P // 2 - HD, P - HD
        v_second = sb("v_second", [P, HEADS * P])
        v_pad = [e_raw[:, 0:HEADS * P], v_second[:]]
        xT, at = carve(e_raw, HEADS * P, FC, S)
        hT, at = carve(e_raw, at, FC, S)
        assert at <= e_raw.shape[1]

        def v_columns(q, at):
            return v_pad[q].rearrange("p (h n) -> p h n", n=P)[:, :, at:at + HD]

        RAW = FC * INTER
        assert IC * HID == RAW and 2 * RAW == NT * HID
        x_flat = x_sb[:].rearrange("p t n -> p (t n)")
        raw_first = [x_flat[:, 0:RAW], x_flat[:, RAW:], x_flat[:, 0:RAW]]

        def raw_matrix(e, i):
            raw = raw_first[i] if isinstance(e, int) and e == 0 else e_raw[:, i * RAW:(i + 1) * RAW]
            return raw.rearrange("p (k n) -> p k n", k=FC if i < 2 else IC)

        area = sb("area", [P, 7168])
        win_raw, at = carve(area, 0, HALVES, DM)
        winT, at = carve(area, at, DI)
        xp_raw, at = carve(area, at, DI)
        xpT, at = carve(area, at, HALVES, 3 * BC + DR)
        dtw_raw, at = carve(area, at, HALVES, DR)
        dtwT, at = carve(area, at, DI)
        conv, at = carve(area, at, B, HALVES, S)
        dt_lo, _ = carve(conv.rearrange("p b h s -> p (b h s)"), 0, T)
        log_rest = conv
        xpad, at = carve(area, at, HALVES, B, DC - 1 + S)
        ln_part, _ = carve(xpad.rearrange("p h b s -> p (h b s)"), 0, B, HALVES, S)
        bc_r, at = carve(area, at, T)
        assert at <= area.shape[1]
        du_flat = du[:].rearrange("p b h s -> p (b h s)")
        c_ctx, at = carve(du_flat, 0, NT, DM)
        ctxT, at = carve(du_flat, at, T)
        w_raw, _ = carve(e_raw, 0, 4, FC, HID)

        dA, at = carve(area, 0, 2, 2, HALVES, S)
        dBu, at = carve(area, at, 2, 2, HALVES, S)
        state, at = carve(area, at, 2, HALVES, S)
        probT, at = carve(area, at, 2, 2, SCORE)
        pv_num = gated[:].rearrange("p h s -> p h s")
        pv_den, at = carve(area, at, FC, S)
        assert at <= area.shape[1]
        silu_g, at = carve(area, 0, 2, BANK)
        h_f, at = carve(area, at, 2, BANK)
        assert at <= 2 * 2 * HALVES * S
        logits, at = carve(area, 2 * 2 * HALVES * S, 2, NT, NE)
        small, at = carve(area, at, 3, NT)
        probs, at = carve(area, at, NT, NE)
        top_val, at = carve(area, at, NT, 8)
        top_idx_f, at = carve(area, at, NT, 8)
        picked, at = carve(area, at, 2, NT, NE)

        split = sb("split", [P, 8192], F32R)
        q4, at = carve(split, 0, PAIRS, S)
        k4, at = carve(split, at, PAIRS, S)
        pickQK, at = carve(split, at, 2, 2, TILE_PAIRS, P)
        q_hi, at = carve(split, at, FC, S)
        q_lo, at = carve(split, at, FC, S)
        k_hi, at = carve(split, at, FC, S)
        k_lo, at = carve(split, at, FC, S)
        assert at <= split.shape[1]
        h_hi, at = carve(split, 0, 2, IC, BANK)
        h_lo, at = carve(split, at, 2, IC, BANK)
        assert at <= split.shape[1]

        psW = stack.enter_context(nc.psum_tensor("psW", [P, 4, BANK], F32))
        psS = stack.enter_context(nc.psum_tensor("psS", [P, 2, BANK], F32))
        psT = stack.enter_context(nc.psum_tensor("psT", [P, 2, BANK], F32))
        psT_b = psT[:, 0, :].bitcast(BF16)

        def bank4(i):
            return psS[:, i, :] if i < 2 else psT[:, i - 2, :]


        ld_ctx, ld_ssm, ld_small, ld_x, ld_attn = (sem(s) for s in ("ld_ctx", "ld_ssm", "ld_small", "ld_x", "ld_attn"))
        ld_expert, stored = sem("ld_expert"), sem("stored")
        consts, consts_b, zeroed = sem("consts"), sem("consts_b"), sem("zeroed")
        inverted = sem("inverted")
        rows_rdy, pick_rdy, v_pad_rdy, ld_res = sem("rows_rdy"), sem("pick_rdy"), sem("v_pad_rdy"), sem("ld_res")
        dve_chain, act_chain, pool_chain = sem("dve_chain"), sem("act_chain"), sem("pool_chain")
        ctxT_ps, ctxT_rdy, ssmT_ps, ssmT_rdy = sem("ctxT_ps"), sem("ctxT_rdy"), sem("ssmT_ps"), sem("ssmT_rdy")
        xin_ps, xpad_rdy, wT_ps, wT_rdy = sem("xin_ps"), sem("xpad_rdy"), sem("wT_ps"), sem("wT_rdy")
        conv_rdy, u_rdy, xdbl_ps, dt_rdy = sem("conv_rdy"), sem("u_rdy"), sem("xdbl_ps"), sem("dt_rdy")
        delta_ps, relu_rdy, exp_rdy, ln_rdy = sem("delta_ps"), sem("relu_rdy"), sem("exp_rdy"), sem("ln_rdy")
        A_rdy, ssm_rdy, area_free = sem("A_rdy"), sem("ssm_rdy"), sem("area_free")
        bc_ps, dA_rdy = sem("bc_ps"), sem("dA_rdy")
        b_used, scanned, hC_rdy, y_added = sem("b_used"), sem("scanned"), sem("hC_rdy"), sem("y_added")
        xT_ps, xT_rdy, q_ps, k_ps, v_ps = (sem(s) for s in ("xT_ps", "xT_rdy", "q_ps", "k_ps", "v_ps"))
        q_hi_rdy, k_hi_rdy, q_lo_rdy, k_lo_rdy, v_rdy = (
            sem(s) for s in ("q_hi_rdy", "k_hi_rdy", "q_lo_rdy", "k_lo_rdy", "v_rdy"))
        q4_ps, q4_rdy, k4_ps, k4_rdy = sem("q4_ps"), sem("q4_rdy"), sem("k4_ps"), sem("k4_rdy")
        score_ps, max_rdy, nm_rdy, nmT_ps, nmT_rdy = (
            sem(s) for s in ("score_ps", "max_rdy", "nm_rdy", "nmT_ps", "nmT_rdy"))
        scoreT_ps, probT_rdy, pv_ps, num_dve = sem("scoreT_ps"), sem("probT_rdy"), sem("pv_ps"), sem("num_dve")
        num_act, hT_rdy, attn_ps, x1_rdy = sem("num_act"), sem("hT_rdy"), sem("attn_ps"), sem("x1_rdy")
        res_rdy, x2_kept = sem("res_rdy"), sem("x2_kept")
        var_rdy, rstd_rdy = sem("var_rdy"), sem("rstd_rdy")
        tanh_rdy, gated_rdy, gatedT_ps, x2_rdy = sem("tanh_rdy"), sem("gated_rdy"), sem("gatedT_ps"), sem("x2_rdy")
        x2T_ps, x2T_rdy, x2lo_rdy, logit_ps = sem("x2T_ps"), sem("x2T_rdy"), sem("x2lo_rdy"), sem("logit_ps")
        logit_taken, shifted, lexp_rdy = sem("logit_taken"), sem("shifted"), sem("lexp_rdy")
        ehi_rdy, elo_rdy = sem("ehi_rdy"), sem("elo_rdy")
        gu_ps, silu_rdy, h_rdy, hhi_rdy, hlo_rdy = (
            sem(s) for s in ("gu_ps", "silu_rdy", "h_rdy", "hhi_rdy", "hlo_rdy"))
        down_ps, summed, final_rdy = sem("down_ps"), sem("summed"), sem("final_rdy")

        block = stack.enter_context(nc.Block())

        @block.sync
        def _(sp):
            sp.dma_start(c_ctx, ctx_in.rearrange("b (q p) d -> p (b q) d", p=P)).then_inc(ld_ctx, 16)
            sp.dma_start(win_raw, in_proj_w.rearrange("(h p) d -> p h d", p=P)).then_inc(ld_ssm, 16)
            sp.dma_start(xp_raw[0:DR + BC, :], x_proj_w).then_inc(ld_ssm, 16)
            sp.dma_start(dtw_raw, dt_proj_w.rearrange("(h p) r -> p h r", p=P)).then_inc(ld_ssm, 16)
            sp.dma_start(convw_sb[:], conv_w.rearrange("(h p) k -> p h k", p=P)).then_inc(ld_small, 16)
            for i, v in enumerate((conv_b, dt_proj_b, D_skip)):
                with nc.allow_non_contiguous_dma(reason="256 values, one to a partition"):
                    sp.dma_start(vec_sb[:, i, :], v.rearrange("(h p) -> p h", p=P)).then_inc(ld_small, 16)
            sp.dma_start(A_sb[:], A_log.rearrange("(h p) n -> p h n", p=P)).then_inc(ld_small, 16)
            sp.dma_start(wr_sb[:], w_router.rearrange("(k p) e -> p k e", p=P)).then_inc(ld_small, 16)
            for i, w in enumerate((Wq, Wk, Wv, Wo)):
                sp.dma_start(w_raw[:, i], w.rearrange("(c p) n -> p c n", p=P)).then_inc(ld_attn, 16)
            sp.dma_start(x_in[:], x[0].rearrange("(q p) d -> p q d", p=P)).then_inc(ld_x, 16)
            sp.dma_start(x_res[:], x[0].rearrange("(q p) d -> p q d", p=P)).then_inc(ld_res, 16)

            def load_expert(e):
                for i, w in enumerate((w_gate, w_up)):
                    sp.dma_start(
                        e_raw[:, i * FC * INTER:(i + 1) * FC * INTER].rearrange("p (k n) -> p k n", k=FC),
                        w[bass.ds(e, 1)].rearrange("o (k p) n -> p (o k) n", p=P),
                    ).then_inc(ld_expert, 16)
                sp.dma_start(
                    e_raw[:, 2 * FC * INTER:].rearrange("p (k n) -> p k n", k=IC),
                    w_down[bass.ds(e, 1)].rearrange("o (k p) n -> p (o k) n", p=P),
                ).then_inc(ld_expert, 16)


            for i, w in enumerate((w_gate, w_up, w_down)):
                if i == 2:
                    sp.wait_ge(elo_rdy, 1)
                sp.dma_start(raw_matrix(0, i), w[0].rearrange("(k p) n -> p k n", p=P)).then_inc(ld_expert, 16)

            def keep_x2(b):
                sp.wait_ge(x2_rdy, b + 1)
                sp.dma_start(x_sb[:, bass.ds(2 * b, QC), :], x1[:]).then_inc(x2_kept, 16)

            with sp.Fori(1, B) as b:
                sp.wait_ge(xT_ps, b)
                sp.dma_start(x_in[:], x[bass.ds(b, 1)].rearrange("o (q p) d -> p (o q) d", p=P)).then_inc(ld_x, 16)
                sp.wait_ge(res_rdy, b)
                sp.dma_start(x_res[:], x[bass.ds(b, 1)].rearrange("o (q p) d -> p (o q) d", p=P)).then_inc(ld_res, 16)
                keep_x2(b - 1)
            sp.wait_ge(attn_ps, B)
            load_expert(1)
            keep_x2(B - 1)
            with sp.Fori(2, NE) as e:
                sp.wait_ge(ehi_rdy, 3 * e)
                sp.wait_ge(elo_rdy, 3 * e)
                load_expert(e)
            for t in range(NT):
                sp.wait_ge(final_rdy, t + 1)
                sp.dma_start(
                    out.rearrange("b (q p) d -> p (b q) d", p=P)[:, t, :], x_sb[:, t, :]
                ).then_inc(stored, 16)
            sp.wait_ge(stored, 16 * NT)

        @block.gpsimd
        def _(pool):
            chain = Chain(pool, pool_chain)
            link = chain.link
            link(pool.memset(ident[:], 0.0))
            pool.affine_select(out=ident[:], in_=ident[:], compare_op=ALU.not_equal, fill=1.0, base=0,
                               pattern=[[-1, P]], channel_multiplier=1).then_inc(consts, 1)
            pool.wait_ge(consts, 1)
            pool.memset(xpad[:, :, :, 0:DC - 1], 0.0).then_inc(zeroed, 1)
            link(pool.tensor_copy(ident_b[:], ident[:]))
            for t in (mask_qk, mask_kq, negmax_p):
                link(pool.memset(t[:], 0.0))
            link(pool.memset(exponent[:], -0.5))
            link(pool.affine_select(out=mask_qk[:], in_=mask_qk[:], compare_op=ALU.is_ge, fill=MASKED, base=0,
                                    pattern=[[-1, P]], channel_multiplier=1))
            link(pool.affine_select(out=mask_kq[:], in_=mask_kq[:], compare_op=ALU.is_ge, fill=MASKED, base=0,
                                    pattern=[[1, P]], channel_multiplier=-1))
            pool.iota(iota8[:], pattern=[[1, NE]], base=0, channel_multiplier=0,
                      allow_small_or_imprecise_dtypes=True).then_inc(consts_b, 1)
            pool.wait_ge(consts_b, 1)
            def split_expert_lo(e, i, odd):
                pool.wait_ge(ehi_rdy, 3 * e + i + 1)
                hi, lo = (eg[odd][:, 0, i], eg[odd][:, 1, i]) if i < 2 else (ed[odd][:, :, 0, :], ed[odd][:, :, 1, :])
                pool.tensor_tensor(lo, raw_matrix(e, i), hi.bitcast(F32), ALU.subtract).then_inc(elo_rdy, 1)

            pool.wait_ge(wT_ps, 4)
            for q in range(QC):
                link(pool.memset(v_pad[q], 0.0))
                pool.memset(v_columns(q, ONES_AT), 1.0).then_inc(v_pad_rdy, 1)
            pool.wait_ge(v_pad_rdy, 2)
            for i in range(3):
                split_expert_lo(0, i, 0)

            pool.wait_ge(area_free, 1)
            pool.memset(dA[:, :, :, :, 0:1].rearrange("p a n h s -> p (a n h) s"), 0.0).then_inc(zeroed, 1)
            pool.wait_ge(zeroed, 2)
            pool.engine_nop().then_inc(y_added, 4)

            def add_states(b, m):
                pool.wait_ge(hC_rdy, b * NP + m + 2)
                for n in range(2):
                    if m == 0 and n == 0:
                        pool.wait_ge(gated_rdy, b + 1)
                        pool.tensor_tensor(y_sum[:], dBu[:, 0, 0], dBu[:, 0, 1], ALU.add).then_inc(y_added, 2)
                    elif m > 0:
                        pool.wait_ge(y_added, b * DS + 2 * m + n + 4)
                        pool.tensor_tensor(y_sum[:], y_sum[:], dBu[:, m % 2, n], ALU.add).then_inc(y_added, 1)

            def inverse_deviation(k):
                pool.wait_ge(var_rdy, k + 1)
                pool.tensor_tensor(rstd[:], rstd[:], exponent[:], ALU.pow).then_inc(rstd_rdy, 1)

            def divide_heads(b):
                pool.wait_ge(inverted, b + 1)
                pool.tensor_tensor(hT, pv_num, pv_den, ALU.mult).then_inc(hT_rdy, 1)

            def expert(e, odd, last=False):
                for th in range(TH):
                    for c in range(IC):
                        split_hidden_lo(e, th, c)
                        if not last and th == 1 and c < 3:
                            split_expert_lo(e + 1, c, 1 - odd)

            def split_hidden_lo(e, th, c):
                pool.wait_ge(hhi_rdy, (e * TH + th) * IC + c + 1)
                pool.tensor_tensor(h_lo[:, th, c, :], h_f[:, c % 2, :], h_hi[:, th, c, :].bitcast(F32),
                                   ALU.subtract).then_inc(hlo_rdy, 1)

            with pool.Fori(0, B - 1) as b:
                for m in range(NP):
                    add_states(b, m)
                divide_heads(b)
                inverse_deviation(2 * b)
                inverse_deviation(2 * b + 1)
            for m in range(NP):
                add_states(B - 1, m)
            divide_heads(B - 1)
            inverse_deviation(2 * B - 2)
            split_hidden_lo(0, 0, 0)
            split_hidden_lo(0, 0, 1)
            inverse_deviation(2 * B - 1)
            split_hidden_lo(0, 0, 2)
            split_hidden_lo(0, 0, 3)
            for c in range(IC):
                split_hidden_lo(0, 1, c)
                if c < 3:
                    split_expert_lo(1, c, 1)
            with pool.Fori(0, (NE - 2) // 2) as j:
                expert(2 * j + 1, 1)
                expert(2 * j + 2, 0)
            expert(NE - 1, 1, last=True)
            for t in range(NT // QC):
                inverse_deviation(2 * B + t)

        @block.scalar
        def _(act):
            act.wait_ge(rows_rdy, 1)
            act.copy(pick[:], rows32[:].rearrange("p (r o) -> p r o", o=1).broadcast_to([3 * BC, BC, P])).then_inc(
                pick_rdy, 1)
            act.wait_ge(ctxT_ps, 1)
            act.copy(ctxT, psS[:].rearrange("p a n -> p (a n)")).then_inc(ctxT_rdy, 1)
            for half in range(HALVES):
                for th in range(TH):
                    act.wait_ge(xin_ps, half * TH + th + 1)
                    act.copy(xpad[:, half, BH * th:BH * (th + 1), DC - 1:],
                             bank4(half * TH + th).rearrange("p (b s) -> p b s", b=BH)).then_inc(xpad_rdy, 1)
            for i in range(4):
                act.wait_ge(wT_ps, i + 1)
                act.copy(wT[:, i], psW[:, i, :].rearrange("p (k n) -> p k n", k=FC)).then_inc(wT_rdy, 1)

            def x_transposed(b):
                act.wait_ge(xT_ps, b + 1)
                act.copy(xT, psW[:, 0, :].rearrange("p (k n) -> p k n", k=FC)).then_inc(xT_rdy, 1)

            def qkv(b):
                act.wait_ge(q_ps, b + 1)
                act.activation(q_hi, psW[:, 1, :].rearrange("p (k n) -> p k n", k=FC), ACT.Copy,
                               scale=SCALE).then_inc(q_hi_rdy, 1)
                act.wait_ge(k_ps, b + 1)
                act.copy(k_hi, psW[:, 2, :].rearrange("p (k n) -> p k n", k=FC)).then_inc(k_hi_rdy, 1)
                act.wait_ge(v_ps, b + 1)
                for q in range(QC):
                    ins = act.copy(v_columns(q, V_AT),
                                   psW[:, 3, q * HID:(q + 1) * HID].rearrange("p (h d) -> p h d", d=HD))
                ins.then_inc(v_rdy, 1)

            def take_q4(b):
                for i in range(4):
                    act.wait_ge(q4_ps, 4 * b + i + 1)
                    act.copy(q4[:, 2 * i:2 * i + 2, :],
                             psW[:, i, :].rearrange("p (j n) -> p j n", j=2)).then_inc(q4_rdy, 1)

            def take_nmT(b):
                act.wait_ge(nmT_ps, b + 1)
                act.copy(nmT[:], psT_b[0:3 * BC, 0:S].rearrange("p (q n) -> p q n", q=QC)).then_inc(nmT_rdy, 1)

            def numerators(b):
                act.wait_ge(pv_ps, (b + 1) * PAIRS + 2)
                act.copy(pv_num[0:P // 2], psT[0:P // 2, 0, :].rearrange("p (k n) -> p k n", k=FC))
                act.copy(pv_den[0:P // 2], psT[P // 2:, 0, :].rearrange("p (k n) -> p k n", k=FC)).then_inc(num_act, 1)

            def half_tanh(b):
                act.wait_ge(x1_rdy, b + 1)
                act.activation(gated[:], x1[:], ACT.Tanh, scale=0.5).then_inc(tanh_rdy, 1)

            def take_x2T(b):
                act.wait_ge(x2T_ps, b + 1)
                act.copy(x2T_hi[:, :, bass.ds(b * S, S)],
                         psT[:, 1, :].rearrange("p (k n) -> p k n", k=FC)).then_inc(x2T_rdy, 1)

            x_transposed(0)
            for half in range(HALVES):
                act.wait_ge(conv_rdy, half + 1)
                act.activation(u_sb[:, :, half, :], conv[:, :, half, :], ACT.Silu).then_inc(u_rdy, 1)
            act.wait_ge(v_pad_rdy, 2)
            qkv(0)
            take_q4(0)
            for half in range(HALVES):
                for th in range(TH):
                    i = half * TH + th
                    act.wait_ge(relu_rdy, i + 1)
                    act.activation(du[:, BH * th:BH * (th + 1), half, :],
                                   psT[:, i % 2, :].rearrange("p (b s) -> p b s", b=BH), ACT.Abs,
                                   bias=vec_sb[:, 1, half:half + 1]).then_inc(act_chain, 1)
            act.wait_ge(act_chain, 4)
            act.activation(du[:], du[:], ACT.Exp, scale=-1.0).then_inc(exp_rdy, 1)
            act.wait_ge(exp_rdy, 1)
            act.activation(ln_part, du[:], ACT.Ln, bias=1.0).then_inc(ln_rdy, 1)
            act.wait_ge(ld_small, 16 * 6)
            act.activation(A_sb[:], A_sb[:], ACT.Exp).then_inc(act_chain, 1)
            act.wait_ge(act_chain, 5)
            act.mul(A_sb[:], A_sb[:], -1.0).then_inc(A_rdy, 1)

            def decay_buffer(b, m):
                act.wait_ge(scanned, b * NP + m + 1)

            def decay(b, m):
                for n in range(2):
                    for half in range(HALVES):
                        act.activation(dA[:, m % 2, n, half, 1:], delta[:, b, half, 1:], ACT.Exp,
                                       scale=A_sb[:, half, 2 * m + n:2 * m + n + 1]).then_inc(dA_rdy, 1)

            def split_expert_hi(e, i, odd):
                if isinstance(e, int) and e == 0:
                    act.wait_ge(ld_expert, 48 if i == 2 else 32)
                else:
                    act.wait_ge(ld_expert, 48 * (e + 1))
                hi = eg[odd][:, 0, i] if i < 2 else ed[odd][:, :, 0, :]
                act.copy(hi, raw_matrix(e, i)).then_inc(ehi_rdy, 1)

            for i in range(3):
                split_expert_hi(0, i, 0)
            take_nmT(0)
            act.wait_ge(A_rdy, 1)
            act.wait_ge(ssm_rdy, 1)
            act.wait_ge(area_free, 1)
            act.wait_ge(scanned, 2)
            decay(0, 0)
            decay(0, 1)

            def exponentials(b):
                for p in range(PAIRS):
                    if p < NP - 2:
                        decay_buffer(b, p + 2)
                    act.wait_ge(scoreT_ps, b * PAIRS + p + 1)
                    act.wait_ge(pv_ps, b * PAIRS + p + 1)
                    w0 = 2 * (p % 2)
                    act.activation(probT[:, p % 2], psW[:, w0:w0 + 2, 0:SCORE], ACT.Exp).then_inc(probT_rdy, 1)
                    if p < NP - 2:
                        decay(b, p + 2)

            with act.Fori(0, B - 1) as b:
                exponentials(b)
                numerators(b)
                decay_buffer(b + 1, 0)
                x_transposed(b + 1)
                decay(b + 1, 0)
                decay_buffer(b + 1, 1)
                qkv(b + 1)
                decay(b + 1, 1)
                take_q4(b + 1)
                half_tanh(b)
                take_x2T(b)
                take_nmT(b + 1)
            exponentials(B - 1)
            numerators(B - 1)

            def gate(e, th, c, first=False):
                k = (e * TH + th) * IC + c
                act.wait_ge(gu_ps, k + 1)
                if not (first and th == 0 and c < 2):
                    act.wait_ge(h_rdy, k - 1)
                act.activation(silu_g[:, c % 2], psW[:, c % 2, :], ACT.Silu, scale=GATE_MULT).then_inc(silu_rdy, 1)

            def split_hidden_hi(e, th, c, first=False):
                act.wait_ge(h_rdy, (e * TH + th) * IC + c + 1)
                if c == 0 and not first:
                    act.wait_ge(down_ps, (e - 1) * NT + (th + 1) * (NT // TH))
                act.copy(h_hi[:, th, c, :], h_f[:, c % 2, :]).then_inc(hhi_rdy, 1)

            def expert(e, odd, first=False, last=False, halves=range(TH)):
                for th in halves:
                    for c in range(IC + 1):
                        if c < IC:
                            gate(e, th, c, first)
                        if c > 0:
                            split_hidden_hi(e, th, c - 1, first)
                        if first and th == 1 and c == 1:
                            act.wait_ge(shifted, 1)
                            act.activation(probs[:], probs[:], ACT.Exp).then_inc(lexp_rdy, 1)
                        if th == 1 and 1 <= c <= 3 and not last:
                            if c == 1 and not first:
                                act.wait_ge(down_ps, e * NT)
                            split_expert_hi(e + 1, c - 1, 1 - odd)

            act.wait_ge(scanned, B * NP + 2)
            gate(0, 0, 0, True)
            half_tanh(B - 1)
            gate(0, 0, 1, True)
            split_hidden_hi(0, 0, 0, True)
            gate(0, 0, 2, True)
            split_hidden_hi(0, 0, 1, True)
            gate(0, 0, 3, True)
            split_hidden_hi(0, 0, 2, True)
            take_x2T(B - 1)
            split_hidden_hi(0, 0, 3, True)
            expert(0, 0, first=True, halves=(1,))
            with act.Fori(0, (NE - 2) // 2) as j:
                expert(2 * j + 1, 1)
                expert(2 * j + 2, 0)
            expert(NE - 1, 1, last=True)

        @block.vector
        def _(dve):
            chain = Chain(dve, dve_chain)
            link = chain.link
            dve.wait_ge(consts, 1)
            link(dve.tensor_tensor(rows32[:], ident[0:3 * BC, 0:BC], ident[0:3 * BC, BC:2 * BC], ALU.add))
            dve.tensor_tensor(rows32[:], rows32[:], ident[0:3 * BC, 2 * BC:3 * BC], ALU.add).then_inc(rows_rdy, 1)
            link(dve.tensor_scalar(pickQK.rearrange("p a h j n -> p (a h j) n"),
                                   ident[:].rearrange("p (o n) -> p o n", o=1).broadcast_to(
                                       [P, 4 * TILE_PAIRS, P]), 0.0, None, ALU.mult))
            for qk in range(2):
                for h in range(2):
                    rows = pickQK[:, qk, h].rearrange("p j (a k d) -> p (j a) k d", a=2, k=4)
                    blocks = slice(h, 4, 2) if qk else slice(2 * h, 2 * h + 2)
                    ins = dve.tensor_copy(rows[:, :, blocks, :], ident[:].rearrange(
                        "p (g o d) -> p g o d", o=1, d=HD).broadcast_to([P, 2 * TILE_PAIRS, 2, HD]))
            ins.then_inc(consts_b, 1)
            dve.wait_ge(ssmT_ps, 1)
            dve.tensor_copy(winT, psT[:, 0, 0:DI])
            xp_ps = psT[:, 0, DI:DI + HALVES * (DR + BC)].rearrange("p (h n) -> p h n", h=HALVES)
            for k in range(3):
                dve.tensor_copy(xpT[:, :, BC * k:BC * (k + 1)], xp_ps[:, :, DR:])
            dve.tensor_copy(xpT[:, :, 3 * BC:], xp_ps[:, :, 0:DR])
            dve.tensor_copy(dtwT[0:DR], psT[0:DR, 1, 0:DI]).then_inc(ssmT_rdy, 1)
            dve.wait_ge(ld_small, 16 * 6)
            dve.wait_ge(zeroed, 1)
            for half in range(HALVES):
                dve.wait_ge(xpad_rdy, TH * (half + 1))
                acc = conv[:, :, half, :]
                link(dve.tensor_scalar(acc, xpad[:, half, :, 0:S], convw_sb[:, half, 0:1], vec_sb[:, 0, half:half + 1],
                                       ALU.mult, ALU.add))
                for k in range(1, DC):
                    ins = dve.scalar_tensor_tensor(out=acc, in0=xpad[:, half, :, k:k + S],
                                                   scalar=convw_sb[:, half, k:k + 1], in1=acc,
                                                   op0=ALU.mult, op1=ALU.add)
                    if k < DC - 1:
                        link(ins)
                    else:
                        ins.then_inc(conv_rdy, 1)

            def split_qk(b):
                dve.wait_ge(q_hi_rdy, b + 1)
                dve.scalar_tensor_tensor(out=q_lo, in0=psW[:, 1, :].rearrange("p (k n) -> p k n", k=FC), scalar=SCALE,
                                         in1=q_hi.bitcast(F32), op0=ALU.mult, op1=ALU.subtract).then_inc(q_lo_rdy, 1)
                dve.wait_ge(k_hi_rdy, b + 1)
                dve.tensor_tensor(k_lo, psW[:, 2, :].rearrange("p (k n) -> p k n", k=FC), k_hi.bitcast(F32),
                                  ALU.subtract).then_inc(k_lo_rdy, 1)

            def take_k4(b):
                for i in range(4):
                    dve.wait_ge(k4_ps, 4 * b + i + 1)
                    dve.tensor_copy(k4[:, 2 * i:2 * i + 2, :],
                                    psW[:, i, :].rearrange("p (j n) -> p j n", j=2)).then_inc(k4_rdy, 1)

            def maxima(b, p):
                dve.wait_ge(score_ps, b * PAIRS + p + 1)
                w0 = 2 * (p % 2)
                dve.tensor_reduce(negmax[:, 0, 2 * p:2 * p + 2], psW[:, w0:w0 + 2, 0:P], AX_X, ALU.max, negate=True)
                dve.tensor_reduce(negmax[:, 1, 2 * p:2 * p + 2], psW[:, w0:w0 + 2, P:SCORE], AX_X, ALU.max,
                                  negate=True).then_inc(max_rdy, 1)

            def split_maxima(b):
                dve.wait_ge(max_rdy, (b + 1) * PAIRS)
                link(dve.tensor_copy(negmax_p[:, :, 0:HEADS], negmax[:]))
                link(dve.tensor_tensor(negmax_r[:], negmax[:], negmax_p[:, :, 0:HEADS], ALU.subtract))
                link(dve.tensor_copy(negmax_p[:, :, BC:BC + HEADS], negmax_r[:]))
                dve.tensor_tensor(negmax_p[:, :, 2 * BC:2 * BC + HEADS], negmax_r[:], negmax_p[:, :, BC:BC + HEADS],
                                  ALU.subtract).then_inc(nm_rdy, 1)

            split_qk(0)
            for th in range(TH):
                dve.wait_ge(xdbl_ps, th + 1)
                dve.tensor_copy(dt_lo[0:DR, th * BANK:(th + 1) * BANK],
                                psS[3 * BC:3 * BC + DR, th, :]).then_inc(dt_rdy, 1)
            take_k4(0)
            for half in range(HALVES):
                for th in range(TH):
                    i = half * TH + th
                    dve.wait_ge(delta_ps, i + 1)
                    dve.tensor_scalar(delta[:, BH * th:BH * (th + 1), half, :],
                                      psT[:, i % 2, :].rearrange("p (b s) -> p b s", b=BH),
                                      vec_sb[:, 1, half:half + 1], 0.0, ALU.add, ALU.max).then_inc(relu_rdy, 1)
            for th in range(TH):
                cols = slice(th * BANK, (th + 1) * BANK)
                bank = psS[0:3 * BC, th, :]
                rest = bc_r[0:3 * BC, cols]
                link(dve.tensor_copy(bc_parts[:, cols], bank))
                link(dve.tensor_tensor(rest, bank, bc_parts[:, cols], ALU.subtract))
                for k in (1, 2):
                    rows = slice(BC * k, BC * (k + 1))
                    link(dve.tensor_copy(bc_parts[rows, cols], rest[rows]))
                link(dve.tensor_tensor(bc_parts[rows, cols], rest[rows], bc_parts[rows, cols], ALU.subtract))
            for p in range(4):
                maxima(0, p)
            dve.wait_ge(exp_rdy, 1)
            link(dve.tensor_scalar(log_rest, du[:], 1.0, -1.0, ALU.add, ALU.add))
            link(dve.tensor_tensor(log_rest, du[:], log_rest, ALU.subtract))
            dve.wait_ge(ln_rdy, 1)
            link(dve.tensor_tensor(log_rest, log_rest, ln_part, ALU.add))
            link(dve.tensor_tensor(delta[:], delta[:], log_rest, ALU.add))
            link(dve.tensor_tensor(du[:], delta[:], u_sb[:], ALU.mult))
            dve.engine_nop().then_inc(area_free, 1)
            dve.engine_nop().then_inc(ssm_rdy, 1)
            for p in range(4, PAIRS):
                maxima(0, p)
            split_maxima(0)
            for half in range(HALVES):
                link(dve.tensor_scalar(u_sb[:, :, half, :], u_sb[:, :, half, :], vec_sb[:, 2, half:half + 1],
                                       None, ALU.mult))
            dve.engine_nop().then_inc(scanned, 2)
            dve.engine_nop().then_inc(b_used, 1)
            dve.engine_nop().then_inc(hC_rdy, 1)
            dve.engine_nop().then_inc(gated_rdy, 1)
            dve.engine_nop().then_inc(x2_kept, 16)
            link(dve.tensor_copy(wr_split[:, :, 0, :], wr_sb[:]))
            link(dve.tensor_tensor(wr_split[:, :, 1, :], wr_sb[:], wr_split[:, :, 0, :].bitcast(F32), ALU.subtract))

            def ssm_pair(b, m):
                g = b * NP + m
                x_in = dBu[:, m % 2]
                dve.wait_ge(bc_ps, 2 * g + 1)
                dve.wait_ge(y_added, 2 * g + 2)
                dve.tensor_tensor(
                    x_in, du[:, bass.ds(b, 1)].broadcast_to([P, 2, HALVES, S]),
                    psS[:, 0, :].rearrange("p (n o s) -> p n o s", n=2, o=1).broadcast_to([P, 2, HALVES, S]),
                    ALU.mult).then_inc(b_used, 1)
                dve.wait_ge(b_used, g + 2)
                dve.wait_ge(dA_rdy, 4 * g + 4)
                if m == 0:
                    dve.wait_ge(zeroed, 2)
                dve.tensor_tensor_scan(
                    state.rearrange("p n h s -> p (n h s)"), dA[:, m % 2].rearrange("p n h s -> p (n h s)"),
                    x_in.rearrange("p n h s -> p (n h s)"), 0.0, ALU.mult, ALU.add).then_inc(scanned, 1)
                dve.wait_ge(scanned, g + 3)
                dve.wait_ge(bc_ps, 2 * g + 2)
                dve.tensor_tensor(
                    x_in, state,
                    psS[:, 1, :].rearrange("p (n o s) -> p n o s", n=2, o=1).broadcast_to([P, 2, HALVES, S]),
                    ALU.mult).then_inc(hC_rdy, 1)

            def norm_stats(src):
                for q in range(QC):
                    dve.bn_stats(stats[:, q], src(q))
                dve.drain()
                for q in range(QC):
                    ins = dve.bn_aggr(mv[:, q], stats[:, q])
                link(ins)
                dve.tensor_scalar(rstd[:], mv[:, :, 1], LN_EPS, None, ALU.add).then_inc(var_rdy, 1)

            def norm_apply(k, src):
                dve.wait_ge(rstd_rdy, k + 1)
                for q in range(QC):
                    ins = dve.tensor_scalar(src(q), src(q), mv[:, q, 0:1], rstd[:, q:q + 1], ALU.subtract, ALU.mult)
                return ins

            def x1_tile(q):
                return x1[:, q]

            def numerators(b):
                dve.wait_ge(pv_ps, (b + 1) * PAIRS + 2)
                dve.tensor_copy(pv_num[P // 2:], psT[0:P // 2, 1, :].rearrange("p (k n) -> p k n", k=FC))
                dve.tensor_copy(pv_den[P // 2:],
                                psT[P // 2:, 1, :].rearrange("p (k n) -> p k n", k=FC)).then_inc(num_dve, 1)

            def invert_sums(b):
                dve.wait_ge(num_act, b + 1)
                dve.wait_ge(num_dve, b + 1)
                dve.reciprocal(pv_den, pv_den).then_inc(inverted, 1)

            def residual(b):
                dve.wait_ge(attn_ps, b + 1)
                dve.wait_ge(ld_res, 16 * b + 16)
                dve.wait_ge(x2_kept, 16 * b + 16)
                dve.tensor_tensor(x1[:], psT[:, 1, :].rearrange("p (q n) -> p q n", q=QC), x_res[:],
                                  ALU.add).then_inc(res_rdy, 1)
                dve.wait_ge(res_rdy, b + 1)
                norm_stats(x1_tile)

            def gating(b):
                dve.wait_ge(x1_rdy, b + 1)
                dve.wait_ge(tanh_rdy, b + 1)
                link(dve.scalar_tensor_tensor(out=gated[:], in0=gated[:], scalar=1.0, in1=x1[:], op0=ALU.add,
                                              op1=ALU.mult))
                dve.wait_ge(y_added, (b + 1) * DS + 4)
                link(dve.tensor_tensor(y_sum[:], u_sb[:, bass.ds(b, 1)].rearrange("p o h s -> p (o h) s"), y_sum[:],
                                       ALU.add))
                dve.scalar_tensor_tensor(out=gated[:], in0=y_sum[:], scalar=0.5, in1=gated[:], op0=ALU.mult,
                                         op1=ALU.mult).then_inc(gated_rdy, 1)

            def add_gated(b):
                dve.wait_ge(gatedT_ps, b + 1)
                link(dve.tensor_tensor(x1[:], psT[:, 0, :].rearrange("p (q n) -> p q n", q=QC), x1[:], ALU.add))
                norm_stats(x1_tile)

            def x2T_low(b):
                dve.wait_ge(x2T_rdy, b + 1)
                dve.tensor_tensor(x2T_lo[:, :, bass.ds(b * S, S)], psT[:, 1, :].rearrange("p (k n) -> p k n", k=FC),
                                  x2T_hi[:, :, bass.ds(b * S, S)].bitcast(F32), ALU.subtract).then_inc(x2lo_rdy, 1)

            ssm_pair(0, 0)
            prep_links = chain.n
            with dve.Fori(0, B - 1) as b:
                chain.at(b * DVE_LINKS + prep_links)
                for m in range(1, NP):
                    ssm_pair(b, m)
                numerators(b)
                invert_sums(b)
                split_qk(b + 1)
                residual(b)
                take_k4(b + 1)
                norm_apply(2 * b, x1_tile).then_inc(x1_rdy, 1)
                maxima(b + 1, 0)
                maxima(b + 1, 1)
                gating(b)
                maxima(b + 1, 2)
                maxima(b + 1, 3)
                add_gated(b)
                maxima(b + 1, 4)
                norm_apply(2 * b + 1, x1_tile).then_inc(x2_rdy, 1)
                maxima(b + 1, 5)
                maxima(b + 1, 6)
                x2T_low(b)
                maxima(b + 1, 7)
                split_maxima(b + 1)
                ssm_pair(b + 1, 0)
                assert chain.n == DVE_LINKS, chain.n
            chain.at((B - 1) * DVE_LINKS + prep_links)
            for m in range(1, NP):
                ssm_pair(B - 1, m)
            numerators(B - 1)
            invert_sums(B - 1)

            def router():
                dve.wait_ge(logit_ps, 1)
                dve.tensor_copy(logits[:], psT[:, 0, 0:2 * NT * NE].rearrange("p (t l e) -> p l t e", l=2, e=NE)
                                ).then_inc(logit_taken, 1)
                dve.wait_ge(logit_taken, 1)
                link(dve.tensor_tensor(probs[:], logits[:, 0], logits[:, 1], ALU.add))
                link(dve.tensor_reduce(small[:, 0, :], probs[:], AX_X, ALU.max))
                dve.tensor_tensor(probs[:], probs[:], per_expert(small[:, 0, :]), ALU.subtract).then_inc(shifted, 1)

            def per_expert(view):
                return view.rearrange("p (t o) -> p t o", o=1).broadcast_to([P, NT, NE])

            def choose():
                dve.wait_ge(lexp_rdy, 1)
                link(dve.tensor_reduce(small[:, 1, :], probs[:], AX_X, ALU.add))
                link(dve.reciprocal(small[:, 2, :], small[:, 1, :]))
                link(dve.scalar_tensor_tensor(out=probs[:], in0=probs[:], scalar=DOWN_MULT,
                                              in1=per_expert(small[:, 2, :]), op0=ALU.mult, op1=ALU.mult))
                for t in range(NT):
                    dve.max(top_val[:, t], probs[:, t])
                dve.drain()
                for t in range(NT):
                    dve.max_index(top_idx[:, t], top_val[:, t], probs[:, t])
                dve.drain()
                link(dve.tensor_copy(top_idx_f[:], top_idx[:]))
                for i in range(2):
                    link(dve.tensor_tensor(picked[:, i], iota8[:].rearrange("p (o e) -> p o e", o=1).broadcast_to(
                        [P, NT, NE]), top_idx_f[:, :, i:i + 1].broadcast_to([P, NT, NE]), ALU.is_equal))
                for i in range(2):
                    link(dve.tensor_tensor(picked[:, i], picked[:, i], top_val[:, :, i:i + 1].broadcast_to([P, NT, NE]),
                                           ALU.mult))
                link(dve.tensor_tensor(w_tok[:], picked[:, 0], picked[:, 1], ALU.add))

            def hidden(e, th, c):
                k = (e * TH + th) * IC + c
                dve.wait_ge(silu_rdy, k + 1)
                if not (isinstance(e, int) and e == 0 and th == 0 and c < 2):
                    dve.wait_ge(hlo_rdy, k - 1)
                dve.tensor_tensor(h_f[:, c % 2], silu_g[:, c % 2], psW[:, 2 + c % 2, :], ALU.mult).then_inc(h_rdy, 1)

            def accumulate(e, th, i, e_of):
                t = th * (NT // TH) + i
                dve.wait_ge(down_ps, e * NT + t + 1)
                bank = bank4(i)
                wt = w_tok[:, t, e_of] if isinstance(e, int) else w_tok[:, t, bass.ds(e, 1)]
                dve.scalar_tensor_tensor(out=x_sb[:, t], in0=bank[:, 0:HID], scalar=wt, in1=x_sb[:, t], op0=ALU.mult,
                                         op1=ALU.add).then_inc(summed, 1)
                dve.wait_ge(summed, 2 * (e * NT + t) + 1)
                dve.scalar_tensor_tensor(out=x_sb[:, t], in0=bank[:, HID:], scalar=wt, in1=x_sb[:, t], op0=ALU.mult,
                                         op1=ALU.add).then_inc(summed, 1)

            def expert(e):
                e_of = slice(e, e + 1) if isinstance(e, int) else None
                e_before = slice(e - 1, e) if isinstance(e, int) else None
                for c in range(IC):
                    hidden(e, 0, c)
                for i in range(4):
                    accumulate(e - 1, 1, i, e_before)
                for c in range(IC):
                    hidden(e, 1, c)
                for i in range(4):
                    accumulate(e, 0, i, e_of)

            residual(B - 1)
            hidden(0, 0, 0)
            norm_apply(2 * B - 2, x1_tile).then_inc(x1_rdy, 1)
            gating(B - 1)
            hidden(0, 0, 1)
            hidden(0, 0, 2)
            add_gated(B - 1)
            norm_apply(2 * B - 1, x1_tile).then_inc(x2_rdy, 1)
            hidden(0, 0, 3)
            x2T_low(B - 1)
            hidden(0, 1, 0)
            router()
            hidden(0, 1, 1)
            choose()
            hidden(0, 1, 2)
            hidden(0, 1, 3)
            dve.wait_ge(x2_kept, 16 * (B + 1))
            for i in range(4):
                accumulate(0, 0, i, slice(0, 1))
            with dve.Fori(0, (NE - 2) // 2) as j:
                expert(2 * j + 1)
                expert(2 * j + 2)
            expert(NE - 1)
            for i in range(4):
                accumulate(NE - 1, 1, i, slice(NE - 1, NE))
            dve.wait_ge(summed, 2 * NE * NT)
            for t in range(NT // QC):
                norm_stats(lambda q: x_sb[:, 2 * t + q])
                norm_apply(2 * B + t, lambda q: x_sb[:, 2 * t + q]).then_inc(final_rdy, 2)

        @block.tensor
        def _(pe):
            def transposes(bank_of, src_of, n, m, ident_of, done):
                for i in range(n):
                    for j in range(m):
                        ins = pe.transpose(bank_of(i, j), src_of(i, j), ident_of)
                ins.then_inc(done, 1)

            pe.wait_ge(consts, 1)
            pe.wait_ge(ld_ctx, 16)
            transposes(lambda i, j: psS[:, i, j * P:(j + 1) * P], lambda i, j: c_ctx[:, 4 * i + j, :], 2, 4, ident[:],
                       ctxT_ps)
            pe.wait_ge(ld_ssm, 48)
            for h in range(HALVES):
                pe.transpose(psT[:, 0, h * P:(h + 1) * P], win_raw[:, h, :], ident[:])
                n = DR + BC
                pe.transpose(psT[:, 0, DI + h * n:DI + (h + 1) * n], xp_raw[0:n, h * P:(h + 1) * P], ident[0:n, 0:n])
                ins = pe.transpose(psT[0:DR, 1, h * P:(h + 1) * P], dtw_raw[:, h, :], ident[:])
            ins.then_inc(ssmT_ps, 1)
            pe.wait_ge(ctxT_rdy, 1)
            pe.wait_ge(ssmT_rdy, 1)
            for half in range(HALVES):
                for th in range(TH):
                    pe.matmul(bank4(half * TH + th), winT[:, half * P:(half + 1) * P],
                              ctxT[:, th * BANK:(th + 1) * BANK], start=True, stop=True).then_inc(xin_ps, 1)
            pe.wait_ge(ld_attn, 64)
            for i in range(4):
                bank = psW[:, i, :]
                transposes(lambda k, c: bank[:, k * HID + c * P:k * HID + (c + 1) * P],
                           lambda k, c: w_raw[:, i, c, k * P:(k + 1) * P], FC, FC, ident[:], wT_ps)

            def transpose_x(b):
                pe.wait_ge(ld_x, 16 * b + 16)
                for q in range(QC):
                    for k in range(FC):
                        ins = pe.transpose(psW[:, 0, k * S + q * P:k * S + (q + 1) * P],
                                           x_in[:, q, k * P:(k + 1) * P], ident[:])
                ins.then_inc(xT_ps, 1)

            def project_qk(b):
                pe.wait_ge(xT_rdy, b + 1)
                for i, done in ((0, q_ps), (1, k_ps)):
                    for c in range(FC):
                        for k in range(FC):
                            ins = pe.matmul(psW[:, 1 + i, c * S:(c + 1) * S], wT[:, i, k, c * P:(c + 1) * P], xT[:, k, :],
                                            start=(k == 0), stop=(k == FC - 1))
                    ins.then_inc(done, 1)

            def project_v():
                for q in range(QC):
                    for k in range(FC):
                        ins = pe.matmul(psW[:, 3, q * HID:(q + 1) * HID], xT[:, k, q * P:(q + 1) * P], wT[:, 2, k, :],
                                        start=(k == 0), stop=(k == FC - 1))
                ins.then_inc(v_ps, 1)

            def stack_q(b):
                pe.wait_ge(q_hi_rdy, b + 1)
                pe.wait_ge(q_lo_rdy, b + 1)
                for i in range(4):
                    if i == 2:
                        pe.wait_ge(k_lo_rdy, b + 1)
                    elif i == 3:
                        pe.wait_ge(v_rdy, b + 1)
                    stack(0, i, q_hi, q_lo, q4_ps)

            def stack_k(b):
                pe.wait_ge(k_lo_rdy, b + 1)
                for i in range(4):
                    pe.wait_ge(q4_rdy, 4 * b + i + 1)
                    stack(1, i, k_hi, k_lo, k4_ps)

            def stack(qk, i, hi, lo, done):
                for j in range(2):
                    t, jj = (2 * i + j) // TILE_PAIRS, (2 * i + j) % TILE_PAIRS
                    pe.matmul(psW[:, i, j * S:(j + 1) * S], pickQK[:, qk, 0, jj, :], hi[:, t, :], start=True,
                              stop=False)
                    ins = pe.matmul(psW[:, i, j * S:(j + 1) * S], pickQK[:, qk, 1, jj, :], lo[:, t, :],
                                    start=False, stop=True)
                ins.then_inc(done, 1)

            def scores(b, p):
                if p == 0:
                    pe.wait_ge(q4_rdy, 4 * b + 4)
                    pe.wait_ge(k4_rdy, 4 * b + 4)
                elif p >= 2:
                    pe.wait_ge(max_rdy, b * PAIRS + p - 1)
                for a in range(2):
                    bank = psW[:, 2 * (p % 2) + a, :]
                    rows = slice(64 * a, 64 * a + 64)
                    pe.matmul(bank[:, 0:P], q4[rows, p, 0:P], k4[rows, p, 0:P], start=True, stop=False)
                    pe.matmul(bank[:, 0:P], ident_b[:], mask_qk[:], start=False, stop=True)
                    pe.matmul(bank[:, P:SCORE], q4[rows, p, P:S], k4[rows, p, :], start=True, stop=True)
                    ins = pe.matmul(bank[:, S:SCORE], ident_b[:], mask_qk[:], start=False, stop=True,
                                    skip_group_check=True)
                ins.then_inc(score_ps, 1)

            def transpose_maxima(b):
                pe.wait_ge(nm_rdy, b + 1)
                for q in range(QC):
                    ins = pe.transpose(psT_b[0:3 * BC, q * P:(q + 1) * P], negmax_p[:, q, :], ident_b[:])
                ins.then_inc(nmT_ps, 1)

            pe.wait_ge(wT_rdy, 4)
            transpose_x(0)
            project_qk(0)
            project_v()
            pe.wait_ge(u_rdy, 2)
            for th in range(TH):
                for half in range(HALVES):
                    ins = pe.matmul(psS[0:3 * BC + DR, th, :], xpT[:, half, :],
                                    u_sb[:, BH * th:BH * (th + 1), half, :], start=(half == 0),
                                    stop=(half == HALVES - 1))
                ins.then_inc(xdbl_ps, 1)
            pe.wait_ge(consts_b, 2)
            stack_q(0)
            pe.wait_ge(dt_rdy, 2)
            for half in range(HALVES):
                for th in range(TH):
                    i = half * TH + th
                    if i == 2:
                        stack_k(0)
                    if i >= 2:
                        pe.wait_ge(relu_rdy, i - 1)
                        pe.wait_ge(act_chain, i - 1)
                    pe.matmul(psT[:, i % 2, :], dtwT[0:DR, half * P:(half + 1) * P],
                              dt_lo[0:DR, th * BANK:(th + 1) * BANK], start=True, stop=True).then_inc(delta_ps, 1)
            for p in range(PAIRS):
                scores(0, p)

            def broadcast_b(b, m):
                pe.wait_ge(b_used, b * NP + m + 1)
                broadcast(b, 0, 2 * m)

            def broadcast_c(b, m):
                pe.wait_ge(hC_rdy, b * NP + m + 1)
                broadcast(b, 1, DS + 2 * m)

            def broadcast(b, bank, row):
                for n in range(2):
                    ins = pe.matmul(psS[:, bank, n * S:(n + 1) * S], pick[:, row + n, :], bc_parts[:, bass.ds(b * S, S)],
                                    start=True, stop=True)
                ins.then_inc(bc_ps, 1)

            def shifted_scores(b, p):
                if p == 0:
                    pe.wait_ge(nmT_rdy, b + 1)
                elif p >= 2:
                    pe.wait_ge(probT_rdy, b * PAIRS + p - 1)
                for a in range(2):
                    bank = psW[:, 2 * (p % 2) + a, :]
                    rows = slice(64 * a, 64 * a + 64)
                    h = 2 * p + a
                    pe.matmul(bank[:, 0:S], k4[rows, p, 0:P], q4[rows, p, :], start=True, stop=False)
                    pe.matmul(bank[:, 0:S], pick[:, h, :], nmT[:].rearrange("p q n -> p (q n)"), start=False,
                              stop=True)
                    pe.matmul(bank[:, 0:P], ident_b[:], mask_kq[:], start=False, stop=True, skip_group_check=True)
                    pe.matmul(bank[:, S:SCORE], k4[rows, p, P:S], q4[rows, p, P:S], start=True, stop=False,
                              skip_group_check=True)
                    pe.matmul(bank[:, S:SCORE], pick[:, h, :], nmT[:, 1, :], start=False, stop=False,
                              skip_group_check=True)
                    ins = pe.matmul(bank[:, S:SCORE], ident_b[:], mask_kq[:], start=False, stop=True,
                                    skip_group_check=True)
                ins.then_inc(scoreT_ps, 1)

            def pv(b, p):
                pe.wait_ge(probT_rdy, b * PAIRS + p + 1)
                for a in range(2):
                    group, j = divmod(2 * p + a, 4)
                    at = (group // 2) * S
                    start = (2 * p + a) * P + V_AT - HD * j
                    pr = probT[:, p % 2, a]
                    pe.matmul(psT[:, group % 2, at:at + S], v_pad[0][:, start:start + P], pr[:, 0:S], start=(j == 0),
                              stop=(j == 3))
                    ins = pe.matmul(psT[:, group % 2, at + P:at + S], v_pad[1][:, start:start + P],
                                    pr[:, S:SCORE], start=False, stop=(j == 3), skip_group_check=True)
                ins.then_inc(pv_ps, 1)

            def attention(b):
                for p in range(PAIRS):
                    if p + 1 < NP:
                        broadcast_b(b, p + 1)
                    shifted_scores(b, p)
                    if p + 1 < NP:
                        broadcast_c(b, p + 1)
                    if p > 0:
                        pv(b, p - 1)
                pv(b, PAIRS - 1)

            def project_out(b):
                pe.wait_ge(hT_rdy, b + 1)
                for q in range(QC):
                    for k in range(FC):
                        ins = pe.matmul(psT[:, 1, q * HID:(q + 1) * HID], hT[:, k, q * P:(q + 1) * P], wT[:, 3, k, :],
                                        start=(k == 0), stop=(k == FC - 1))
                ins.then_inc(attn_ps, 1)

            def transpose_gated(b):
                pe.wait_ge(gated_rdy, b + 2)
                for q in range(QC):
                    for k in range(HALVES):
                        ins = pe.transpose(psT[:, 0, q * HID + k * P:q * HID + (k + 1) * P],
                                           gated[:, k, q * P:(q + 1) * P], ident[:])
                ins.then_inc(gatedT_ps, 1)

            def transpose_x2(b):
                pe.wait_ge(x2_rdy, b + 1)
                for q in range(QC):
                    for k in range(FC):
                        ins = pe.transpose(psT[:, 1, k * S + q * P:k * S + (q + 1) * P],
                                           x1[:, q, k * P:(k + 1) * P], ident[:])
                ins.then_inc(x2T_ps, 1)

            pe.wait_ge(relu_rdy, 4)
            pe.wait_ge(act_chain, 4)
            pe.wait_ge(pick_rdy, 1)
            pe.wait_ge(ssm_rdy, 1)
            transpose_maxima(0)
            pe.nop().then_inc(pv_ps, 2)
            broadcast_b(0, 0)
            broadcast_c(0, 0)
            pe.wait_ge(area_free, 1)
            with pe.Fori(0, B - 1) as b:
                attention(b)
                pe.wait_ge(probT_rdy, (b + 1) * PAIRS)
                transpose_x(b + 1)
                project_qk(b + 1)
                project_v()
                project_out(b)
                stack_q(b + 1)
                stack_k(b + 1)
                for p in range(PAIRS):
                    scores(b + 1, p)
                    if p == 3:
                        transpose_gated(b)
                    elif p == 6:
                        transpose_x2(b)
                broadcast_b(b + 1, 0)
                broadcast_c(b + 1, 0)
                pe.wait_ge(x2lo_rdy, b + 1)
                transpose_maxima(b + 1)
            attention(B - 1)

            def gate_up(e, odd, th, c):
                k = (e * TH + th) * IC + c
                if not (isinstance(e, int) and e == 0 and th == 0 and c < 2):
                    pe.wait_ge(h_rdy, k - 1)
                for mat in range(2):
                    bank = psW[:, 2 * mat + c % 2, :]
                    n = 0
                    for part, xT_part in ((0, x2T_hi), (0, x2T_lo), (1, x2T_hi)):
                        for kk in range(FC):
                            ins = pe.matmul(bank, eg[odd][:, part, mat, kk, c * P:(c + 1) * P],
                                            xT_part[:, kk, th * BANK:(th + 1) * BANK], start=(n == 0), stop=(n == 5))
                            n += 1
                ins.then_inc(gu_ps, 1)

            def down(e, odd, th, i):
                t = th * (NT // TH) + i
                if not (isinstance(e, int) and e == 0 and th == 0):
                    pe.wait_ge(summed, 2 * (e * NT + t - 3))
                bank = bank4(i)
                cols = slice(i * P, (i + 1) * P)
                for c in range(IC):
                    pe.matmul(bank, h_hi[:, th, c, cols], ed[odd][:, c].rearrange("p l n -> p (l n)"), start=(c == 0),
                              stop=(c == IC - 1))
                for c in range(IC):
                    ins = pe.matmul(bank[:, 0:HID], h_lo[:, th, c, cols], ed[odd][:, c, 0, :], start=False,
                                    stop=(c == IC - 1), skip_group_check=True)
                ins.then_inc(down_ps, 1)

            def route():
                for t in range(NT):
                    cols = slice(t * P, (t + 1) * P)
                    at = 2 * NE * t
                    for k in range(FC):
                        pe.matmul(psT[:, 0, at:at + 2 * NE], x2T_hi[:, k, cols],
                                  wr_split[:, k].rearrange("p l e -> p (l e)"), start=(k == 0), stop=(k == FC - 1))
                    for k in range(FC):
                        ins = pe.matmul(psT[:, 0, at:at + NE], x2T_lo[:, k, cols], wr_split[:, k, 0, :], start=False,
                                        stop=(k == FC - 1), skip_group_check=True)
                ins.then_inc(logit_ps, 1)

            def expert(e, odd):
                pe.wait_ge(elo_rdy, 3 * e + 3)
                for c in range(IC):
                    gate_up(e, odd, 0, c)
                pe.wait_ge(hlo_rdy, e * TH * IC)
                for i in range(4):
                    down(e - 1, 1 - odd, 1, i)
                for c in range(IC):
                    gate_up(e, odd, 1, c)
                pe.wait_ge(hlo_rdy, (e * TH + 1) * IC)
                for i in range(4):
                    down(e, odd, 0, i)

            pe.wait_ge(elo_rdy, 3)
            pe.wait_ge(x2lo_rdy, B // TH)
            pe.wait_ge(probT_rdy, B * PAIRS)
            gate_up(0, 0, 0, 0)
            project_out(B - 1)
            gate_up(0, 0, 0, 1)
            gate_up(0, 0, 0, 2)
            transpose_gated(B - 1)
            gate_up(0, 0, 0, 3)
            transpose_x2(B - 1)
            pe.wait_ge(x2lo_rdy, B)
            gate_up(0, 0, 1, 0)
            route()
            for c in range(1, IC):
                gate_up(0, 0, 1, c)
            pe.wait_ge(hlo_rdy, IC)
            pe.wait_ge(logit_taken, 1)
            for i in range(4):
                down(0, 0, 0, i)
            with pe.Fori(0, (NE - 2) // 2) as j:
                expert(2 * j + 1, 1)
                expert(2 * j + 2, 0)
            expert(NE - 1, 1)
            pe.wait_ge(hlo_rdy, NE * TH * IC)
            for i in range(4):
                down(NE - 1, 1, 1, i)


_INS = ['x', 'ctx_1024', 'L0_attn_Wq', 'L0_attn_Wk', 'L0_attn_Wv', 'L0_attn_Wo', 'L0_xattn_in_proj_w',
        'L0_xattn_conv_w', 'L0_xattn_conv_b', 'L0_xattn_x_proj_w', 'L0_xattn_dt_proj_w', 'L0_xattn_dt_proj_b',
        'L0_xattn_A_log', 'L0_xattn_D', 'L0_ffn_w_router', 'L0_ffn_w_gate', 'L0_ffn_w_up', 'L0_ffn_w_down']
_OUTS = [((4, 256, 256), 'float32')]


def kernel(**inputs):
    import numpy as _np
    import concourse.bacc as _bacc
    from concourse import mybir as _mybir
    from concourse.bass_utils import run_bass_kernel_spmd as _run

    nc = _bacc.Bacc("TRN2", target_bir_lowering=False, num_devices=1)
    arrays, args = {}, []
    for name in _INS:
        a = _np.ascontiguousarray(inputs[name])
        arrays[f"in_{name}_dram"] = a
        args.append(nc.dram_tensor(f"in_{name}_dram", a.shape, _mybir.dt.from_np(a.dtype), kind="ExternalInput").ap())
    for i, (shape, dtype) in enumerate(_OUTS):
        dt = _mybir.dt.from_np(_np.dtype(dtype))
        args.append(nc.dram_tensor(f"out_{i}_dram", shape, dt, kind="ExternalOutput").ap())
    decoder_layer(nc, *args)
    r = _run(nc, [arrays], core_ids=[0])
    got = tuple(r.results[0][f"out_{i}_dram"] for i in range(len(_OUTS)))
    return got[0]
```

```python
from contextlib import ExitStack

import concourse.bass as bass
from concourse import mybir

F32 = mybir.dt.float32
F32R = mybir.dt.float32r
BF16 = mybir.dt.bfloat16
U32 = mybir.dt.uint32
ALU = mybir.AluOpType
ACT = mybir.ActivationFunctionType
AX_X = mybir.AxisListType.X

P = 128
LN_EPS = 1e-5
MASKED = -1e38
GATE_MULT = 0.5
DOWN_MULT = 0.25
BANK = 512

DVE_LINKS = 6


class Chain:

    def __init__(self, engine, semaphore):
        self.engine, self.semaphore, self.base, self.n = engine, semaphore, 0, 0

    def at(self, base):
        self.base, self.n = base, 0

    def link(self, ins):
        self.n += 1
        ins.then_inc(self.semaphore, 1)
        self.engine.wait_ge(self.semaphore, self.base + self.n)


def carve(tensor, at, *shape):
    n = 1
    for s in shape:
        n *= s
    view = tensor[:, at:at + n]
    if len(shape) > 1:
        names = "abcde"[: len(shape)]
        view = view.rearrange(f"p ({' '.join(names)}) -> p {' '.join(names)}", **dict(zip(names, shape)))
    return view, at + n


def decoder_layer(
    nc: bass.Bass,
    x: bass.AP,
    ctx_in: bass.AP,
    Wq: bass.AP,
    Wk: bass.AP,
    Wv: bass.AP,
    Wo: bass.AP,
    in_proj_w: bass.AP,
    conv_w: bass.AP,
    conv_b: bass.AP,
    x_proj_w: bass.AP,
    dt_proj_w: bass.AP,
    dt_proj_b: bass.AP,
    A_log: bass.AP,
    D_skip: bass.AP,
    w_router: bass.AP,
    w_gate: bass.AP,
    w_up: bass.AP,
    w_down: bass.AP,
    out: bass.AP,
):
    B, S, HID = x.shape
    DM = ctx_in.shape[2]
    DI, DC = conv_w.shape
    DS = A_log.shape[1]
    DR = dt_proj_w.shape[1]
    NE, _, INTER = w_gate.shape
    HEADS = 16
    HD = HID // HEADS
    QC = S // P
    FC = HID // P
    NT = B * QC
    T = B * S
    HALVES = DI // P
    PAIRS = HEADS // 2
    TILE_PAIRS = PAIRS // FC
    IC = INTER // P
    SCORE = P + S
    SCALE = float(HD) ** -0.5
    BC = 2 * DS
    NP = DS // 2
    POOL_PAIRS = (1, 4, 6)
    DVE_PAIRS = tuple(m for m in range(NP) if m not in POOL_PAIRS)
    TH = T // BANK
    BH = B // TH
    assert DM == P and DI == S == HID and QC == FC == HALVES == 2 and HD == 16 and BC == 32 and TH == 2

    with ExitStack() as stack:
        def sb(name, shape, dt=F32):
            return stack.enter_context(nc.sbuf_tensor(name, shape, dt))

        def sem(name):
            return stack.enter_context(nc.semaphore(name))

        ident = sb("ident", [P, P])
        ident_b = sb("ident_b", [P, P], BF16)
        mask_qk = sb("mask_qk", [P, P], BF16)
        mask_kq = sb("mask_kq", [P, P], BF16)
        rows32 = sb("rows32", [3 * BC, BC])
        rows32_b = sb("rows32_b", [3 * BC, BC], BF16)
        iota8 = sb("iota8", [P, NE])
        exponent = sb("exponent", [P, QC])
        wT = sb("wT", [P, 4, FC, HID])
        wr_sb = sb("wr_sb", [P, FC, NE])
        convw_sb = sb("convw_sb", [P, HALVES, DC])
        vec_sb = sb("vec_sb", [P, 3, HALVES])
        A_sb = sb("A_sb", [P, HALVES, DS])
        delta = sb("delta", [P, B, HALVES, S])
        du = sb("du", [P, B, HALVES, S])
        u_sb = sb("u_sb", [P, B, HALVES, S])
        y_sum = sb("y_sum", [P, HALVES, S])
        bc_parts = sb("bc_parts", [3 * BC, T], BF16)
        x_in = sb("x_in", [P, QC, HID])
        x_res = sb("x_res", [P, QC, HID])
        x_sb = sb("x_sb", [P, NT, HID])
        x2T_hi = sb("x2T_hi", [P, FC, T], F32R)
        x2T_lo = sb("x2T_lo", [P, FC, T], F32R)
        w_tok = sb("w_tok", [P, NT, NE])
        x1 = sb("x1", [P, QC, HID])
        gated = sb("gated", [P, HALVES, S])
        stats = sb("stats", [P, QC, 6])
        mv = sb("mv", [P, 2, QC, 2])
        rstd = sb("rstd", [P, 2, QC])
        wr_split = sb("wr_split", [P, FC, 2, NE], F32R)
        top_idx = sb("top_idx", [P, NT, 8], U32)
        negmax = sb("negmax", [P, QC, HEADS])
        negmax_r = sb("negmax_r", [P, QC, HEADS])
        negmax_p = sb("negmax_p", [P, QC, 3 * BC], BF16)
        nmT = sb("nmT", [3 * BC, QC, P], BF16)
        e_raw = sb("e_raw", [P, 6 * INTER])
        SPLIT_W = 4 * FC * INTER + 2 * IC * HID
        weights = sb("weights", [P, 2, SPLIT_W], F32R)
        eg, ed = [], []
        for buf in range(2):
            view, at = carve(weights[:, buf], 0, 2, 2, FC, INTER)
            eg.append(view)
            view, at = carve(weights[:, buf], at, IC, 2, HID)
            ed.append(view)
        V_AT, ONES_AT = P // 2 - HD, P - HD
        v_second = sb("v_second", [P, HEADS * P])
        v_pad = [e_raw[:, 0:HEADS * P], v_second[:]]
        xT, at = carve(e_raw, HEADS * P, FC, S)
        hT, at = carve(e_raw, at, FC, S)
        assert at <= e_raw.shape[1]

        def v_columns(q, at):
            return v_pad[q].rearrange("p (h n) -> p h n", n=P)[:, :, at:at + HD]

        RAW = FC * INTER
        assert IC * HID == RAW and 2 * RAW == NT * HID
        x_flat = x_sb[:].rearrange("p t n -> p (t n)")
        raw_first = [x_flat[:, 0:RAW], x_flat[:, RAW:], x_flat[:, 0:RAW]]

        def raw_matrix(e, i):
            raw = raw_first[i] if isinstance(e, int) and e == 0 else e_raw[:, i * RAW:(i + 1) * RAW]
            return raw.rearrange("p (k n) -> p k n", k=FC if i < 2 else IC)

        area = sb("area", [P, 9216])
        win_raw, at = carve(area, 0, HALVES, DM)
        winT, at = carve(area, at, DI)
        xp_raw, at = carve(area, at, DI)
        xpT, at = carve(area, at, HALVES, 3 * BC + DR)
        dtw_raw, at = carve(area, at, HALVES, DR)
        dtwT, at = carve(area, at, DI)
        conv, at = carve(area, at, B, HALVES, S)
        dt_lo, _ = carve(conv.rearrange("p b h s -> p (b h s)"), 0, T)
        log_rest = conv
        xpad, at = carve(area, at, HALVES, B, DC - 1 + S)
        ln_part, _ = carve(xpad.rearrange("p h b s -> p (h b s)"), 0, B, HALVES, S)
        bc_r, at = carve(area, at, T)
        assert at <= area.shape[1]
        du_flat = du[:].rearrange("p b h s -> p (b h s)")
        c_ctx, at = carve(du_flat, 0, NT, DM)
        ctxT, at = carve(du_flat, at, T)
        w_raw, _ = carve(e_raw, 0, 4, FC, HID)

        dA, at = carve(area, 0, 2, 2, HALVES, S)
        dBu, at = carve(area, at, 2, 2, HALVES, S)
        states, at = carve(area, at, 3, 2, HALVES, S)
        c_rows, at = carve(area, at, 2, S)
        probT, at = carve(area, at, 2, 2, SCORE)
        pv_num = gated[:]
        pv_den = c_rows
        assert at <= area.shape[1]
        silu_g, at = carve(area, 0, 2, BANK)
        h_f, at = carve(area, at, 2, BANK)
        assert at <= 2 * 2 * HALVES * S
        logits, at = carve(area, 2 * 2 * HALVES * S, 2, NT, NE)
        small, at = carve(area, at, 3, NT)
        probs, at = carve(area, at, NT, NE)
        top_val, at = carve(area, at, NT, 8)
        top_idx_f, at = carve(area, at, NT, 8)
        picked, at = carve(area, at, 2, NT, NE)

        split = sb("split", [P, 8192], F32R)
        q4, at = carve(split, 0, PAIRS, S)
        k4, at = carve(split, at, PAIRS, S)
        pickQK, at = carve(split, at, 2, 2, TILE_PAIRS, P)
        q_hi, at = carve(split, at, FC, S)
        q_lo, at = carve(split, at, FC, S)
        k_hi, at = carve(split, at, FC, S)
        k_lo, at = carve(split, at, FC, S)
        assert at <= split.shape[1]
        h_hi, at = carve(split, 0, 2, IC, BANK)
        h_lo, at = carve(split, at, 2, IC, BANK)
        assert at <= split.shape[1]

        psW = stack.enter_context(nc.psum_tensor("psW", [P, 4, BANK], F32))
        psS = stack.enter_context(nc.psum_tensor("psS", [P, 2, BANK], F32))
        psT = stack.enter_context(nc.psum_tensor("psT", [P, 2, BANK], F32))
        psT_b = psT[:, 0, :].bitcast(BF16)

        def bank4(i):
            return psS[:, i, :] if i < 2 else psT[:, i - 2, :]

        def pick(r):
            return rows32_b[:, r:r + 1].broadcast_to([3 * BC, P])

        ld_ctx, ld_ssm, ld_small, ld_x, ld_attn = (sem(s) for s in ("ld_ctx", "ld_ssm", "ld_small", "ld_x", "ld_attn"))
        ld_expert, stored = sem("ld_expert"), sem("stored")
        consts, consts_b, zeroed = sem("consts"), sem("consts_b"), sem("zeroed")
        inverted = sem("inverted")
        rest_rdy, second_rdy, Du_rdy = sem("rest_rdy"), sem("second_rdy"), sem("Du_rdy")
        pick_rdy, v_pad_rdy, ld_res = sem("pick_rdy"), sem("v_pad_rdy"), sem("ld_res")
        dve_chain, act_chain, pool_chain = sem("dve_chain"), sem("act_chain"), sem("pool_chain")
        ctxT_ps, ctxT_rdy, ssmT_ps, ssmT_rdy = sem("ctxT_ps"), sem("ctxT_rdy"), sem("ssmT_ps"), sem("ssmT_rdy")
        xin_ps, xpad_rdy, wT_ps, wT_rdy = sem("xin_ps"), sem("xpad_rdy"), sem("wT_ps"), sem("wT_rdy")
        conv_rdy, u_rdy, xdbl_ps, dt_rdy = sem("conv_rdy"), sem("u_rdy"), sem("xdbl_ps"), sem("dt_rdy")
        delta_ps, relu_rdy, exp_rdy, ln_rdy = sem("delta_ps"), sem("relu_rdy"), sem("exp_rdy"), sem("ln_rdy")
        A_rdy, ssm_rdy, area_free = sem("A_rdy"), sem("ssm_rdy"), sem("area_free")
        b_ps, c_ps, dA_rdy = sem("b_ps"), sem("c_ps"), sem("dA_rdy")
        c_rows_rdy, hC_pool = sem("c_rows_rdy"), sem("hC_pool")
        gate_rdy = sem("gate_rdy")
        b_used, scanned, hC_rdy, y_added = sem("b_used"), sem("scanned"), sem("hC_rdy"), sem("y_added")
        xT_ps, xT_rdy, q_ps, k_ps, v_ps = (sem(s) for s in ("xT_ps", "xT_rdy", "q_ps", "k_ps", "v_ps"))
        q_hi_rdy, k_hi_rdy, q_lo_rdy, k_lo_rdy, v_rdy = (
            sem(s) for s in ("q_hi_rdy", "k_hi_rdy", "q_lo_rdy", "k_lo_rdy", "v_rdy"))
        q4_ps, k4_ps = sem("q4_ps"), sem("k4_ps")
        q4_even, q4_odd, k4_even, k4_odd = sem("q4_even"), sem("q4_odd"), sem("k4_even"), sem("k4_odd")
        score_ps, max_rdy, nm_rdy, nmT_ps, nmT_rdy = (
            sem(s) for s in ("score_ps", "max_rdy", "nm_rdy", "nmT_ps", "nmT_rdy"))
        scoreT_ps, probT_rdy, pv_ps, num_dve = sem("scoreT_ps"), sem("probT_rdy"), sem("pv_ps"), sem("num_dve")
        num_act, hT_rdy, attn_ps, x1_rdy = sem("num_act"), sem("hT_rdy"), sem("attn_ps"), sem("x1_rdy")
        res_rdy, x2_kept = sem("res_rdy"), sem("x2_kept")
        var_rdy, rstd_rdy = sem("var_rdy"), sem("rstd_rdy")
        tanh_rdy, gated_rdy, gatedT_ps, x2_rdy = sem("tanh_rdy"), sem("gated_rdy"), sem("gatedT_ps"), sem("x2_rdy")
        x2T_ps, x2T_rdy, x2lo_rdy, logit_ps = sem("x2T_ps"), sem("x2T_rdy"), sem("x2lo_rdy"), sem("logit_ps")
        logit_taken, shifted, lexp_rdy = sem("logit_taken"), sem("shifted"), sem("lexp_rdy")
        ehi_rdy, elo_rdy = sem("ehi_rdy"), sem("elo_rdy")
        gu_ps, silu_rdy, h_rdy, hhi_rdy, hlo_rdy = (
            sem(s) for s in ("gu_ps", "silu_rdy", "h_rdy", "hhi_rdy", "hlo_rdy"))
        down_ps, summed, final_rdy = sem("down_ps"), sem("summed"), sem("final_rdy")

        block = stack.enter_context(nc.Block())

        @block.sync
        def _(sp):
            sp.dma_start(c_ctx, ctx_in.rearrange("b (q p) d -> p (b q) d", p=P)).then_inc(ld_ctx, 16)
            sp.dma_start(win_raw, in_proj_w.rearrange("(h p) d -> p h d", p=P)).then_inc(ld_ssm, 16)
            sp.dma_start(xp_raw[0:DR + BC, :], x_proj_w).then_inc(ld_ssm, 16)
            sp.dma_start(dtw_raw, dt_proj_w.rearrange("(h p) r -> p h r", p=P)).then_inc(ld_ssm, 16)
            sp.dma_start(convw_sb[:], conv_w.rearrange("(h p) k -> p h k", p=P)).then_inc(ld_small, 16)
            for i, v in enumerate((conv_b, dt_proj_b, D_skip)):
                with nc.allow_non_contiguous_dma(reason="256 values, one to a partition"):
                    sp.dma_start(vec_sb[:, i, :], v.rearrange("(h p) -> p h", p=P)).then_inc(ld_small, 16)
            sp.dma_start(A_sb[:], A_log.rearrange("(h p) n -> p h n", p=P)).then_inc(ld_small, 16)
            sp.dma_start(wr_sb[:], w_router.rearrange("(k p) e -> p k e", p=P)).then_inc(ld_small, 16)
            for i, w in enumerate((Wq, Wk, Wv, Wo)):
                sp.dma_start(w_raw[:, i], w.rearrange("(c p) n -> p c n", p=P)).then_inc(ld_attn, 16)
            sp.dma_start(x_in[:], x[0].rearrange("(q p) d -> p q d", p=P)).then_inc(ld_x, 16)
            sp.dma_start(x_res[:], x[0].rearrange("(q p) d -> p q d", p=P)).then_inc(ld_res, 16)

            def load_expert(e):
                for i, w in enumerate((w_gate, w_up)):
                    sp.dma_start(
                        e_raw[:, i * FC * INTER:(i + 1) * FC * INTER].rearrange("p (k n) -> p k n", k=FC),
                        w[bass.ds(e, 1)].rearrange("o (k p) n -> p (o k) n", p=P),
                    ).then_inc(ld_expert, 16)
                sp.dma_start(
                    e_raw[:, 2 * FC * INTER:].rearrange("p (k n) -> p k n", k=IC),
                    w_down[bass.ds(e, 1)].rearrange("o (k p) n -> p (o k) n", p=P),
                ).then_inc(ld_expert, 16)

            for i, w in enumerate((w_gate, w_up, w_down)):
                if i == 2:
                    sp.wait_ge(elo_rdy, 1)
                sp.dma_start(raw_matrix(0, i), w[0].rearrange("(k p) n -> p k n", p=P)).then_inc(ld_expert, 16)

            def keep_x2(b):
                sp.wait_ge(x2_rdy, b + 1)
                sp.dma_start(x_sb[:, bass.ds(2 * b, QC), :], x1[:]).then_inc(x2_kept, 16)

            with sp.Fori(1, B) as b:
                sp.wait_ge(xT_ps, b)
                sp.dma_start(x_in[:], x[bass.ds(b, 1)].rearrange("o (q p) d -> p (o q) d", p=P)).then_inc(ld_x, 16)
                sp.wait_ge(res_rdy, b)
                sp.dma_start(x_res[:], x[bass.ds(b, 1)].rearrange("o (q p) d -> p (o q) d", p=P)).then_inc(ld_res, 16)
                keep_x2(b - 1)
            sp.wait_ge(attn_ps, B)
            load_expert(1)
            keep_x2(B - 1)
            with sp.Fori(2, NE) as e:
                sp.wait_ge(ehi_rdy, 3 * e)
                sp.wait_ge(elo_rdy, 3 * e)
                load_expert(e)
            for t in range(NT):
                sp.wait_ge(final_rdy, t + 1)
                sp.dma_start(
                    out.rearrange("b (q p) d -> p (b q) d", p=P)[:, t, :], x_sb[:, t, :]
                ).then_inc(stored, 16)
            sp.wait_ge(stored, 16 * NT)

        @block.gpsimd
        def _(pool):
            chain = Chain(pool, pool_chain)
            link = chain.link
            link(pool.memset(ident[:], 0.0))
            pool.affine_select(out=ident[:], in_=ident[:], compare_op=ALU.not_equal, fill=1.0, base=0,
                               pattern=[[-1, P]], channel_multiplier=1).then_inc(consts, 1)
            pool.wait_ge(consts, 1)
            pool.memset(xpad[:, :, :, 0:DC - 1], 0.0).then_inc(zeroed, 1)
            link(pool.tensor_copy(ident_b[:], ident[:]))
            for t in (mask_qk, mask_kq, negmax_p):
                link(pool.memset(t[:], 0.0))
            link(pool.memset(exponent[:], -0.5))
            link(pool.affine_select(out=mask_qk[:], in_=mask_qk[:], compare_op=ALU.is_ge, fill=MASKED, base=0,
                                    pattern=[[-1, P]], channel_multiplier=1))
            link(pool.affine_select(out=mask_kq[:], in_=mask_kq[:], compare_op=ALU.is_ge, fill=MASKED, base=0,
                                    pattern=[[1, P]], channel_multiplier=-1))
            pool.iota(iota8[:], pattern=[[1, NE]], base=0, channel_multiplier=0,
                      allow_small_or_imprecise_dtypes=True).then_inc(consts_b, 1)
            pool.wait_ge(consts_b, 1)

            def split_expert_lo(e, i, odd):
                pool.wait_ge(ehi_rdy, 3 * e + i + 1)
                hi, lo = (eg[odd][:, 0, i], eg[odd][:, 1, i]) if i < 2 else (ed[odd][:, :, 0, :], ed[odd][:, :, 1, :])
                pool.tensor_tensor(lo, raw_matrix(e, i), hi.bitcast(F32), ALU.subtract).then_inc(elo_rdy, 1)

            pool.wait_ge(wT_ps, 4)
            for q in range(QC):
                link(pool.memset(v_pad[q], 0.0))
                pool.memset(v_columns(q, ONES_AT), 1.0).then_inc(v_pad_rdy, 1)
            pool.wait_ge(v_pad_rdy, 2)
            for i in range(3):
                split_expert_lo(0, i, 0)
            pool.wait_ge(rest_rdy, 1)
            second = slice(B // 2, B)
            link(pool.tensor_tensor(log_rest[:, second], du[:, second], log_rest[:, second], ALU.subtract))
            pool.wait_ge(ln_rdy, 1)
            link(pool.tensor_tensor(log_rest[:, second], log_rest[:, second], ln_part[:, second], ALU.add))
            link(pool.tensor_tensor(delta[:, second], delta[:, second], log_rest[:, second], ALU.add))
            pool.tensor_tensor(du[:, second], delta[:, second], u_sb[:, second], ALU.mult).then_inc(second_rdy, 1)
            pool.wait_ge(second_rdy, 1)
            pool.engine_nop().then_inc(area_free, 1)

            pool.wait_ge(area_free, 2)
            pool.memset(dA[:, :, :, :, 0:1].rearrange("p a n h s -> p (a n h) s"), 0.0).then_inc(zeroed, 1)
            pool.wait_ge(zeroed, 2)
            pool.engine_nop().then_inc(y_added, 4)

            def add_states(b, m):
                g = b * NP + m
                if m in POOL_PAIRS:
                    at = b * len(POOL_PAIRS) + POOL_PAIRS.index(m)
                    pool.wait_ge(c_rows_rdy, at + 1)
                    pool.wait_ge(scanned, g + 3)
                    pool.tensor_tensor(states[:, m % 3], states[:, m % 3], c_rows.rearrange(
                        "p n (o s) -> p n o s", o=1).broadcast_to([P, 2, HALVES, S]), ALU.mult).then_inc(hC_pool, 1)
                    pool.wait_ge(hC_pool, at + 2)
                else:
                    pool.wait_ge(hC_rdy, b * len(DVE_PAIRS) + DVE_PAIRS.index(m) + 1)
                for n in range(2):
                    if m == 0 and n == 0:
                        pool.wait_ge(gated_rdy, b + 1)
                        pool.tensor_tensor(y_sum[:], states[:, 0, 0], states[:, 0, 1],
                                           ALU.add).then_inc(y_added, 2)
                    elif m > 0:
                        pool.wait_ge(y_added, 2 * g + n + 4)
                        pool.tensor_tensor(y_sum[:], y_sum[:], states[:, m % 3, n], ALU.add).then_inc(y_added, 1)

            def gate_output():
                pool.tensor_tensor(gated[:], y_sum[:], gated[:], ALU.mult).then_inc(gated_rdy, 1)

            def inverse_deviation(k, n=0):
                pool.wait_ge(var_rdy, k + 1)
                pool.tensor_tensor(rstd[:, n], rstd[:, n], exponent[:], ALU.pow).then_inc(rstd_rdy, 1)

            def divide_heads(b):
                pool.wait_ge(inverted, b + 1)
                pool.tensor_tensor(hT, pv_num, pv_den, ALU.mult).then_inc(hT_rdy, 1)

            def expert(e, odd, last=False):
                for th in range(TH):
                    for c in range(IC):
                        split_hidden_lo(e, th, c)
                        if not last and th == 0 and c >= 2:
                            split_expert_lo(e + 1, c - 2, 1 - odd)
                        elif not last and th == 1 and c == 1:
                            split_expert_lo(e + 1, 2, 1 - odd)

            def split_hidden_lo(e, th, c):
                pool.wait_ge(hhi_rdy, (e * TH + th) * IC + c + 1)
                pool.tensor_tensor(h_lo[:, th, c, :], h_f[:, c % 2, :], h_hi[:, th, c, :].bitcast(F32),
                                   ALU.subtract).then_inc(hlo_rdy, 1)

            with pool.Fori(0, B - 1) as b:
                for m in range(NP):
                    add_states(b, m)
                divide_heads(b)
                inverse_deviation(2 * b)
                pool.wait_ge(gate_rdy, b + 1)
                gate_output()
                inverse_deviation(2 * b + 1)
            for m in range(NP):
                add_states(B - 1, m)
            divide_heads(B - 1)
            split_hidden_lo(0, 0, 0)
            split_hidden_lo(0, 0, 1)
            inverse_deviation(2 * B - 2)
            split_hidden_lo(0, 0, 2)
            pool.wait_ge(gate_rdy, B)
            gate_output()
            split_hidden_lo(0, 0, 3)
            inverse_deviation(2 * B - 1)
            for i in range(3):
                split_expert_lo(1, i, 1)
            for c in range(IC):
                split_hidden_lo(0, 1, c)
            with pool.Fori(0, (NE - 2) // 2) as j:
                expert(2 * j + 1, 1)
                expert(2 * j + 2, 0)
            expert(NE - 1, 1, last=True)
            for t in range(NT // QC):
                inverse_deviation(2 * B + t, t % 2)

        @block.scalar
        def _(act):
            act.wait_ge(ctxT_ps, 1)
            act.copy(ctxT, psS[:].rearrange("p a n -> p (a n)")).then_inc(ctxT_rdy, 1)
            for half in range(HALVES):
                for th in range(TH):
                    act.wait_ge(xin_ps, half * TH + th + 1)
                    act.copy(xpad[:, half, BH * th:BH * (th + 1), DC - 1:],
                             bank4(half * TH + th).rearrange("p (b s) -> p b s", b=BH)).then_inc(xpad_rdy, 1)
            for i in range(4):
                act.wait_ge(wT_ps, i + 1)
                act.copy(wT[:, i], psW[:, i, :].rearrange("p (k n) -> p k n", k=FC)).then_inc(wT_rdy, 1)

            def x_transposed(b):
                act.wait_ge(xT_ps, b + 1)
                act.copy(xT, psW[:, 0, :].rearrange("p (k n) -> p k n", k=FC)).then_inc(xT_rdy, 1)

            def qkv(b):
                act.wait_ge(q_ps, b + 1)
                act.activation(q_hi, psW[:, 1, :].rearrange("p (k n) -> p k n", k=FC), ACT.Copy,
                               scale=SCALE).then_inc(q_hi_rdy, 1)
                act.wait_ge(k_ps, b + 1)
                act.copy(k_hi, psW[:, 2, :].rearrange("p (k n) -> p k n", k=FC)).then_inc(k_hi_rdy, 1)
                act.wait_ge(v_ps, b + 1)
                for q in range(QC):
                    ins = act.copy(v_columns(q, V_AT),
                                   psW[:, 3, q * HID:(q + 1) * HID].rearrange("p (h d) -> p h d", d=HD))
                ins.then_inc(v_rdy, 1)

            def take_q4(b):
                for i in (0, 2):
                    act.wait_ge(q4_ps, 4 * b + i + 1)
                    act.copy(q4[:, 2 * i:2 * i + 2, :],
                             psW[:, i, :].rearrange("p (j n) -> p j n", j=2)).then_inc(q4_even, 1)

            def take_k4(b):
                for i in (0, 2):
                    act.wait_ge(k4_ps, 4 * b + i + 1)
                    act.copy(k4[:, 2 * i:2 * i + 2, :],
                             psW[:, i, :].rearrange("p (j n) -> p j n", j=2)).then_inc(k4_even, 1)

            def take_nmT(b):
                act.wait_ge(nmT_ps, b + 1)
                act.copy(nmT[:], psT_b[0:3 * BC, 0:S].rearrange("p (q n) -> p q n", q=QC)).then_inc(nmT_rdy, 1)

            def numerators(b):
                act.wait_ge(pv_ps, (b + 1) * PAIRS + 2)
                act.wait_ge(hC_pool, (b + 1) * len(POOL_PAIRS) + 1)
                act.copy(pv_num[0:P // 2], psT[0:P // 2, 0, :].rearrange("p (k n) -> p k n", k=FC))
                act.copy(pv_den[0:P // 2], psT[P // 2:, 0, :].rearrange("p (k n) -> p k n", k=FC)).then_inc(num_act, 1)

            def half_tanh(b):
                act.wait_ge(x1_rdy, b + 1)
                act.activation(gated[:], x1[:], ACT.Tanh, scale=0.5).then_inc(tanh_rdy, 1)

            def take_x2T(b):
                act.wait_ge(x2T_ps, b + 1)
                act.copy(x2T_hi[:, :, bass.ds(b * S, S)],
                         psT[:, 1, :].rearrange("p (k n) -> p k n", k=FC)).then_inc(x2T_rdy, 1)

            def split_expert_hi(e, i, odd):
                if isinstance(e, int) and e == 0:
                    act.wait_ge(ld_expert, 48 if i == 2 else 32)
                else:
                    act.wait_ge(ld_expert, 48 * (e + 1))
                hi = eg[odd][:, 0, i] if i < 2 else ed[odd][:, :, 0, :]
                act.copy(hi, raw_matrix(e, i)).then_inc(ehi_rdy, 1)

            x_transposed(0)
            for half in range(HALVES):
                act.wait_ge(conv_rdy, half + 1)
                act.activation(u_sb[:, :, half, :], conv[:, :, half, :], ACT.Silu).then_inc(u_rdy, 1)
            act.wait_ge(v_pad_rdy, 2)
            qkv(0)
            split_expert_hi(0, 0, 0)
            take_q4(0)
            split_expert_hi(0, 1, 0)
            take_k4(0)
            for half in range(HALVES):
                for th in range(TH):
                    i = half * TH + th
                    act.wait_ge(relu_rdy, i + 1)
                    act.activation(du[:, BH * th:BH * (th + 1), half, :],
                                   psT[:, i % 2, :].rearrange("p (b s) -> p b s", b=BH), ACT.Abs,
                                   bias=vec_sb[:, 1, half:half + 1]).then_inc(act_chain, 1)
            act.wait_ge(act_chain, 4)
            act.activation(du[:], du[:], ACT.Exp, scale=-1.0).then_inc(exp_rdy, 1)
            act.wait_ge(exp_rdy, 1)
            act.activation(ln_part, du[:], ACT.Ln, bias=1.0).then_inc(ln_rdy, 1)
            split_expert_hi(0, 2, 0)
            act.wait_ge(ld_small, 16 * 6)
            act.activation(A_sb[:], A_sb[:], ACT.Exp).then_inc(act_chain, 1)
            act.wait_ge(act_chain, 5)
            act.mul(A_sb[:], A_sb[:], -1.0).then_inc(A_rdy, 1)

            def decay_buffer(b, m):
                act.wait_ge(scanned, b * NP + m + 1)

            def decay(b, m):
                for n in range(2):
                    for half in range(HALVES):
                        act.activation(dA[:, m % 2, n, half, 1:], delta[:, b, half, 1:], ACT.Exp,
                                       scale=A_sb[:, half, 2 * m + n:2 * m + n + 1]).then_inc(dA_rdy, 1)

            act.wait_ge(A_rdy, 1)
            act.wait_ge(ssm_rdy, 1)
            act.wait_ge(area_free, 2)
            act.wait_ge(Du_rdy, 1)
            for half in range(HALVES):
                act.activation(u_sb[:, :, half, :], u_sb[:, :, half, :], ACT.Identity,
                               scale=vec_sb[:, 2, half:half + 1]).then_inc(Du_rdy, 1)
            take_nmT(0)
            act.wait_ge(scanned, 2)
            decay(0, 0)
            decay(0, 1)

            def exponentials(b):
                for p in range(PAIRS):
                    if p < NP - 2:
                        decay_buffer(b, p + 2)
                    act.wait_ge(scoreT_ps, b * PAIRS + p + 1)
                    act.wait_ge(pv_ps, b * PAIRS + p + 1)
                    w0 = 2 * (p % 2)
                    act.activation(probT[:, p % 2], psW[:, w0:w0 + 2, 0:SCORE], ACT.Exp).then_inc(probT_rdy, 1)
                    if p < NP - 2:
                        decay(b, p + 2)
                    if p + 1 in POOL_PAIRS:
                        at = b * len(POOL_PAIRS) + POOL_PAIRS.index(p + 1)
                        act.wait_ge(c_ps, b * NP + p + 2)
                        act.wait_ge(hC_pool, at + 1)
                        act.copy(c_rows, psS[:, 1, :].rearrange("p (n s) -> p n s", n=2)).then_inc(c_rows_rdy, 1)

            with act.Fori(0, B - 1) as b:
                exponentials(b)
                numerators(b)
                decay_buffer(b + 1, 0)
                x_transposed(b + 1)
                decay(b + 1, 0)
                decay_buffer(b + 1, 1)
                qkv(b + 1)
                decay(b + 1, 1)
                take_q4(b + 1)
                take_k4(b + 1)
                half_tanh(b)
                take_x2T(b)
                take_nmT(b + 1)
            exponentials(B - 1)
            numerators(B - 1)

            def gate(e, th, c, first=False):
                k = (e * TH + th) * IC + c
                act.wait_ge(gu_ps, k + 1)
                if not (first and th == 0 and c < 2):
                    act.wait_ge(h_rdy, k - 1)
                act.activation(silu_g[:, c % 2], psW[:, c % 2, :], ACT.Silu, scale=GATE_MULT).then_inc(silu_rdy, 1)

            def split_hidden_hi(e, th, c, first=False):
                act.wait_ge(h_rdy, (e * TH + th) * IC + c + 1)
                if c == 0 and not first:
                    act.wait_ge(down_ps, (e - 1) * NT + (th + 1) * (NT // TH))
                act.copy(h_hi[:, th, c, :], h_f[:, c % 2, :]).then_inc(hhi_rdy, 1)

            def expert(e, odd, first=False, last=False, halves=range(TH)):
                for th in halves:
                    for c in range(IC + 1):
                        if c < IC:
                            gate(e, th, c, first)
                        if c > 0:
                            split_hidden_hi(e, th, c - 1, first)
                        if first and th == 1 and c == 1:
                            act.wait_ge(shifted, 1)
                            act.activation(probs[:], probs[:], ACT.Exp).then_inc(lexp_rdy, 1)
                        if first:
                            continue
                        if not last and th == 0 and c >= 3:
                            split_expert_hi(e + 1, c - 3, 1 - odd)
                        elif not last and th == 1 and c == 1:
                            act.wait_ge(down_ps, e * NT)
                            split_expert_hi(e + 1, 2, 1 - odd)

            act.wait_ge(scanned, B * NP + 2)
            gate(0, 0, 0, True)
            gate(0, 0, 1, True)
            split_hidden_hi(0, 0, 0, True)
            split_hidden_hi(0, 0, 1, True)
            gate(0, 0, 2, True)
            half_tanh(B - 1)
            split_hidden_hi(0, 0, 2, True)
            gate(0, 0, 3, True)
            split_hidden_hi(0, 0, 3, True)
            take_x2T(B - 1)
            for i in range(3):
                split_expert_hi(1, i, 1)
            expert(0, 0, first=True, halves=(1,))
            with act.Fori(0, (NE - 2) // 2) as j:
                expert(2 * j + 1, 1)
                expert(2 * j + 2, 0)
            expert(NE - 1, 1, last=True)

        @block.vector
        def _(dve):
            chain = Chain(dve, dve_chain)
            link = chain.link
            dve.wait_ge(consts, 1)
            link(dve.tensor_tensor(rows32[:], ident[0:3 * BC, 0:BC], ident[0:3 * BC, BC:2 * BC], ALU.add))
            link(dve.tensor_tensor(rows32[:], rows32[:], ident[0:3 * BC, 2 * BC:3 * BC], ALU.add))
            dve.tensor_copy(rows32_b[:, 0:DS], rows32[:, 0:DS])
            dve.tensor_scalar(rows32_b[:, DS:], rows32[:, DS:], 0.5, None, ALU.mult).then_inc(pick_rdy, 1)
            link(dve.tensor_scalar(pickQK.rearrange("p a h j n -> p (a h j) n"),
                                   ident[:].rearrange("p (o n) -> p o n", o=1).broadcast_to(
                                       [P, 4 * TILE_PAIRS, P]), 0.0, None, ALU.mult))
            for qk in range(2):
                for h in range(2):
                    rows = pickQK[:, qk, h].rearrange("p j (a k d) -> p (j a) k d", a=2, k=4)
                    blocks = slice(h, 4, 2) if qk else slice(2 * h, 2 * h + 2)
                    ins = dve.tensor_copy(rows[:, :, blocks, :], ident[:].rearrange(
                        "p (g o d) -> p g o d", o=1, d=HD).broadcast_to([P, 2 * TILE_PAIRS, 2, HD]))
            ins.then_inc(consts_b, 1)
            dve.wait_ge(ssmT_ps, 1)
            dve.tensor_copy(winT, psT[:, 0, 0:DI])
            xp_ps = psT[:, 0, DI:DI + HALVES * (DR + BC)].rearrange("p (h n) -> p h n", h=HALVES)
            for k in range(3):
                dve.tensor_copy(xpT[:, :, BC * k:BC * (k + 1)], xp_ps[:, :, DR:])
            dve.tensor_copy(xpT[:, :, 3 * BC:], xp_ps[:, :, 0:DR])
            dve.tensor_copy(dtwT[0:DR], psT[0:DR, 1, 0:DI]).then_inc(ssmT_rdy, 1)
            dve.wait_ge(ld_small, 16 * 6)
            dve.tensor_scalar(vec_sb[:, 2, :], vec_sb[:, 2, :], 0.5, None, ALU.mult).then_inc(Du_rdy, 1)
            dve.wait_ge(zeroed, 1)
            for half in range(HALVES):
                dve.wait_ge(xpad_rdy, TH * (half + 1))
                acc = conv[:, :, half, :]
                link(dve.tensor_scalar(acc, xpad[:, half, :, 0:S], convw_sb[:, half, 0:1], vec_sb[:, 0, half:half + 1],
                                       ALU.mult, ALU.add))
                for k in range(1, DC):
                    ins = dve.scalar_tensor_tensor(out=acc, in0=xpad[:, half, :, k:k + S],
                                                   scalar=convw_sb[:, half, k:k + 1], in1=acc,
                                                   op0=ALU.mult, op1=ALU.add)
                    if k < DC - 1:
                        link(ins)
                    else:
                        ins.then_inc(conv_rdy, 1)

            def split_qk(b):
                dve.wait_ge(q_hi_rdy, b + 1)
                dve.scalar_tensor_tensor(out=q_lo, in0=psW[:, 1, :].rearrange("p (k n) -> p k n", k=FC), scalar=SCALE,
                                         in1=q_hi.bitcast(F32), op0=ALU.mult, op1=ALU.subtract).then_inc(q_lo_rdy, 1)
                dve.wait_ge(k_hi_rdy, b + 1)
                dve.tensor_tensor(k_lo, psW[:, 2, :].rearrange("p (k n) -> p k n", k=FC), k_hi.bitcast(F32),
                                  ALU.subtract).then_inc(k_lo_rdy, 1)

            def take_q4(b):
                for i in (1, 3):
                    dve.wait_ge(q4_ps, 4 * b + i + 1)
                    dve.tensor_copy(q4[:, 2 * i:2 * i + 2, :],
                                    psW[:, i, :].rearrange("p (j n) -> p j n", j=2)).then_inc(q4_odd, 1)

            def take_k4(b):
                for i in (1, 3):
                    dve.wait_ge(k4_ps, 4 * b + i + 1)
                    dve.tensor_copy(k4[:, 2 * i:2 * i + 2, :],
                                    psW[:, i, :].rearrange("p (j n) -> p j n", j=2)).then_inc(k4_odd, 1)

            def maxima(b, p):
                dve.wait_ge(score_ps, b * PAIRS + p + 1)
                w0 = 2 * (p % 2)
                dve.tensor_reduce(negmax[:, 0, 2 * p:2 * p + 2], psW[:, w0:w0 + 2, 0:P], AX_X, ALU.max, negate=True)
                dve.tensor_reduce(negmax[:, 1, 2 * p:2 * p + 2], psW[:, w0:w0 + 2, P:SCORE], AX_X, ALU.max,
                                  negate=True).then_inc(max_rdy, 1)

            def split_maxima(b):
                dve.wait_ge(max_rdy, (b + 1) * PAIRS)
                link(dve.tensor_copy(negmax_p[:, :, 0:HEADS], negmax[:]))
                link(dve.tensor_tensor(negmax_r[:], negmax[:], negmax_p[:, :, 0:HEADS], ALU.subtract))
                link(dve.tensor_copy(negmax_p[:, :, BC:BC + HEADS], negmax_r[:]))
                dve.tensor_tensor(negmax_p[:, :, 2 * BC:2 * BC + HEADS], negmax_r[:], negmax_p[:, :, BC:BC + HEADS],
                                  ALU.subtract).then_inc(nm_rdy, 1)

            split_qk(0)
            for th in range(TH):
                dve.wait_ge(xdbl_ps, th + 1)
                dve.tensor_copy(dt_lo[0:DR, th * BANK:(th + 1) * BANK],
                                psS[3 * BC:3 * BC + DR, th, :]).then_inc(dt_rdy, 1)
            take_q4(0)
            take_k4(0)
            for half in range(HALVES):
                for th in range(TH):
                    i = half * TH + th
                    dve.wait_ge(delta_ps, i + 1)
                    dve.tensor_scalar(delta[:, BH * th:BH * (th + 1), half, :],
                                      psT[:, i % 2, :].rearrange("p (b s) -> p b s", b=BH),
                                      vec_sb[:, 1, half:half + 1], 0.0, ALU.add, ALU.max).then_inc(relu_rdy, 1)
            for th in range(TH):
                cols = slice(th * BANK, (th + 1) * BANK)
                bank = psS[0:3 * BC, th, :]
                rest = bc_r[0:3 * BC, cols]
                link(dve.tensor_copy(bc_parts[:, cols], bank))
                link(dve.tensor_tensor(rest, bank, bc_parts[:, cols], ALU.subtract))
                for k in (1, 2):
                    rows = slice(BC * k, BC * (k + 1))
                    link(dve.tensor_copy(bc_parts[rows, cols], rest[rows]))
                link(dve.tensor_tensor(bc_parts[rows, cols], rest[rows], bc_parts[rows, cols], ALU.subtract))
            dve.wait_ge(exp_rdy, 1)
            link(dve.tensor_scalar(log_rest, du[:], 1.0, -1.0, ALU.add, ALU.add))
            dve.engine_nop().then_inc(rest_rdy, 1)
            first = slice(0, B // 2)
            link(dve.tensor_tensor(log_rest[:, first], du[:, first], log_rest[:, first], ALU.subtract))
            dve.wait_ge(ln_rdy, 1)
            link(dve.tensor_tensor(log_rest[:, first], log_rest[:, first], ln_part[:, first], ALU.add))
            link(dve.tensor_tensor(delta[:, first], delta[:, first], log_rest[:, first], ALU.add))
            link(dve.tensor_tensor(du[:, first], delta[:, first], u_sb[:, first], ALU.mult))
            dve.engine_nop().then_inc(area_free, 1)
            dve.engine_nop().then_inc(ssm_rdy, 1)
            for p in range(PAIRS):
                maxima(0, p)
            split_maxima(0)
            dve.engine_nop().then_inc(scanned, 2)
            dve.engine_nop().then_inc(b_used, 1)
            dve.engine_nop().then_inc(hC_pool, 1)
            dve.engine_nop().then_inc(gated_rdy, 1)
            dve.engine_nop().then_inc(x2_kept, 16)
            link(dve.tensor_copy(wr_split[:, :, 0, :], wr_sb[:]))
            link(dve.tensor_tensor(wr_split[:, :, 1, :], wr_sb[:], wr_split[:, :, 0, :].bitcast(F32), ALU.subtract))

            def multiply_b(b, m):
                g = b * NP + m
                dve.wait_ge(b_ps, g + 1)
                dve.tensor_tensor(
                    dBu[:, m % 2], du[:, bass.ds(b, 1)].broadcast_to([P, 2, HALVES, S]),
                    psS[:, 0, :].rearrange("p (n o s) -> p n o s", n=2, o=1).broadcast_to([P, 2, HALVES, S]),
                    ALU.mult).then_inc(b_used, 1)

            def scan(b, m):
                g = b * NP + m
                dve.wait_ge(b_used, g + 2)
                dve.wait_ge(dA_rdy, 4 * g + 4)
                if m == 0:
                    dve.wait_ge(zeroed, 2)
                dve.wait_ge(y_added, 2 * g + (2 if m < 2 else 0))
                dve.tensor_tensor_scan(
                    states[:, m % 3].rearrange("p n h s -> p (n h s)"), dA[:, m % 2].rearrange("p n h s -> p (n h s)"),
                    dBu[:, m % 2].rearrange("p n h s -> p (n h s)"), 0.0, ALU.mult, ALU.add).then_inc(scanned, 1)

            def multiply_c(b, m):
                if m in POOL_PAIRS:
                    return
                g = b * NP + m
                dve.wait_ge(scanned, g + 3)
                dve.wait_ge(c_ps, g + 1)
                dve.tensor_tensor(
                    states[:, m % 3], states[:, m % 3],
                    psS[:, 1, :].rearrange("p (n o s) -> p n o s", n=2, o=1).broadcast_to([P, 2, HALVES, S]),
                    ALU.mult).then_inc(hC_rdy, 1)

            def ssm(b):
                for m in range(1, NP):
                    multiply_b(b, m)
                    multiply_c(b, m - 1)
                    scan(b, m)
                multiply_c(b, NP - 1)

            def norm_stats(src, n=0):
                for q in range(QC):
                    dve.bn_stats(stats[:, q], src(q))
                dve.drain()
                for q in range(QC):
                    ins = dve.bn_aggr(mv[:, n, q], stats[:, q])
                link(ins)
                dve.tensor_scalar(rstd[:, n], mv[:, n, :, 1], LN_EPS, None, ALU.add).then_inc(var_rdy, 1)

            def norm_apply(k, src, n=0):
                dve.wait_ge(rstd_rdy, k + 1)
                for q in range(QC):
                    ins = dve.tensor_scalar(src(q), src(q), mv[:, n, q, 0:1], rstd[:, n, q:q + 1], ALU.subtract, ALU.mult)
                return ins

            def x1_tile(q):
                return x1[:, q]

            def numerators(b):
                dve.wait_ge(pv_ps, (b + 1) * PAIRS + 2)
                dve.wait_ge(hC_pool, (b + 1) * len(POOL_PAIRS) + 1)
                dve.tensor_copy(pv_num[P // 2:], psT[0:P // 2, 1, :].rearrange("p (k n) -> p k n", k=FC))
                dve.tensor_copy(pv_den[P // 2:],
                                psT[P // 2:, 1, :].rearrange("p (k n) -> p k n", k=FC)).then_inc(num_dve, 1)

            def invert_sums(b):
                dve.wait_ge(num_act, b + 1)
                dve.wait_ge(num_dve, b + 1)
                dve.reciprocal(pv_den, pv_den).then_inc(inverted, 1)

            def residual(b):
                dve.wait_ge(attn_ps, b + 1)
                dve.wait_ge(ld_res, 16 * b + 16)
                dve.wait_ge(x2_kept, 16 * b + 16)
                dve.tensor_tensor(x1[:], psT[:, 1, :].rearrange("p (q n) -> p q n", q=QC), x_res[:],
                                  ALU.add).then_inc(res_rdy, 1)
                dve.wait_ge(res_rdy, b + 1)
                norm_stats(x1_tile)

            def gating(b):
                dve.wait_ge(Du_rdy, 3)
                dve.wait_ge(x1_rdy, b + 1)
                dve.wait_ge(tanh_rdy, b + 1)
                dve.scalar_tensor_tensor(out=gated[:], in0=gated[:], scalar=1.0, in1=x1[:], op0=ALU.add,
                                         op1=ALU.mult)
                dve.wait_ge(y_added, (b + 1) * DS + 4)
                dve.tensor_tensor(y_sum[:], u_sb[:, bass.ds(b, 1)].rearrange("p o h s -> p (o h) s"), y_sum[:],
                                  ALU.add).then_inc(gate_rdy, 1)

            def add_gated(b):
                dve.wait_ge(gatedT_ps, b + 1)
                link(dve.tensor_tensor(x1[:], psT[:, 0, :].rearrange("p (q n) -> p q n", q=QC), x1[:], ALU.add))
                norm_stats(x1_tile)

            def x2T_low(b):
                dve.wait_ge(x2T_rdy, b + 1)
                dve.tensor_tensor(x2T_lo[:, :, bass.ds(b * S, S)], psT[:, 1, :].rearrange("p (k n) -> p k n", k=FC),
                                  x2T_hi[:, :, bass.ds(b * S, S)].bitcast(F32), ALU.subtract).then_inc(x2lo_rdy, 1)

            dve.wait_ge(area_free, 2)
            multiply_b(0, 0)
            scan(0, 0)
            prep_links = chain.n
            with dve.Fori(0, B - 1) as b:
                chain.at(b * DVE_LINKS + prep_links)
                ssm(b)
                numerators(b)
                invert_sums(b)
                split_qk(b + 1)
                multiply_b(b + 1, 0)
                scan(b + 1, 0)
                residual(b)
                take_q4(b + 1)
                take_k4(b + 1)
                norm_apply(2 * b, x1_tile).then_inc(x1_rdy, 1)
                maxima(b + 1, 0)
                maxima(b + 1, 1)
                gating(b)
                maxima(b + 1, 2)
                maxima(b + 1, 3)
                add_gated(b)
                maxima(b + 1, 4)
                norm_apply(2 * b + 1, x1_tile).then_inc(x2_rdy, 1)
                maxima(b + 1, 5)
                maxima(b + 1, 6)
                x2T_low(b)
                maxima(b + 1, 7)
                split_maxima(b + 1)
                assert chain.n == DVE_LINKS, chain.n
            chain.at((B - 1) * DVE_LINKS + prep_links)
            ssm(B - 1)
            numerators(B - 1)
            invert_sums(B - 1)

            def router():
                dve.wait_ge(logit_ps, 1)
                dve.tensor_copy(logits[:], psT[:, 0, 0:2 * NT * NE].rearrange("p (t l e) -> p l t e", l=2, e=NE)
                                ).then_inc(logit_taken, 1)
                dve.wait_ge(logit_taken, 1)
                link(dve.tensor_tensor(probs[:], logits[:, 0], logits[:, 1], ALU.add))
                link(dve.tensor_reduce(small[:, 0, :], probs[:], AX_X, ALU.max))
                dve.tensor_tensor(probs[:], probs[:], per_expert(small[:, 0, :]), ALU.subtract).then_inc(shifted, 1)

            def per_expert(view):
                return view.rearrange("p (t o) -> p t o", o=1).broadcast_to([P, NT, NE])

            def choose():
                dve.wait_ge(lexp_rdy, 1)
                link(dve.tensor_reduce(small[:, 1, :], probs[:], AX_X, ALU.add))
                link(dve.reciprocal(small[:, 2, :], small[:, 1, :]))
                link(dve.scalar_tensor_tensor(out=probs[:], in0=probs[:], scalar=DOWN_MULT,
                                              in1=per_expert(small[:, 2, :]), op0=ALU.mult, op1=ALU.mult))
                for t in range(NT):
                    dve.max(top_val[:, t], probs[:, t])
                dve.drain()
                for t in range(NT):
                    dve.max_index(top_idx[:, t], top_val[:, t], probs[:, t])
                dve.drain()
                link(dve.tensor_copy(top_idx_f[:], top_idx[:]))
                for i in range(2):
                    link(dve.tensor_tensor(picked[:, i], iota8[:].rearrange("p (o e) -> p o e", o=1).broadcast_to(
                        [P, NT, NE]), top_idx_f[:, :, i:i + 1].broadcast_to([P, NT, NE]), ALU.is_equal))
                for i in range(2):
                    link(dve.tensor_tensor(picked[:, i], picked[:, i], top_val[:, :, i:i + 1].broadcast_to([P, NT, NE]),
                                           ALU.mult))
                link(dve.tensor_tensor(w_tok[:], picked[:, 0], picked[:, 1], ALU.add))

            def hidden(e, th, c):
                k = (e * TH + th) * IC + c
                dve.wait_ge(silu_rdy, k + 1)
                if not (isinstance(e, int) and e == 0 and th == 0 and c < 2):
                    dve.wait_ge(hlo_rdy, k - 1)
                dve.tensor_tensor(h_f[:, c % 2], silu_g[:, c % 2], psW[:, 2 + c % 2, :], ALU.mult).then_inc(h_rdy, 1)

            def accumulate(e, th, i, e_of):
                t = th * (NT // TH) + i
                dve.wait_ge(down_ps, e * NT + t + 1)
                bank = bank4(i)
                wt = w_tok[:, t, e_of] if isinstance(e, int) else w_tok[:, t, bass.ds(e, 1)]
                dve.scalar_tensor_tensor(out=x_sb[:, t], in0=bank[:, 0:HID], scalar=wt, in1=x_sb[:, t], op0=ALU.mult,
                                         op1=ALU.add).then_inc(summed, 1)
                dve.wait_ge(summed, 2 * (e * NT + t) + 1)
                dve.scalar_tensor_tensor(out=x_sb[:, t], in0=bank[:, HID:], scalar=wt, in1=x_sb[:, t], op0=ALU.mult,
                                         op1=ALU.add).then_inc(summed, 1)

            def expert(e):
                e_of = slice(e, e + 1) if isinstance(e, int) else None
                e_before = slice(e - 1, e) if isinstance(e, int) else None
                for c in range(IC):
                    hidden(e, 0, c)
                for i in range(4):
                    accumulate(e - 1, 1, i, e_before)
                for c in range(IC):
                    hidden(e, 1, c)
                for i in range(4):
                    accumulate(e, 0, i, e_of)

            hidden(0, 0, 0)
            hidden(0, 0, 1)
            residual(B - 1)
            norm_apply(2 * B - 2, x1_tile).then_inc(x1_rdy, 1)
            hidden(0, 0, 2)
            gating(B - 1)
            hidden(0, 0, 3)
            add_gated(B - 1)
            norm_apply(2 * B - 1, x1_tile).then_inc(x2_rdy, 1)
            x2T_low(B - 1)
            hidden(0, 1, 0)
            router()
            hidden(0, 1, 1)
            choose()
            hidden(0, 1, 2)
            hidden(0, 1, 3)
            dve.wait_ge(x2_kept, 16 * (B + 1))
            for i in range(4):
                accumulate(0, 0, i, slice(0, 1))
            with dve.Fori(0, (NE - 2) // 2) as j:
                expert(2 * j + 1)
                expert(2 * j + 2)
            expert(NE - 1)

            def tiles(t):
                return lambda q: x_sb[:, 2 * t + q]

            def final_stats(t):
                dve.wait_ge(summed, 2 * ((NE - 1) * NT + 2 * t + 2))
                norm_stats(tiles(t), t % 2)

            def final_apply(t):
                norm_apply(2 * B + t, tiles(t), t % 2).then_inc(final_rdy, 2)

            final_stats(0)
            final_stats(1)
            final_apply(0)
            final_apply(1)
            accumulate(NE - 1, 1, 0, slice(NE - 1, NE))
            accumulate(NE - 1, 1, 1, slice(NE - 1, NE))
            final_stats(2)
            accumulate(NE - 1, 1, 2, slice(NE - 1, NE))
            final_apply(2)
            accumulate(NE - 1, 1, 3, slice(NE - 1, NE))
            final_stats(3)
            final_apply(3)

        @block.tensor
        def _(pe):
            def transposes(bank_of, src_of, n, m, ident_of, done):
                for i in range(n):
                    for j in range(m):
                        ins = pe.transpose(bank_of(i, j), src_of(i, j), ident_of)
                ins.then_inc(done, 1)

            pe.wait_ge(consts, 1)
            pe.wait_ge(ld_ctx, 16)
            transposes(lambda i, j: psS[:, i, j * P:(j + 1) * P], lambda i, j: c_ctx[:, 4 * i + j, :], 2, 4, ident[:],
                       ctxT_ps)
            pe.wait_ge(ld_ssm, 48)
            for h in range(HALVES):
                pe.transpose(psT[:, 0, h * P:(h + 1) * P], win_raw[:, h, :], ident[:])
                n = DR + BC
                pe.transpose(psT[:, 0, DI + h * n:DI + (h + 1) * n], xp_raw[0:n, h * P:(h + 1) * P], ident[0:n, 0:n])
                ins = pe.transpose(psT[0:DR, 1, h * P:(h + 1) * P], dtw_raw[:, h, :], ident[:])
            ins.then_inc(ssmT_ps, 1)
            pe.wait_ge(ctxT_rdy, 1)
            pe.wait_ge(ssmT_rdy, 1)
            for half in range(HALVES):
                for th in range(TH):
                    pe.matmul(bank4(half * TH + th), winT[:, half * P:(half + 1) * P],
                              ctxT[:, th * BANK:(th + 1) * BANK], start=True, stop=True).then_inc(xin_ps, 1)
            pe.wait_ge(ld_attn, 64)
            for i in range(4):
                bank = psW[:, i, :]
                transposes(lambda k, c: bank[:, k * HID + c * P:k * HID + (c + 1) * P],
                           lambda k, c: w_raw[:, i, c, k * P:(k + 1) * P], FC, FC, ident[:], wT_ps)

            def transpose_x(b):
                pe.wait_ge(ld_x, 16 * b + 16)
                for q in range(QC):
                    for k in range(FC):
                        ins = pe.transpose(psW[:, 0, k * S + q * P:k * S + (q + 1) * P],
                                           x_in[:, q, k * P:(k + 1) * P], ident[:])
                ins.then_inc(xT_ps, 1)

            def project_qk(b):
                pe.wait_ge(xT_rdy, b + 1)
                for i, done in ((0, q_ps), (1, k_ps)):
                    for c in range(FC):
                        for k in range(FC):
                            ins = pe.matmul(psW[:, 1 + i, c * S:(c + 1) * S], wT[:, i, k, c * P:(c + 1) * P], xT[:, k, :],
                                            start=(k == 0), stop=(k == FC - 1))
                    ins.then_inc(done, 1)

            def project_v():
                for q in range(QC):
                    for k in range(FC):
                        ins = pe.matmul(psW[:, 3, q * HID:(q + 1) * HID], xT[:, k, q * P:(q + 1) * P], wT[:, 2, k, :],
                                        start=(k == 0), stop=(k == FC - 1))
                ins.then_inc(v_ps, 1)

            def stack_q(b):
                pe.wait_ge(q_hi_rdy, b + 1)
                pe.wait_ge(q_lo_rdy, b + 1)
                for i in range(4):
                    if i == 2:
                        pe.wait_ge(k_lo_rdy, b + 1)
                    elif i == 3:
                        pe.wait_ge(v_rdy, b + 1)
                    stack(0, i, q_hi, q_lo, q4_ps)

            def stack_k(b):
                pe.wait_ge(k_lo_rdy, b + 1)
                for i in range(4):
                    pe.wait_ge(q4_odd if i % 2 else q4_even, 2 * b + i // 2 + 1)
                    stack(1, i, k_hi, k_lo, k4_ps)

            def stack(qk, i, hi, lo, done):
                for j in range(2):
                    t, jj = (2 * i + j) // TILE_PAIRS, (2 * i + j) % TILE_PAIRS
                    pe.matmul(psW[:, i, j * S:(j + 1) * S], pickQK[:, qk, 0, jj, :], hi[:, t, :], start=True,
                              stop=False)
                    ins = pe.matmul(psW[:, i, j * S:(j + 1) * S], pickQK[:, qk, 1, jj, :], lo[:, t, :],
                                    start=False, stop=True)
                ins.then_inc(done, 1)

            def scores(b, p):
                if p == 0:
                    pe.wait_ge(k4_even, 2 * b + 2)
                    pe.wait_ge(k4_odd, 2 * b + 2)
                elif p >= 2:
                    pe.wait_ge(max_rdy, b * PAIRS + p - 1)
                for a in range(2):
                    bank = psW[:, 2 * (p % 2) + a, :]
                    rows = slice(64 * a, 64 * a + 64)
                    pe.matmul(bank[:, 0:P], q4[rows, p, 0:P], k4[rows, p, 0:P], start=True, stop=False)
                    pe.matmul(bank[:, 0:P], ident_b[:], mask_qk[:], start=False, stop=True)
                    pe.matmul(bank[:, P:SCORE], q4[rows, p, P:S], k4[rows, p, :], start=True, stop=True)
                    ins = pe.matmul(bank[:, S:SCORE], ident_b[:], mask_qk[:], start=False, stop=True,
                                    skip_group_check=True)
                ins.then_inc(score_ps, 1)

            def transpose_maxima(b):
                pe.wait_ge(nm_rdy, b + 1)
                for q in range(QC):
                    ins = pe.transpose(psT_b[0:3 * BC, q * P:(q + 1) * P], negmax_p[:, q, :], ident_b[:])
                ins.then_inc(nmT_ps, 1)

            pe.wait_ge(wT_rdy, 4)
            transpose_x(0)
            project_qk(0)
            project_v()
            pe.wait_ge(u_rdy, 2)
            for th in range(TH):
                for half in range(HALVES):
                    ins = pe.matmul(psS[0:3 * BC + DR, th, :], xpT[:, half, :],
                                    u_sb[:, BH * th:BH * (th + 1), half, :], start=(half == 0),
                                    stop=(half == HALVES - 1))
                ins.then_inc(xdbl_ps, 1)
            pe.wait_ge(consts_b, 2)
            stack_q(0)
            pe.wait_ge(dt_rdy, 2)
            for half in range(HALVES):
                for th in range(TH):
                    i = half * TH + th
                    if i == 2:
                        stack_k(0)
                    if i >= 2:
                        pe.wait_ge(relu_rdy, i - 1)
                        pe.wait_ge(act_chain, i - 1)
                    pe.matmul(psT[:, i % 2, :], dtwT[0:DR, half * P:(half + 1) * P],
                              dt_lo[0:DR, th * BANK:(th + 1) * BANK], start=True, stop=True).then_inc(delta_ps, 1)
            for p in range(PAIRS):
                scores(0, p)

            def broadcast_b(b, m):
                pe.wait_ge(b_used, b * NP + m + 1)
                broadcast(b, 0, 2 * m, b_ps)

            def broadcast_c(b, m):
                of_dve = len([k for k in DVE_PAIRS if k < m])
                if m == 0 and isinstance(b, int) and b == 0:
                    pass
                elif m == 0 or m - 1 in DVE_PAIRS:
                    pe.wait_ge(hC_rdy, b * len(DVE_PAIRS) + of_dve)
                else:
                    pe.wait_ge(c_rows_rdy, b * len(POOL_PAIRS) + m - of_dve)
                broadcast(b, 1, DS + 2 * m, c_ps)

            def broadcast(b, bank, row, done):
                for n in range(2):
                    ins = pe.matmul(psS[:, bank, n * S:(n + 1) * S], pick(row + n), bc_parts[:, bass.ds(b * S, S)],
                                    start=True, stop=True)
                ins.then_inc(done, 1)

            def shifted_scores(b, p):
                if p == 0:
                    pe.wait_ge(nmT_rdy, b + 1)
                elif p >= 2:
                    pe.wait_ge(probT_rdy, b * PAIRS + p - 1)
                for a in range(2):
                    bank = psW[:, 2 * (p % 2) + a, :]
                    rows = slice(64 * a, 64 * a + 64)
                    h = 2 * p + a
                    pe.matmul(bank[:, 0:S], k4[rows, p, 0:P], q4[rows, p, :], start=True, stop=False)
                    pe.matmul(bank[:, 0:S], pick(h), nmT[:].rearrange("p q n -> p (q n)"), start=False,
                              stop=True)
                    pe.matmul(bank[:, 0:P], ident_b[:], mask_kq[:], start=False, stop=True, skip_group_check=True)
                    pe.matmul(bank[:, S:SCORE], k4[rows, p, P:S], q4[rows, p, P:S], start=True, stop=False,
                              skip_group_check=True)
                    pe.matmul(bank[:, S:SCORE], pick(h), nmT[:, 1, :], start=False, stop=False,
                              skip_group_check=True)
                    ins = pe.matmul(bank[:, S:SCORE], ident_b[:], mask_kq[:], start=False, stop=True,
                                    skip_group_check=True)
                ins.then_inc(scoreT_ps, 1)

            def pv(b, p):
                pe.wait_ge(probT_rdy, b * PAIRS + p + 1)
                for a in range(2):
                    group, j = divmod(2 * p + a, 4)
                    at = (group // 2) * S
                    start = (2 * p + a) * P + V_AT - HD * j
                    pr = probT[:, p % 2, a]
                    pe.matmul(psT[:, group % 2, at:at + S], v_pad[0][:, start:start + P], pr[:, 0:S], start=(j == 0),
                              stop=(j == 3))
                    ins = pe.matmul(psT[:, group % 2, at + P:at + S], v_pad[1][:, start:start + P],
                                    pr[:, S:SCORE], start=False, stop=(j == 3), skip_group_check=True)
                ins.then_inc(pv_ps, 1)

            def attention(b):
                broadcast_b(b, 1)
                for p in range(PAIRS):
                    shifted_scores(b, p)
                    if p + 1 < NP:
                        broadcast_c(b, p + 1)
                    if p + 2 < NP:
                        broadcast_b(b, p + 2)
                    if p > 0:
                        pv(b, p - 1)
                pv(b, PAIRS - 1)

            def project_out(b):
                pe.wait_ge(hT_rdy, b + 1)
                for q in range(QC):
                    for k in range(FC):
                        ins = pe.matmul(psT[:, 1, q * HID:(q + 1) * HID], hT[:, k, q * P:(q + 1) * P], wT[:, 3, k, :],
                                        start=(k == 0), stop=(k == FC - 1))
                ins.then_inc(attn_ps, 1)

            def transpose_gated(b):
                pe.wait_ge(gated_rdy, b + 2)
                for q in range(QC):
                    for k in range(HALVES):
                        ins = pe.transpose(psT[:, 0, q * HID + k * P:q * HID + (k + 1) * P],
                                           gated[:, k, q * P:(q + 1) * P], ident[:])
                ins.then_inc(gatedT_ps, 1)

            def transpose_x2(b):
                pe.wait_ge(x2_rdy, b + 1)
                for q in range(QC):
                    for k in range(FC):
                        ins = pe.transpose(psT[:, 1, k * S + q * P:k * S + (q + 1) * P],
                                           x1[:, q, k * P:(k + 1) * P], ident[:])
                ins.then_inc(x2T_ps, 1)

            pe.wait_ge(relu_rdy, 4)
            pe.wait_ge(act_chain, 4)
            pe.wait_ge(pick_rdy, 1)
            pe.wait_ge(ssm_rdy, 1)
            transpose_maxima(0)
            pe.nop().then_inc(pv_ps, 2)
            broadcast_b(0, 0)
            broadcast_c(0, 0)
            pe.wait_ge(area_free, 2)
            with pe.Fori(0, B - 1) as b:
                attention(b)
                pe.wait_ge(probT_rdy, (b + 1) * PAIRS)
                transpose_x(b + 1)
                broadcast_b(b + 1, 0)
                broadcast_c(b + 1, 0)
                project_qk(b + 1)
                project_v()
                project_out(b)
                stack_q(b + 1)
                stack_k(b + 1)
                for p in range(PAIRS):
                    scores(b + 1, p)
                    if p == 3:
                        transpose_gated(b)
                    elif p == 6:
                        transpose_x2(b)
                pe.wait_ge(x2lo_rdy, b + 1)
                transpose_maxima(b + 1)
            attention(B - 1)

            def gate_up(e, odd, th, c):
                k = (e * TH + th) * IC + c
                if not (isinstance(e, int) and e == 0 and th == 0 and c < 2):
                    pe.wait_ge(h_rdy, k - 1)
                for mat in range(2):
                    bank = psW[:, 2 * mat + c % 2, :]
                    n = 0
                    for part, xT_part in ((0, x2T_hi), (0, x2T_lo), (1, x2T_hi)):
                        for kk in range(FC):
                            ins = pe.matmul(bank, eg[odd][:, part, mat, kk, c * P:(c + 1) * P],
                                            xT_part[:, kk, th * BANK:(th + 1) * BANK], start=(n == 0), stop=(n == 5))
                            n += 1
                ins.then_inc(gu_ps, 1)

            def down(e, odd, th, i):
                t = th * (NT // TH) + i
                if not (isinstance(e, int) and e == 0 and th == 0):
                    pe.wait_ge(summed, 2 * (e * NT + t - 3))
                bank = bank4(i)
                cols = slice(i * P, (i + 1) * P)
                for c in range(IC):
                    pe.matmul(bank, h_hi[:, th, c, cols], ed[odd][:, c].rearrange("p l n -> p (l n)"), start=(c == 0),
                              stop=(c == IC - 1))
                for c in range(IC):
                    ins = pe.matmul(bank[:, 0:HID], h_lo[:, th, c, cols], ed[odd][:, c, 0, :], start=False,
                                    stop=(c == IC - 1), skip_group_check=True)
                ins.then_inc(down_ps, 1)

            def route():
                for t in range(NT):
                    cols = slice(t * P, (t + 1) * P)
                    at = 2 * NE * t
                    for k in range(FC):
                        pe.matmul(psT[:, 0, at:at + 2 * NE], x2T_hi[:, k, cols],
                                  wr_split[:, k].rearrange("p l e -> p (l e)"), start=(k == 0), stop=(k == FC - 1))
                    for k in range(FC):
                        ins = pe.matmul(psT[:, 0, at:at + NE], x2T_lo[:, k, cols], wr_split[:, k, 0, :], start=False,
                                        stop=(k == FC - 1), skip_group_check=True)
                ins.then_inc(logit_ps, 1)

            def expert(e, odd):
                pe.wait_ge(elo_rdy, 3 * e + 2)
                for c in range(IC):
                    gate_up(e, odd, 0, c)
                pe.wait_ge(hlo_rdy, e * TH * IC)
                for i in range(4):
                    down(e - 1, 1 - odd, 1, i)
                for c in range(IC):
                    gate_up(e, odd, 1, c)
                pe.wait_ge(hlo_rdy, (e * TH + 1) * IC)
                pe.wait_ge(elo_rdy, 3 * e + 3)
                for i in range(4):
                    down(e, odd, 0, i)

            pe.wait_ge(elo_rdy, 3)
            pe.wait_ge(x2lo_rdy, B // TH)
            pe.wait_ge(probT_rdy, B * PAIRS)
            gate_up(0, 0, 0, 0)
            gate_up(0, 0, 0, 1)
            project_out(B - 1)
            gate_up(0, 0, 0, 2)
            gate_up(0, 0, 0, 3)
            transpose_gated(B - 1)
            pe.wait_ge(hlo_rdy, IC)
            down(0, 0, 0, 0)
            down(0, 0, 0, 1)
            transpose_x2(B - 1)
            pe.wait_ge(x2lo_rdy, B)
            gate_up(0, 0, 1, 0)
            route()
            for c in range(1, IC):
                gate_up(0, 0, 1, c)
            pe.wait_ge(logit_taken, 1)
            down(0, 0, 0, 2)
            down(0, 0, 0, 3)
            with pe.Fori(0, (NE - 2) // 2) as j:
                expert(2 * j + 1, 1)
                expert(2 * j + 2, 0)
            expert(NE - 1, 1)
            pe.wait_ge(hlo_rdy, NE * TH * IC)
            for i in range(4):
                down(NE - 1, 1, 1, i)


_INS = ['x', 'ctx_1024', 'L0_attn_Wq', 'L0_attn_Wk', 'L0_attn_Wv', 'L0_attn_Wo', 'L0_xattn_in_proj_w',
        'L0_xattn_conv_w', 'L0_xattn_conv_b', 'L0_xattn_x_proj_w', 'L0_xattn_dt_proj_w', 'L0_xattn_dt_proj_b',
        'L0_xattn_A_log', 'L0_xattn_D', 'L0_ffn_w_router', 'L0_ffn_w_gate', 'L0_ffn_w_up', 'L0_ffn_w_down']
_OUTS = [((4, 256, 256), 'float32')]


def kernel(**inputs):
    import numpy as _np
    import concourse.bacc as _bacc
    from concourse import mybir as _mybir
    from concourse.bass_utils import run_bass_kernel_spmd as _run

    nc = _bacc.Bacc("TRN2", target_bir_lowering=False, num_devices=1)
    arrays, args = {}, []
    for name in _INS:
        a = _np.ascontiguousarray(inputs[name])
        arrays[f"in_{name}_dram"] = a
        args.append(nc.dram_tensor(f"in_{name}_dram", a.shape, _mybir.dt.from_np(a.dtype), kind="ExternalInput").ap())
    for i, (shape, dtype) in enumerate(_OUTS):
        dt = _mybir.dt.from_np(_np.dtype(dtype))
        args.append(nc.dram_tensor(f"out_{i}_dram", shape, dt, kind="ExternalOutput").ap())
    decoder_layer(nc, *args)
    r = _run(nc, [arrays], core_ids=[0])
    got = tuple(r.results[0][f"out_{i}_dram"] for i in range(len(_OUTS)))
    return got[0]
```
